# Optimizing a Trainium2 kernel written in Bass

```python
import numpy as np
import jax
import jax.numpy as jnp

def _softmax(x, axis=-1):
    return jax.nn.softmax(x, axis=axis)

def _gelu(x):
    return jax.nn.gelu(x, approximate=True)

def _silu(x):
    return jax.nn.silu(x)

def _sigmoid(x):
    return jax.nn.sigmoid(x)

def _layernorm(x, axis=-1, eps=1e-05):
    m = jnp.mean(x, axis=axis, keepdims=True)
    v = jnp.var(x, axis=axis, keepdims=True)
    return (x - m) / jnp.sqrt(v + eps)

def _scatter_add(tgt, idx, src, axis=0):
    return tgt.at[idx].add(src)

def _segment_sum(src, seg, n):
    return jax.ops.segment_sum(src, seg, n)
kernel_name = 'mk_conv_attn_hybrid_d4_conv_nhwc128_r4_1b296e'

def setup_inputs(seed: int=0):
    np.random.seed(seed)
    _w = jnp.asarray

    def _rec_inputs():
        import jax
        import jax.numpy as jnp
        _gk = jax.random.key(seed)
        x = -0.0002023 + 1 * jax.random.normal(jax.random.fold_in(_gk, 1), (16, 56, 56, 32), jnp.float32)
        return x
    x = _rec_inputs()

    def _L0_conv_setup():
        import jax, jax.numpy as jnp
        import numpy as np
        WS = 7
        DISP = WS // 2
        HEADS = 4
        HEAD_DIM = 32
        DIM = 32
        INNER = HEADS * HEAD_DIM
        B, H, W = (16, 56, 56)
        NW_H, NW_W = (H // WS, W // WS)

        def _create_mask(ws, disp, upper_lower, left_right):
            mask = np.zeros((ws * ws, ws * ws), dtype=np.float32)
            if upper_lower:
                mask[-disp * ws:, :-disp * ws] = -np.inf
                mask[:-disp * ws, -disp * ws:] = -np.inf
            if left_right:
                mask = mask.reshape(ws, ws, ws, ws)
                mask[:, -disp:, :, :-disp] = -np.inf
                mask[:, :-disp, :, -disp:] = -np.inf
                mask = mask.reshape(ws * ws, ws * ws)
            return mask
        _UL = _create_mask(WS, DISP, True, False)
        _LR = _create_mask(WS, DISP, False, True)
        _MASK_NP = np.zeros((NW_H * NW_W, WS * WS, WS * WS), dtype=np.float32)
        _MASK_NP[-NW_W:] += _UL
        _MASK_NP[NW_W - 1::NW_W] += _LR
        MASK = jnp.asarray(_MASK_NP)
        _idx = np.array([[x, y] for x in range(WS) for y in range(WS)])
        REL_IDX = jnp.asarray(_idx[None, :, :] - _idx[:, None, :] + WS - 1)
        key = jax.random.key(seed)
        k1, k2, k3, k4, k5 = jax.random.split(key, 5)
        return {'x': jax.random.normal(k1, (B, H, W, DIM), dtype=jnp.float32), 'w_qkv': jax.random.normal(k2, (DIM, 3 * INNER), dtype=jnp.float32) * DIM ** (-0.5), 'pos_emb': jax.random.normal(k3, (2 * WS - 1, 2 * WS - 1), dtype=jnp.float32), 'w_out': jax.random.normal(k4, (INNER, DIM), dtype=jnp.float32) * INNER ** (-0.5), 'b_out': jax.random.normal(k5, (DIM,), dtype=jnp.float32) * 0.01}
    _L0_conv_all = _L0_conv_setup()
    _L0_conv_in = {k: v for k, v in _L0_conv_all.items() if k in ('w_qkv', 'pos_emb', 'w_out', 'b_out')}
    del _L0_conv_all

    def _L1_conv_setup():
        import jax, jax.numpy as jnp
        import numpy as np
        DM, DFF = (32, 128)
        B, D, L, FACTOR = (8, 16, 64, 10)

        def _ln(x, g, b):
            m = jnp.mean(x, axis=-1, keepdims=True)
            v = jnp.mean(jnp.square(x - m), axis=-1, keepdims=True)
            return (x - m) * jax.lax.rsqrt(v + 1e-05) * g + b

        def _mlp(x, W1, b1, W2, b2):
            return jax.nn.gelu(x @ W1 + b1, approximate=False) @ W2 + b2
        key = jax.random.key(seed)
        ks = jax.random.split(key, 9)
        f32 = jnp.float32
        return {'x': jax.random.normal(ks[0], (B, D, L, DM), f32), 'router': jax.random.normal(ks[1], (L, FACTOR, DM), f32), 'bo_time': jax.random.normal(ks[2], (DM,), f32) * 0.02, 'bo_send': jax.random.normal(ks[3], (DM,), f32) * 0.02, 'bo_recv': jax.random.normal(ks[4], (DM,), f32) * 0.02, 'g1': jnp.ones((DM,), f32), 'be1': jnp.zeros((DM,), f32), 'g2': jnp.ones((DM,), f32), 'be2': jnp.zeros((DM,), f32), 'g3': jnp.ones((DM,), f32), 'be3': jnp.zeros((DM,), f32), 'g4': jnp.ones((DM,), f32), 'be4': jnp.zeros((DM,), f32), 'W1a': jax.random.normal(ks[5], (DM, DFF), f32) * 0.02, 'b1a': jnp.zeros((DFF,), f32), 'W2a': jax.random.normal(ks[6], (DFF, DM), f32) * 0.02, 'b2a': jnp.zeros((DM,), f32), 'W1b': jax.random.normal(ks[7], (DM, DFF), f32) * 0.02, 'b1b': jnp.zeros((DFF,), f32), 'W2b': jax.random.normal(ks[8], (DFF, DM), f32) * 0.02, 'b2b': jnp.zeros((DM,), f32)}
    _L1_conv_all = _L1_conv_setup()
    _L1_conv_in = {k: v for k, v in _L1_conv_all.items() if k in ('router', 'bo_time', 'bo_send', 'bo_recv', 'g1', 'be1', 'g2', 'be2', 'g3', 'be3', 'g4', 'be4', 'W1a', 'b1a', 'W2a', 'b2a', 'W1b', 'b1b', 'W2b', 'b2b')}
    del _L1_conv_all

    def _L2_attn_setup():
        import jax, jax.numpy as jnp
        import numpy as np
        B, S, D = (4, 1024, 32)
        key = jax.random.key(seed)
        k1, k2, k3, k4 = jax.random.split(key, 4)
        emb = jax.random.normal(k1, (B, S, D), dtype=jnp.float32)
        lim = float(np.sqrt(6.0 / (D + D)))
        W_Q = jax.random.uniform(k2, (D, D), jnp.float32, -lim, lim)
        W_K = jax.random.uniform(k3, (D, D), jnp.float32, -lim, lim)
        W_V = jax.random.uniform(k4, (D, D), jnp.float32, -lim, lim)
        return {'embeddings': emb, 'W_Q': W_Q, 'W_K': W_K, 'W_V': W_V}
    _L2_attn_all = _L2_attn_setup()
    _L2_attn_in = {k: v for k, v in _L2_attn_all.items() if k in ('W_Q', 'W_K', 'W_V')}
    del _L2_attn_all

    def _L2_ffn_setup():
        import jax, jax.numpy as jnp
        import numpy as np
        B, S, D, E, H, O, K = (128, 512, 32, 16, 128, 32, 8)
        key = jax.random.key(seed)
        k0, k1, k2, k3 = jax.random.split(key, 4)
        x = jax.random.normal(k0, (B, S, D), dtype=jnp.float32)
        gate_w = jax.random.normal(k1, (E, D), dtype=jnp.float32) * (1.0 / np.sqrt(D))
        gate_b = jnp.zeros((E,), dtype=jnp.float32)
        weight1 = jax.random.uniform(k2, (E, D + 1, H), dtype=jnp.float32, minval=-1.0, maxval=1.0) * (1.0 / np.sqrt(D + 1))
        weight2 = jax.random.uniform(k3, (E, H + 1, O), dtype=jnp.float32, minval=-1.0, maxval=1.0) * (1.0 / np.sqrt(H + 1))
        return {'x': x, 'gate_w': gate_w, 'gate_b': gate_b, 'weight1': weight1, 'weight2': weight2}
    _L2_ffn_all = _L2_ffn_setup()
    _L2_ffn_in = {k: v for k, v in _L2_ffn_all.items() if k in ('gate_w', 'gate_b', 'weight1', 'weight2')}
    del _L2_ffn_all

    def _L3_attn_setup():
        import jax, jax.numpy as jnp
        import numpy as np
        B, T, C = (4, 1024, 32)
        key = jax.random.key(seed)
        k1, k2, k3, k4 = jax.random.split(key, 4)
        x = jax.random.normal(k1, (B, T, C), dtype=jnp.float32)
        s = 1.0 / np.sqrt(C)
        Wq = jax.random.normal(k2, (C, C), dtype=jnp.float32) * s
        Wk = jax.random.normal(k3, (C, C), dtype=jnp.float32) * s
        Wv = jax.random.normal(k4, (C, C), dtype=jnp.float32) * s
        return {'x': x, 'Wq': Wq, 'Wk': Wk, 'Wv': Wv}
    _L3_attn_all = _L3_attn_setup()
    _L3_attn_in = {k: v for k, v in _L3_attn_all.items() if k in ('Wq', 'Wk', 'Wv')}
    del _L3_attn_all

    def _L3_ffn_setup():
        import jax, jax.numpy as jnp
        import numpy as np
        B, S, D, E, H, O, K = (128, 512, 32, 16, 128, 32, 8)
        key = jax.random.key(seed)
        k0, k1, k2, k3 = jax.random.split(key, 4)
        x = jax.random.normal(k0, (B, S, D), dtype=jnp.float32)
        gate_w = jax.random.normal(k1, (E, D), dtype=jnp.float32) * (1.0 / np.sqrt(D))
        gate_b = jnp.zeros((E,), dtype=jnp.float32)
        weight1 = jax.random.uniform(k2, (E, D + 1, H), dtype=jnp.float32, minval=-1.0, maxval=1.0) * (1.0 / np.sqrt(D + 1))
        weight2 = jax.random.uniform(k3, (E, H + 1, O), dtype=jnp.float32, minval=-1.0, maxval=1.0) * (1.0 / np.sqrt(H + 1))
        return {'x': x, 'gate_w': gate_w, 'gate_b': gate_b, 'weight1': weight1, 'weight2': weight2}
    _L3_ffn_all = _L3_ffn_setup()
    _L3_ffn_in = {k: v for k, v in _L3_ffn_all.items() if k in ('gate_w', 'gate_b', 'weight1', 'weight2')}
    del _L3_ffn_all
    return {'x': x, 'L0_conv_w_qkv': _L0_conv_in['w_qkv'], 'L0_conv_pos_emb': _L0_conv_in['pos_emb'], 'L0_conv_w_out': _L0_conv_in['w_out'], 'L0_conv_b_out': _L0_conv_in['b_out'], 'L1_conv_router': _L1_conv_in['router'], 'L1_conv_bo_time': _L1_conv_in['bo_time'], 'L1_conv_bo_send': _L1_conv_in['bo_send'], 'L1_conv_bo_recv': _L1_conv_in['bo_recv'], 'L1_conv_g1': _L1_conv_in['g1'], 'L1_conv_be1': _L1_conv_in['be1'], 'L1_conv_g2': _L1_conv_in['g2'], 'L1_conv_be2': _L1_conv_in['be2'], 'L1_conv_g3': _L1_conv_in['g3'], 'L1_conv_be3': _L1_conv_in['be3'], 'L1_conv_g4': _L1_conv_in['g4'], 'L1_conv_be4': _L1_conv_in['be4'], 'L1_conv_W1a': _L1_conv_in['W1a'], 'L1_conv_b1a': _L1_conv_in['b1a'], 'L1_conv_W2a': _L1_conv_in['W2a'], 'L1_conv_b2a': _L1_conv_in['b2a'], 'L1_conv_W1b': _L1_conv_in['W1b'], 'L1_conv_b1b': _L1_conv_in['b1b'], 'L1_conv_W2b': _L1_conv_in['W2b'], 'L1_conv_b2b': _L1_conv_in['b2b'], 'L2_attn_W_Q': _L2_attn_in['W_Q'], 'L2_attn_W_K': _L2_attn_in['W_K'], 'L2_attn_W_V': _L2_attn_in['W_V'], 'L2_ffn_gate_w': _L2_ffn_in['gate_w'], 'L2_ffn_gate_b': _L2_ffn_in['gate_b'], 'L2_ffn_weight1': _L2_ffn_in['weight1'], 'L2_ffn_weight2': _L2_ffn_in['weight2'], 'L3_attn_Wq': _L3_attn_in['Wq'], 'L3_attn_Wk': _L3_attn_in['Wk'], 'L3_attn_Wv': _L3_attn_in['Wv'], 'L3_ffn_gate_w': _L3_ffn_in['gate_w'], 'L3_ffn_gate_b': _L3_ffn_in['gate_b'], 'L3_ffn_weight1': _L3_ffn_in['weight1'], 'L3_ffn_weight2': _L3_ffn_in['weight2']}

def reference(x, L0_conv_w_qkv, L0_conv_pos_emb, L0_conv_w_out, L0_conv_b_out, L1_conv_router, L1_conv_bo_time, L1_conv_bo_send, L1_conv_bo_recv, L1_conv_g1, L1_conv_be1, L1_conv_g2, L1_conv_be2, L1_conv_g3, L1_conv_be3, L1_conv_g4, L1_conv_be4, L1_conv_W1a, L1_conv_b1a, L1_conv_W2a, L1_conv_b2a, L1_conv_W1b, L1_conv_b1b, L1_conv_W2b, L1_conv_b2b, L2_attn_W_Q, L2_attn_W_K, L2_attn_W_V, L2_ffn_gate_w, L2_ffn_gate_b, L2_ffn_weight1, L2_ffn_weight2, L3_attn_Wq, L3_attn_Wk, L3_attn_Wv, L3_ffn_gate_w, L3_ffn_gate_b, L3_ffn_weight1, L3_ffn_weight2):
    import jax
    import jax.numpy as jnp

    def _L0_conv_ref(x, w_qkv, pos_emb, w_out, b_out):
        import jax, jax.numpy as jnp
        import numpy as np
        WS = 7
        DISP = WS // 2
        HEADS = 4
        HEAD_DIM = 32
        DIM = 32
        INNER = HEADS * HEAD_DIM
        B, H, W = (16, 56, 56)
        NW_H, NW_W = (H // WS, W // WS)

        def _create_mask(ws, disp, upper_lower, left_right):
            mask = np.zeros((ws * ws, ws * ws), dtype=np.float32)
            if upper_lower:
                mask[-disp * ws:, :-disp * ws] = -np.inf
                mask[:-disp * ws, -disp * ws:] = -np.inf
            if left_right:
                mask = mask.reshape(ws, ws, ws, ws)
                mask[:, -disp:, :, :-disp] = -np.inf
                mask[:, :-disp, :, -disp:] = -np.inf
                mask = mask.reshape(ws * ws, ws * ws)
            return mask
        _UL = _create_mask(WS, DISP, True, False)
        _LR = _create_mask(WS, DISP, False, True)
        _MASK_NP = np.zeros((NW_H * NW_W, WS * WS, WS * WS), dtype=np.float32)
        _MASK_NP[-NW_W:] += _UL
        _MASK_NP[NW_W - 1::NW_W] += _LR
        MASK = jnp.asarray(_MASK_NP)
        _idx = np.array([[x, y] for x in range(WS) for y in range(WS)])
        REL_IDX = jnp.asarray(_idx[None, :, :] - _idx[:, None, :] + WS - 1)
        scale = HEAD_DIM ** (-0.5)
        x = jnp.roll(x, (-DISP, -DISP), axis=(1, 2))
        b = x.shape[0]
        qkv = x @ w_qkv
        q, k, v = jnp.split(qkv, 3, axis=-1)

        def to_windows(t):
            t = t.reshape(b, NW_H, WS, NW_W, WS, HEADS, HEAD_DIM)
            return t.transpose(0, 5, 1, 3, 2, 4, 6).reshape(b, HEADS, NW_H * NW_W, WS * WS, HEAD_DIM)
        q, k, v = (to_windows(q), to_windows(k), to_windows(v))
        dots = jnp.einsum('bhwid,bhwjd->bhwij', q, k) * scale
        bias = pos_emb[REL_IDX[:, :, 0], REL_IDX[:, :, 1]]
        dots = dots + bias[None, None, None] + MASK[None, None]
        attn = jax.nn.softmax(dots, axis=-1)
        out = jnp.einsum('bhwij,bhwjd->bhwid', attn, v)
        out = out.reshape(b, HEADS, NW_H, NW_W, WS, WS, HEAD_DIM)
        out = out.transpose(0, 2, 4, 3, 5, 1, 6).reshape(b, H, W, INNER)
        out = out @ w_out + b_out
        return jnp.roll(out, (DISP, DISP), axis=(1, 2))

    def _L1_conv_ref(x, router, bo_time, bo_send, bo_recv, g1, be1, g2, be2, g3, be3, g4, be4, W1a, b1a, W2a, b2a, W1b, b1b, W2b, b2b):
        import jax, jax.numpy as jnp
        import numpy as np
        DM, DFF = (32, 128)
        B, D, L, FACTOR = (8, 16, 64, 10)

        def _ln(x, g, b):
            m = jnp.mean(x, axis=-1, keepdims=True)
            v = jnp.mean(jnp.square(x - m), axis=-1, keepdims=True)
            return (x - m) * jax.lax.rsqrt(v + 1e-05) * g + b

        def _mlp(x, W1, b1, W2, b2):
            return jax.nn.gelu(x @ W1 + b1, approximate=False) @ W2 + b2
        b, d, l, dm = x.shape
        time_in = x.reshape(b * d, l, dm)
        dim_in = _ln(time_in + bo_time, g1, be1)
        dim_in = _ln(dim_in + _mlp(dim_in, W1a, b1a, W2a, b2a), g2, be2)
        dim_send = dim_in.reshape(b, d, l, dm).transpose(0, 2, 1, 3).reshape(b * l, d, dm)
        dim_enc = _ln(dim_send + bo_recv, g3, be3)
        dim_enc = _ln(dim_enc + _mlp(dim_enc, W1b, b1b, W2b, b2b), g4, be4)
        return dim_enc.reshape(b, l, d, dm).transpose(0, 2, 1, 3)

    def _L2_attn_ref(embeddings, W_Q, W_K, W_V):
        import jax, jax.numpy as jnp
        import numpy as np
        B, S, D = (4, 1024, 32)
        _, seq_len, d = embeddings.shape
        Q = embeddings @ W_Q
        K = embeddings @ W_K
        V = embeddings @ W_V
        scale = 1.0 / jnp.sqrt(jnp.float32(d))
        scores = jnp.einsum('bqd,bkd->bqk', Q, K) * scale
        causal = jnp.tril(jnp.ones((seq_len, seq_len), dtype=bool))
        masked = jnp.where(causal[None, :, :], scores, jnp.float32(-jnp.inf))
        probs = jax.nn.softmax(masked, axis=-1)
        return jnp.einsum('bqk,bkd->bqd', probs, V)

    def _L2_ffn_ref(x, gate_w, gate_b, weight1, weight2):
        import jax, jax.numpy as jnp
        import numpy as np
        B, S, D, E, H, O, K = (128, 512, 32, 16, 128, 32, 8)
        Bn, Sn, Dn = x.shape
        logits = jnp.einsum('bsd,ed->bse', x, gate_w) + gate_b
        probs = jax.nn.softmax(logits, axis=1)
        vals, idx = jax.lax.top_k(probs.transpose(0, 2, 1), K)
        topv = vals.transpose(0, 2, 1)
        topi = idx.transpose(0, 2, 1)
        flat_idx = topi.reshape(Bn, K * E)
        gathered = jnp.take_along_axis(x, flat_idx[:, :, None], axis=1)
        gathered = gathered.reshape(Bn, K, E, Dn)
        pooled = jnp.einsum('bked,bke->bed', gathered, topv)
        ones = jnp.ones((E, Bn, 1), dtype=x.dtype)
        h = jnp.concatenate([pooled.transpose(1, 0, 2), ones], axis=-1)
        h = jax.nn.gelu(jnp.einsum('ebd,edh->ebh', h, weight1), approximate=False)
        h = jnp.concatenate([h, ones], axis=-1)
        out = jnp.einsum('ebh,eho->ebo', h, weight2)
        out = out.transpose(1, 0, 2)
        weighted = jnp.einsum('beo,bke->bkeo', out, topv).reshape(Bn, K * E, O)
        outputs = jnp.zeros((Bn, Sn, O), dtype=x.dtype)
        outputs = outputs.at[jnp.arange(Bn)[:, None], flat_idx].add(weighted)
        return outputs

    def _L3_attn_ref(x, Wq, Wk, Wv):
        import jax, jax.numpy as jnp
        import numpy as np
        B, T, C = (4, 1024, 32)
        q = jnp.einsum('btc,dc->btd', x, Wq)
        k = jnp.einsum('btc,dc->btd', x, Wk)
        v = jnp.einsum('btc,dc->btd', x, Wv)
        scale = 1.0 / jnp.sqrt(jnp.asarray(x.shape[-1], x.dtype))
        att = jnp.einsum('btd,bsd->bts', q, k) * scale
        causal = jnp.tril(jnp.ones((x.shape[1], x.shape[1]), dtype=bool))
        att = jnp.where(causal[None, :, :], att, -jnp.inf)
        w = jax.nn.softmax(att, axis=-1)
        out = jnp.einsum('bts,bsd->btd', w, v)
        return out

    def _L3_ffn_ref(x, gate_w, gate_b, weight1, weight2):
        import jax, jax.numpy as jnp
        import numpy as np
        B, S, D, E, H, O, K = (128, 512, 32, 16, 128, 32, 8)
        Bn, Sn, Dn = x.shape
        logits = jnp.einsum('bsd,ed->bse', x, gate_w) + gate_b
        probs = jax.nn.softmax(logits, axis=1)
        vals, idx = jax.lax.top_k(probs.transpose(0, 2, 1), K)
        topv = vals.transpose(0, 2, 1)
        topi = idx.transpose(0, 2, 1)
        flat_idx = topi.reshape(Bn, K * E)
        gathered = jnp.take_along_axis(x, flat_idx[:, :, None], axis=1)
        gathered = gathered.reshape(Bn, K, E, Dn)
        pooled = jnp.einsum('bked,bke->bed', gathered, topv)
        ones = jnp.ones((E, Bn, 1), dtype=x.dtype)
        h = jnp.concatenate([pooled.transpose(1, 0, 2), ones], axis=-1)
        h = jax.nn.gelu(jnp.einsum('ebd,edh->ebh', h, weight1), approximate=False)
        h = jnp.concatenate([h, ones], axis=-1)
        out = jnp.einsum('ebh,eho->ebo', h, weight2)
        out = out.transpose(1, 0, 2)
        weighted = jnp.einsum('beo,bke->bkeo', out, topv).reshape(Bn, K * E, O)
        outputs = jnp.zeros((Bn, Sn, O), dtype=x.dtype)
        outputs = outputs.at[jnp.arange(Bn)[:, None], flat_idx].add(weighted)
        return outputs

    def _gn(v, G=32, eps=1e-05):
        B_, H_, W_, C_ = v.shape
        g = v.reshape(B_, H_, W_, G, C_ // G)
        m = jnp.mean(g, axis=(1, 2, 4), keepdims=True)
        s = jnp.var(g, axis=(1, 2, 4), keepdims=True)
        return ((g - m) / jnp.sqrt(s + eps)).reshape(v.shape)

    def _ln_c(v, eps=1e-06):
        m = jnp.mean(v, axis=-1, keepdims=True)
        s = jnp.var(v, axis=-1, keepdims=True)
        return (v - m) / jnp.sqrt(s + eps)

    def _ln_t(v, eps=1e-05):
        m = jnp.mean(v, axis=-1, keepdims=True)
        s = jnp.var(v, axis=-1, keepdims=True)
        return (v - m) / jnp.sqrt(s + eps)

    def _to_tokens(v):
        B_, H_, W_, C_ = v.shape
        return v.reshape(B_, H_ * W_, C_)

    def _from_tokens(t, like):
        return t.reshape(like.shape)
    x = x + _L0_conv_ref(_gn(x), L0_conv_w_qkv, L0_conv_pos_emb, L0_conv_w_out, L0_conv_b_out)
    x = _L1_conv_ref(x, L1_conv_router, L1_conv_bo_time, L1_conv_bo_send, L1_conv_bo_recv, L1_conv_g1, L1_conv_be1, L1_conv_g2, L1_conv_be2, L1_conv_g3, L1_conv_be3, L1_conv_g4, L1_conv_be4, L1_conv_W1a, L1_conv_b1a, L1_conv_W2a, L1_conv_b2a, L1_conv_W1b, L1_conv_b1b, L1_conv_W2b, L1_conv_b2b)
    t = _to_tokens(x)
    t = t + _L2_attn_ref(_ln_t(t), L2_attn_W_Q, L2_attn_W_K, L2_attn_W_V)
    t = t + _L2_ffn_ref(_ln_t(t), L2_ffn_gate_w, L2_ffn_gate_b, L2_ffn_weight1, L2_ffn_weight2)
    t = t + _L3_attn_ref(_ln_t(t), L3_attn_Wq, L3_attn_Wk, L3_attn_Wv)
    t = t + _L3_ffn_ref(_ln_t(t), L3_ffn_gate_w, L3_ffn_gate_b, L3_ffn_weight1, L3_ffn_weight2)
    x = _from_tokens(t, x)
    return x

_drawn_inputs = setup_inputs


def setup_inputs(seed=0):
    import zlib

    import numpy as np

    out = dict(_drawn_inputs(seed))
    spreads = {'L1_conv_g1': (1.0, 0.2),
     'L1_conv_be1': (0.0, 0.1),
     'L1_conv_g2': (1.0, 0.2),
     'L1_conv_be2': (0.0, 0.1),
     'L1_conv_g3': (1.0, 0.2),
     'L1_conv_be3': (0.0, 0.1),
     'L1_conv_g4': (1.0, 0.2),
     'L1_conv_be4': (0.0, 0.1),
     'L1_conv_b1a': (0.0, 0.472),
     'L1_conv_b2a': (0.0, 0.1),
     'L1_conv_b1b': (0.0, 0.393),
     'L1_conv_b2b': (0.0, 0.1),
     'L2_ffn_gate_b': (0.0, 0.8),
     'L3_ffn_gate_b': (0.0, 0.1)}
    factors = {'L0_conv_b_out': 3.682,
     'L1_conv_W1a': 4.429,
     'L1_conv_W1b': 4.395,
     'L2_ffn_gate_w': 8.0,
     'L2_ffn_weight1': 8.0,
     'L2_ffn_weight2': 8.0,
     'L3_ffn_gate_w': 8.0,
     'L3_ffn_weight1': 8.0,
     'L3_ffn_weight2': 8.0}
    for name, (base, spread) in spreads.items():
        noise = np.random.default_rng([zlib.crc32(name.encode()), seed]).standard_normal(out[name].shape)
        drawn = base * np.exp(spread * noise) if base else spread * noise
        out[name] = jnp.asarray(drawn.astype(out[name].dtype))
    for name, factor in factors.items():
        out[name] = (out[name] * factor).astype(out[name].dtype)
    return out
```

```python
from contextlib import ExitStack

import concourse.bass as bass
from concourse import mybir
from concourse.alu_op_type import AluOpType as ALU


class Shared:
    pass

F32, BF16, I32 = mybir.dt.float32, mybir.dt.bfloat16, mybir.dt.int32
ACT = mybir.ActivationFunctionType
AX = mybir.AxisListType

P = 128
C = 32
S = 56 * 56
NT = -(-S // P)
LAST = S - (NT - 1) * P
NEG = -1e30


def make_constants(nc, ctx):
    def sb(name, shape, dt):
        return ctx.enter_context(nc.sbuf_tensor(name, shape, dt))
    k = Shared()
    k.ident = sb("ident", [P, P], F32)
    k.ident_bf = sb("ident_bf", [P, P], BF16)
    k.mask_qk = sb("mask_qk", [P, P], BF16)
    k.mask_kq = sb("mask_kq", [P, 4 * P], BF16)
    k.basis = sb("basis", [C, 4 * C], F32)
    made = ctx.enter_context(nc.semaphore("const_made"))
    with nc.Block() as block:
        @block.gpsimd
        def _(pool):
            nc.gpsimd.memset(k.ident[:], 0.0).then_inc(made, 1)
            nc.gpsimd.memset(k.mask_qk[:], 0.0).then_inc(made, 1)
            nc.gpsimd.memset(k.mask_kq[:], 0.0).then_inc(made, 1)
            nc.gpsimd.memset(k.basis[:], 0.0).then_inc(made, 1)
            pool.wait_ge(made, 4)
            nc.gpsimd.affine_select(out=k.ident[:], in_=k.ident[:], compare_op=ALU.not_equal, fill=1.0,
                                    base=0, pattern=[[-1, P]], channel_multiplier=1).then_inc(made, 1)
            nc.gpsimd.affine_select(out=k.mask_qk[:], in_=k.mask_qk[:], compare_op=ALU.is_ge, fill=NEG,
                                    base=0, pattern=[[-1, P]], channel_multiplier=1).then_inc(made, 1)
            nc.gpsimd.affine_select(out=k.mask_kq[:], in_=k.mask_kq[:], compare_op=ALU.is_ge, fill=NEG,
                                    base=-3 * P, pattern=[[1, 4 * P]], channel_multiplier=-1).then_inc(made, 1)
            nc.gpsimd.affine_select(out=k.basis[:].rearrange("p (r c) -> p r c", r=4),
                                    in_=k.basis[:].rearrange("p (r c) -> p r c", r=4),
                                    compare_op=ALU.not_equal, fill=1.0,
                                    base=0, pattern=[[0, 4], [-1, C]], channel_multiplier=1).then_inc(made, 1)
            pool.wait_ge(made, 8)
            nc.gpsimd.memset(k.basis[0:1, :], -1.0).then_inc(made, 1)
            nc.gpsimd.tensor_copy(k.ident_bf[:], k.ident[:]).then_inc(made, 1)
            pool.wait_ge(made, 10)
            nc.gpsimd.memset(k.basis[:, 0:4 * C:C], 0.0).then_inc(made, 1)
            pool.wait_ge(made, 11)
    return k


def token_stats(nc, m, eps, tag):
    GB = min(4, m.NB)
    NG = m.NB // GB
    W = GB * NT
    with ExitStack() as ctx:
        def sem(name):
            return ctx.enter_context(nc.semaphore(f"{tag}_{name}"))
        cent = ctx.enter_context(nc.sbuf_tensor(f"{tag}_cent", [P, 2, W, C], F32))
        sq = ctx.enter_context(nc.sbuf_tensor(f"{tag}_sq", [P, 2, W, C], F32))
        var = ctx.enter_context(nc.sbuf_tensor(f"{tag}_var", [P, m.NB * NT], F32))
        sd = ctx.enter_context(nc.sbuf_tensor(f"{tag}_sd", [P, m.NB * NT], F32))
        summed, scaled, centred = sem("summed"), sem("scaled"), sem("centred")
        squared, var_summed, var_scaled = sem("squared"), sem("var_summed"), sem("var_scaled")
        rooted, pad_done = sem("rooted"), sem("pad_done")
        tok = [m.T[:, g * GB:(g + 1) * GB, :, :].rearrange("p b t c -> p (b t) c") for g in range(NG)]
        mean = [m.mean[:, g * GB:(g + 1) * GB, :].rearrange("p b t -> p (b t)") for g in range(NG)]
        with nc.Block() as block:
            @block.vector
            def _(dve):
                def sum_squares(g):
                    dve.wait_ge(squared, g + 1)
                    nc.vector.tensor_reduce(var[:, g * W:(g + 1) * W], sq[:, g % 2], AX.X,
                                            ALU.add).then_inc(var_summed, 1)

                for g in range(NG):
                    nc.vector.tensor_reduce(mean[g], tok[g], AX.X, ALU.add).then_inc(summed, 1)
                    dve.wait_ge(summed, g + 1)
                    nc.vector.tensor_scalar(mean[g], mean[g], 1.0 / C, None, ALU.mult).then_inc(scaled, 1)
                    dve.wait_ge(scaled, g + 1)
                    if g >= 2:
                        dve.wait_ge(squared, g - 1)
                    nc.vector.tensor_tensor(cent[:, g % 2], tok[g], mean[g][:, :, None].to_broadcast([P, W, C]),
                                            ALU.subtract).then_inc(centred, 1)
                    if g >= 1:
                        sum_squares(g - 1)
                sum_squares(NG - 1)
                dve.wait_ge(var_summed, NG)
                nc.vector.tensor_scalar(var[:], var[:], 1.0 / C, eps, ALU.mult, ALU.add).then_inc(var_scaled, 1)
                dve.wait_ge(rooted, 1)
                nc.vector.reciprocal(m.rstd[:, 0:m.NB, :].rearrange("p b t -> p (b t)"), sd[:]).then_inc(pad_done, 1)
                nc.vector.memset(m.mean[:, m.NB, :], 0.0).then_inc(pad_done, 1)
                nc.vector.memset(m.rstd[:, m.NB, :], 1.0).then_inc(pad_done, 1)
                dve.wait_ge(pad_done, 3)

            @block.scalar
            def _(act):
                for g in range(NG):
                    act.wait_ge(centred, g + 1)
                    if g >= 2:
                        act.wait_ge(var_summed, g - 1)
                    nc.scalar.activation(sq[:, g % 2], cent[:, g % 2], ACT.Square).then_inc(squared, 1)
                act.wait_ge(var_scaled, 1)
                nc.scalar.activation(sd[:], var[:], ACT.Sqrt).then_inc(rooted, 1)


def causal_attention(nc, m, k, wq, wk, wv, tag):
    NB = m.NB
    QB = 512
    NJ = -(-S // QB)
    QT = QB // P
    n_tiles = [QT * (j + 1) if j < NJ - 1 else NT for j in range(NJ)]
    first = [sum(n_tiles[:j]) for j in range(NJ)]
    TILES = sum(n_tiles)
    q_tiles = [QT] * (NJ - 1) + [NT - QT * (NJ - 1)]
    MAXES = sum(q_tiles[j] * (j + 1) for j in range(NJ))
    first_max = [sum(q_tiles[i] * (i + 1) for i in range(j)) for j in range(NJ)]
    RS, RP, RM, RQ = 2, 8, 3, 3
    TG = 8
    NTG = -(-NT // TG)
    LEAD = 2

    def rows(t):
        return P if t < NT - 1 else LAST

    def width(j):
        return QB if j < NJ - 1 else LAST

    with ExitStack() as ctx:
        def sb(name, shape, dt):
            return ctx.enter_context(nc.sbuf_tensor(f"{tag}_{name}", shape, dt))

        def pb(name, shape, dt):
            return ctx.enter_context(nc.psum_tensor(f"{tag}_{name}", shape, dt))

        def sem(name):
            return ctx.enter_context(nc.semaphore(f"{tag}_{name}"))

        V = sb("v", [P, 2, NT, C], F32)
        VT = sb("vT", [C, NT * P], F32)
        Q = sb("q", [P, NT, C], F32)
        RES = sb("res", [P, NT, C], F32)
        VA = sb("va", [P, NT, 4, C], BF16)
        VB = sb("vb", [P, NT, 2, C], BF16)
        QA = sb("qa", [P, 2, NT, 4, C], BF16)
        QBp = sb("qb", [P, NT, 2, C], BF16)
        VAT = sb("vaT", [P, 2, S], BF16)
        VBT = sb("vbT", [2 * C, 2, S], BF16)
        QAT = sb("qaT", [P, 2, S], BF16)
        QBT = sb("qbT", [2 * C, 2, S], BF16)
        QS = sb("qs", [P, RQ, QB], BF16)
        E = sb("e", [P, RP, QB], F32)
        MX = sb("mx", [P, QT, NJ], F32)
        NM = sb("nm", [P, QT], F32)
        NR = sb("nr", [P, QT], F32)
        O = sb("o", [P, 2, QB], F32)
        RD = sb("rd", [P, QT], F32)
        OT = sb("ot", [P, QT, C], F32)
        A = sb("A", [C, C], F32)
        WF = sb("wf", [P, C + 1], F32)
        WQ, WK, WV = sb("wq", [C, C], F32), sb("wk", [C, C], F32), sb("wv", [C, C], F32)
        WQB, WKB = sb("wqb", [C, C], F32), sb("wkb", [C, C], F32)

        SC = [pb(f"sc{i}", [P, QB], F32) for i in range(RS)]
        MB = [pb(f"mb{i}", [P, QB], F32) for i in range(RM)]
        ACC = pb("acc", [P, QB], F32)
        MA = pb("ma", [P, 2 * QB], BF16)
        MD = pb("md", [P, QB], F32)
        MAf = MA[:].bitcast(F32)

        w_in, w_mm, w_out = sem("w_in"), sem("w_mm"), sem("w_out")
        with nc.Block() as block:
            @block.sync
            def _(sp):
                sp.dma_start(WQ[:], wq).then_inc(w_in, 16)
                sp.dma_start(WK[:], wk).then_inc(w_in, 16)
                sp.dma_start(WV[:], wv).then_inc(w_in, 16)

            @block.tensor
            def _(pe):
                pe.wait_ge(w_in, 48)
                b = k.basis[:, 0:C]
                nc.tensor.matmul(MD[0:C, 0:C], WQ[:], b, start=True, stop=True).then_inc(w_mm, 1)
                pe.wait_ge(w_out, 1)
                nc.tensor.matmul(MD[0:C, 0:C], WK[:], b, start=True, stop=True).then_inc(w_mm, 1)
                pe.wait_ge(w_out, 2)
                nc.tensor.matmul(MD[0:C, 0:C], WQB[:], WKB[:], start=True, stop=True).then_inc(w_mm, 1)
                pe.wait_ge(w_out, 3)
                nc.tensor.matmul(MD[:, 0:C], k.basis[:], WV[:], start=True, stop=True).then_inc(w_mm, 1)

            @block.vector
            def _(dve):
                dve.wait_ge(w_mm, 1)
                nc.vector.tensor_copy(WQB[:], MD[0:C, 0:C]).then_inc(w_out, 1)
                dve.wait_ge(w_mm, 2)
                nc.vector.tensor_copy(WKB[:], MD[0:C, 0:C]).then_inc(w_out, 1)
                dve.wait_ge(w_mm, 3)
                nc.vector.tensor_scalar(A[:], MD[0:C, 0:C], float(C) ** -0.5, None, ALU.mult).then_inc(w_out, 1)
                dve.wait_ge(w_mm, 4)
                nc.vector.tensor_copy(WF[:, 0:C], MD[:, 0:C]).then_inc(w_out, 1)
                for g in range(4):
                    nc.vector.tensor_copy(WF[g * C:(g + 1) * C, C:C + 1], k.ident[0:C, 0:1]).then_inc(w_out, 1)
                nc.vector.memset(V[:, :, :, 0:1], 1.0).then_inc(w_out, 1)
                nc.vector.memset(Q[:, NT - 1], 0.0).then_inc(w_out, 1)
                dve.wait_ge(w_out, 10)

        v_ready = sem("v_ready")
        v_parts = sem("v_parts")
        q_parts = sem("q_parts")
        pool_step = sem("pool_step")
        ma_full, ma_read = sem("ma_full"), sem("ma_read")
        md_full, md_read = sem("md_full"), sem("md_read")
        max_full, max_read = sem("max_full"), sem("max_read")
        shift_step, shift_ready = sem("shift_step"), sem("shift_ready")
        scores_full, exp_done = sem("scores_full"), sem("exp_done")
        pv_done = sem("pv_done")
        acc_read = sem("acc_read")
        out_step, out_done = sem("out_step"), sem("out_done")

        def prep_items():
            vt = [("vT", f) for f in range(-(-NT // 4))]
            q = [("q", f) for f in range(-(-NT // 16))]
            vs = [(s, f) for f in range(-(-NT // TG)) for s in ("va", "vb")]
            qs = [(s, f) for f in range(-(-NT // TG)) for s in ("qa", "qb")]
            return vt, q, vs, qs

        def max_items(j):
            return [("max", j, i, c) for i in range(q_tiles[j]) for c in range(j + 1)]

        vt, q, vs, qs = prep_items()
        prologue = vt + q + vs + qs + max_items(0) + [("shift", 0)] + max_items(1)
        extra = {1: vt, 2: q, 3: vs, 4: qs}
        PLAN = []
        for j in range(NJ):
            ahead = max_items((j + LEAD) % NJ)
            items = [("final", j - 1)] if j else []
            items += ahead[:2] + [("shift", (j + 1) % NJ)] + extra.get(j, []) + ahead[2:]
            n = n_tiles[j]
            PLAN.append([items[len(items) * u // n:len(items) * (u + 1) // n] for u in range(n)])
        flat = [x for step in PLAN for after in step for x in after] + [("final", NJ - 1)]

        def indices(items):
            kinds = {"vT": "ma", "va": "ma", "vb": "ma", "qa": "ma", "qb": "ma", "shift": "ma",
                     "q": "md", "final": "md", "max": "max"}
            seen = {"ma": 0, "md": 0, "max": 0}
            at = {}
            for x in items:
                at[x] = seen[kinds[x[0]]]
                seen[kinds[x[0]]] += 1
            return at, seen

        AT0, PRO = indices(prologue)
        AT1, PER = indices(flat)

        def before(g, kind):
            return 1 if g is None else g * PER[kind] + (1 + PRO[kind])

        def tiles_before(g):
            return g * TILES + 1

        def blocks_before(g):
            return g * NJ + 1

        PS = 9

        with nc.Block() as block:
            @block.gpsimd
            def _(pool):
                for s in (v_ready, v_parts, q_parts, pool_step):
                    pool.sem_inc(s, 1)

                def copy(out, in_):
                    return nc.gpsimd.tensor_scalar(out, in_, 1.0, 0.0, ALU.mult, ALU.add)

                def prepare(g, img, par):
                    n = [img * PS + 1]

                    def step(ins):
                        n[0] = n[0] + 1
                        ins.then_inc(pool_step, 1)
                        pool.wait_ge(pool_step, n[0])
                        pool.nop(nofuse=True)

                    pair = [P, NT, 2, C]
                    if g is not None:
                        pool.wait_ge(pv_done, tiles_before(g))
                    step(nc.gpsimd.tensor_tensor(
                        RES[:, :, 1:C], m.T[:, img, :, 1:C],
                        m.mean[:, img, :][:, :, None].to_broadcast([P, NT, C - 1]), ALU.subtract))
                    nc.gpsimd.tensor_tensor(
                        V[:, par, :, 1:C], RES[:, :, 1:C],
                        m.rstd[:, img, :][:, :, None].to_broadcast([P, NT, C - 1]), ALU.mult).then_inc(v_ready, 1)
                    pool.wait_ge(v_ready, img + 2)
                    if g is not None:
                        pool.wait_ge(ma_full, before(g, "ma") - 1)
                    pool.nop(nofuse=True)
                    step(copy(VA[:, :, 0:4:2, :], V[:, par][:, :, None, :].to_broadcast(pair)))
                    step(nc.gpsimd.tensor_tensor(RES[:], V[:, par], VA[:, :, 0, :], ALU.subtract))
                    step(copy(VA[:, :, 1:4:2, :], RES[:][:, :, None, :].to_broadcast(pair)))
                    step(nc.gpsimd.tensor_tensor(VB[:, :, 0, :], RES[:], VA[:, :, 1, :], ALU.subtract))
                    copy(VB[:, :, 1, :], VA[:, :, 0, :]).then_inc(v_parts, 1)
                    at = AT0 if g is None else AT1
                    pool.wait_ge(md_read, before(g, "md") + at[("q", len(q) - 1)] + 1)
                    pool.nop(nofuse=True)
                    step(copy(QA[:, par, :, 0:2, :], Q[:][:, :, None, :].to_broadcast(pair)))
                    step(nc.gpsimd.tensor_tensor(RES[:], Q[:], QA[:, par, :, 0, :], ALU.subtract))
                    step(copy(QA[:, par, :, 2:4, :], RES[:][:, :, None, :].to_broadcast(pair)))
                    step(nc.gpsimd.tensor_tensor(QBp[:, :, 1, :], RES[:], QA[:, par, :, 2, :], ALU.subtract))
                    copy(QBp[:, :, 0, :], QA[:, par, :, 0, :]).then_inc(q_parts, 1)

                prepare(None, 0, 0)
                with pool.Fori(0, NB // 2) as pair_of:
                    for par in range(2):
                        g = pair_of * 2 + par
                        prepare(g, g + 1, 1 - par)

            @block.tensor
            def _(pe):
                def item(g, img, par, x, at):
                    kind = x[0]
                    if kind == "max":
                        _, j, i, c = x
                        par_m = par if (g is None or j < LEAD) else 1 - par
                        n, qt = at[x], QT * j + i
                        r, hi = rows(qt), min(QB * (c + 1), P * (qt + 1), S)
                        bank = MB[n % RM]
                        pe.wait_ge(max_read, before(g, "max") + max(n - RM + 1, 0))
                        if i == 0 and c == 0:
                            if g is None:
                                pe.wait_ge(ma_read, before(None, "ma") + AT0[qs[-1]] + 1)
                            elif j == 0:
                                pe.wait_ge(ma_read, before(g, "ma") + AT1[qs[-1]] + 1)
                        q_t = QAT[:, par_m, qt * P:qt * P + r]
                        if c < j:
                            nc.tensor.matmul(bank[0:r, 0:QB], q_t, VAT[:, par_m, c * QB:hi],
                                             start=True, stop=True).then_inc(max_full, 1)
                        else:
                            w = hi - c * QB
                            nc.tensor.matmul(bank[0:r, 0:w], q_t, VAT[:, par_m, c * QB:hi], start=True, stop=False)
                            nc.tensor.matmul(bank[0:r, w - r:w], k.ident_bf[0:r, 0:r], k.mask_qk[0:r, 0:r],
                                             start=False, stop=True).then_inc(max_full, 1)
                        return
                    if kind in ("q", "final"):
                        pe.wait_ge(md_read, before(g, "md") + at[x])
                        if kind == "q":
                            pe.wait_ge(ma_read, before(g, "ma") + at[vt[-1]] + 1)
                            for t in range(16 * x[1], min(16 * x[1] + 16, NT)):
                                o = (t % 16) * C
                                last = nc.tensor.matmul(MD[0:rows(t), o:o + C], VT[:, t * P:t * P + rows(t)], A[:],
                                                        start=True, stop=True)
                        else:
                            j = x[1]
                            pe.wait_ge(acc_read, blocks_before(g) + j + 1)
                            for i in range(q_tiles[j]):
                                r = rows(QT * j + i)
                                o = i * (C + 1)
                                last = nc.tensor.matmul(MD[0:r, o:o + C + 1],
                                                        O[:, (1 - par + j) % 2, i * P:i * P + r], WF[:],
                                                        start=True, stop=True)
                        last.then_inc(md_full, 1)
                        return
                    pe.wait_ge(ma_read, before(g, "ma") + at[x])
                    if kind == "vT":
                        if x[1] == 0:
                            pe.wait_ge(v_ready, img + 2)
                        pe.nop(nofuse=True)
                        for t in range(4 * x[1], min(4 * x[1] + 4, NT)):
                            o = (t % 4) * P
                            last = nc.tensor.transpose(MAf[0:C, o:o + rows(t)], V[0:rows(t), par, t, :],
                                                       k.ident[0:rows(t), 0:rows(t)])
                    elif kind == "shift":
                        j = x[1]
                        par_s = par if j == 0 else 1 - par
                        pe.wait_ge(shift_ready, (blocks_before(img) if j == 0 else blocks_before(g)) + j + 1)
                        if j == NJ - 1:
                            pe.nop(nofuse=True)
                        for i in range(q_tiles[j]):
                            r = rows(QT * j + i)
                            last = nc.tensor.transpose(MA[:, i * P:i * P + r],
                                                       QA[0:r, par_s, QT * j + i].rearrange("p s c -> p (s c)"),
                                                       k.ident_bf[0:r, 0:r])
                    else:
                        src = {"va": VA[:], "vb": VB[:], "qa": QA[:, par], "qb": QBp[:]}[kind]
                        m_rows = P if kind in ("va", "qa") else 2 * C
                        if x[1] == 0:
                            pe.wait_ge(v_parts if kind in ("va", "vb") else q_parts, img + 2)
                        pe.nop(nofuse=True)
                        for t in range(TG * x[1], min(TG * x[1] + TG, NT)):
                            o = (t % TG) * P
                            last = nc.tensor.transpose(MA[0:m_rows, o:o + rows(t)],
                                                       src[0:rows(t), t].rearrange("p s c -> p (s c)"),
                                                       k.ident_bf[0:rows(t), 0:rows(t)])
                    last.then_inc(ma_full, 1)

                def weigh(g, par, j, u):
                    i = first[j] + u
                    r, d = rows(u), u - QT * j
                    c0 = P * d if d > 0 and j > 0 else 0
                    w = width(j)
                    cg = C * (u % 4)
                    pe.wait_ge(exp_done, tiles_before(g) + i + 1)
                    if u == 0:
                        pe.wait_ge(acc_read, blocks_before(g) + j)
                    if r < P:
                        pe.nop(nofuse=True)
                    nc.tensor.matmul(ACC[cg:cg + C, c0:w], V[0:r, par, u, :], E[0:r, i % RP, c0:w],
                                     start=(u < 4), stop=(u >= n_tiles[j] - 4)).then_inc(pv_done, 1)

                def turn(g, par):
                    for j in range(NJ):
                        w = width(j)
                        slot = (par + j) % 2
                        done = 0
                        for u in range(n_tiles[j]):
                            i = first[j] + u
                            r, d = rows(u), u - QT * j
                            c0 = P * d if d > 0 and j > 0 else 0
                            bank = SC[i % RS]
                            pe.wait_ge(exp_done, tiles_before(g) + max(i - 1, 0))
                            if u == 0:
                                if j == 0:
                                    n = before(g, "ma") - (PER["ma"] - AT1[("shift", 0)] - 1)
                                    pe.wait_ge(ma_read, n)
                                else:
                                    pe.wait_ge(ma_read, before(g, "ma") + AT1[("shift", j)] + 1)
                            kt = slice(u * P, u * P + r)
                            nc.tensor.matmul(bank[0:r, c0:w], VAT[:, par, kt], QS[:, slot, c0:w],
                                             start=True, stop=False)
                            last = nc.tensor.matmul(bank[0:r, c0:w], VBT[:, par, kt],
                                                    QBT[:, par, j * QB + c0:j * QB + w], start=False, stop=d < 0)
                            if d >= 0:
                                lo = 0 if j == 0 else c0
                                hi = min(P * (d + 1), w)
                                at = 3 * P - (P * d - lo)
                                last = nc.tensor.matmul(bank[0:r, lo:hi], k.ident_bf[0:r, 0:r],
                                                        k.mask_kq[0:r, at:at + hi - lo], start=False, stop=True)
                            last.then_inc(scores_full, 1)
                            for x in PLAN[j][u]:
                                item(g, g + 1, 1 - par, x, AT1)
                            if u % 4 == 1 and u >= 5:
                                for v in range(done, done + 4):
                                    weigh(g, par, j, v)
                                done += 4
                        for v in range(done, n_tiles[j]):
                            weigh(g, par, j, v)
                    item(g, g + 1, 1 - par, ("final", NJ - 1), AT1)

                for x in prologue:
                    item(None, 0, 0, x, AT0)
                with pe.Fori(0, NB // 2) as pair_of:
                    for par in range(2):
                        turn(pair_of * 2 + par, par)

            @block.scalar
            def _(act):
                for s in (ma_read, exp_done):
                    act.sem_inc(s, 1)

                def item(g, img, par, x, at):
                    kind = x[0]
                    if kind not in ("vT", "shift", "va", "vb", "qa", "qb"):
                        return
                    act.wait_ge(ma_full, before(g, "ma") + at[x])
                    if kind == "shift":
                        j = x[1]
                        slot = ((par if j == 0 else 1 - par) + j) % 2
                        w = width(j)
                        ins = nc.scalar.copy(QS[:, slot, 0:w], MA[:, 0:w])
                    elif kind == "vT":
                        lo, hi = 4 * P * x[1], min(4 * P * (x[1] + 1), S)
                        ins = nc.scalar.copy(VT[:, lo:hi], MAf[0:C, 0:hi - lo])
                    else:
                        dst = {"va": VAT, "vb": VBT, "qa": QAT, "qb": QBT}[kind]
                        lo, hi = TG * P * x[1], min(TG * P * (x[1] + 1), S)
                        n = dst.shape[0]
                        ins = nc.scalar.copy(dst[:, par, lo:hi], MA[0:n, 0:hi - lo])
                    ins.then_inc(ma_read, 1)

                nc.scalar.preload_act_table(ACT.Exp)
                for x in prologue:
                    item(None, 0, 0, x, AT0)
                with act.Fori(0, NB // 2) as pair_of:
                    for par in range(2):
                        g = pair_of * 2 + par
                        for j in range(NJ):
                            w = width(j)
                            for u in range(n_tiles[j]):
                                i = first[j] + u
                                r, d = rows(u), u - QT * j
                                c0 = P * d if d > 0 and j > 0 else 0
                                act.wait_ge(scores_full, tiles_before(g) - 1 + i + 1)
                                act.wait_ge(pv_done, tiles_before(g) + (i - RP + 1 if i >= RP else 0))
                                nc.scalar.activation(E[0:r, i % RP, c0:w], SC[i % RS][0:r, c0:w],
                                                     ACT.Exp).then_inc(exp_done, 1)
                                for x in PLAN[j][u]:
                                    item(g, g + 1, 1 - par, x, AT1)

            @block.vector
            def _(dve):
                for s in (md_read, max_read, shift_ready, acc_read, pv_done, shift_step, out_step, out_done):
                    dve.sem_inc(s, 1)

                def shift(g, blk, par_m, j, n):
                    nq, r = q_tiles[j], rows(QT * j)
                    hi = QA[0:r, par_m, QT * j:QT * j + nq, 0, 0:1]
                    lo = QA[0:r, par_m, QT * j:QT * j + nq, 2, 0:1]
                    nm, nr = NM[0:r, 0:nq, None], NR[0:r, 0:nq, None]
                    dve.wait_ge(max_read, before(g, "max") + n + 1)
                    nc.vector.tensor_reduce(NM[0:r, 0:nq], MX[0:r, 0:nq, 0:j + 1], AX.X, ALU.max,
                                            negate=True).then_inc(shift_step, 1)
                    dve.wait_ge(shift_step, blk * 3 + 2)
                    nc.vector.tensor_copy(hi, nm).then_inc(shift_step, 1)
                    dve.wait_ge(shift_step, blk * 3 + 3)
                    dve.wait_ge(shift_ready, blk + 1)
                    nc.vector.tensor_tensor(nr, nm, hi, ALU.subtract).then_inc(shift_step, 1)
                    dve.wait_ge(shift_step, blk * 3 + 4)
                    nc.vector.tensor_copy(lo, nr).then_inc(shift_ready, 1)

                def item(g, img, par, x, at):
                    kind = x[0]
                    if kind == "max":
                        _, j, i, c = x
                        n, qt = at[x], QT * j + i
                        r, w = rows(qt), min(QB * (c + 1), P * (qt + 1), S) - c * QB
                        later = g is None or j < LEAD
                        blk = (img if later else g) * NJ + j
                        if i == 0 and c == 0:
                            dve.wait_ge(shift_step, blk * 3 + 1)
                        dve.wait_ge(max_full, before(g, "max") + n)
                        nc.vector.tensor_reduce(MX[0:r, i, c:c + 1], MB[n % RM][0:r, 0:w], AX.X,
                                                ALU.max).then_inc(max_read, 1)
                        if i == q_tiles[j] - 1 and c == j:
                            shift(g, blk, par if later else 1 - par, j, n)
                    elif kind == "q":
                        lo, hi = 16 * x[1], min(16 * (x[1] + 1), NT)
                        full = min(hi, NT - 1)
                        dve.wait_ge(md_full, before(g, "md") + at[x])
                        dve.wait_ge(q_parts, img + 1)
                        if hi > full:
                            nc.vector.tensor_copy(Q[0:LAST, full], MD[0:LAST, (full - lo) * C:(hi - lo) * C])
                        nc.vector.tensor_copy(Q[:, lo:full].rearrange("p t c -> p (t c)"),
                                              MD[:, 0:(full - lo) * C]).then_inc(md_read, 1)
                    elif kind == "final":
                        j = x[1]
                        nq, r = q_tiles[j], rows(QT * j)
                        blk = g * NJ + j
                        md = MD[0:r, 0:nq * (C + 1)].rearrange("p (q c) -> p q c", c=C + 1)
                        dve.wait_ge(md_full, before(g, "md") + at[x])
                        dve.wait_ge(md_read, before(g, "md") + at[x])
                        nc.vector.reciprocal(RD[0:r, 0:nq, None], md[:, :, C:C + 1]).then_inc(out_step, 1)
                        dve.wait_ge(out_step, blk + 2)
                        dve.wait_ge(out_done, blk + 1)
                        nc.vector.tensor_tensor(OT[0:r, 0:nq], md[:, :, 0:C],
                                                RD[0:r, 0:nq, None].to_broadcast([r, nq, C]),
                                                ALU.mult).then_inc(md_read, 1)
                        dve.wait_ge(md_read, before(g, "md") + at[x] + 1)
                        t = m.T[0:r, g, QT * j:QT * j + nq, :]
                        nc.vector.tensor_tensor(t, t, OT[0:r, 0:nq], ALU.add).then_inc(out_done, 1)

                for x in prologue:
                    item(None, 0, 0, x, AT0)
                with dve.Fori(0, NB // 2) as pair_of:
                    for par in range(2):
                        g = pair_of * 2 + par
                        for j in range(NJ):
                            for u in range(n_tiles[j]):
                                for x in PLAN[j][u]:
                                    item(g, g + 1, 1 - par, x, AT1)
                            w = width(j)
                            dve.wait_ge(pv_done, tiles_before(g) + first[j] + n_tiles[j])
                            nc.vector.tensor_copy(O[:, (par + j) % 2, 0:w], ACC[:, 0:w]).then_inc(acc_read, 1)
                        item(g, g + 1, 1 - par, ("final", NJ - 1), AT1)
                dve.wait_ge(out_done, NB * NJ + 1)


HID = 128
MAGIC = 0x5F3759DF


def rsqrt_steps(nc, y, v, t, step):
    step(nc.vector.tensor_single_scalar(y.bitcast(I32), v.bitcast(I32), 1, ALU.logical_shift_right))
    step(nc.vector.tensor_scalar(y.bitcast(I32), y.bitcast(I32), -1.0, float(MAGIC), ALU.mult, ALU.add))
    for _ in range(3):
        step(nc.vector.tensor_tensor(t, y, y, ALU.mult))
        step(nc.vector.tensor_tensor(t, t, v, ALU.mult))
        step(nc.vector.tensor_scalar(t, t, -0.5, 1.5, ALU.mult, ALU.add))
        step(nc.vector.tensor_tensor(y, y, t, ALU.mult))


RSQRT_STEPS = 14


def token_mlps(nc, m, k, w, eps, tag):
    QD = 4
    NQ = m.NB // QD
    PAIR = 2 if NQ % 2 == 0 else 1
    QB, TB = 512, 4
    NF = -(-NT // TB)
    W = NT * QD

    def rows(t):
        return P if t < NT - 1 else LAST

    def span(f):
        return QB * f, min(QB * (f + 1), S)

    with ExitStack() as ctx:
        def sb(name, shape, dt=F32):
            return ctx.enter_context(nc.sbuf_tensor(f"{tag}_{name}", shape, dt))

        def pb(name, shape, dt=F32):
            return ctx.enter_context(nc.psum_tensor(f"{tag}_{name}", shape, dt))

        def sem(name):
            return ctx.enter_context(nc.semaphore(f"{tag}_{name}"))

        X = [sb(f"x{s}", [P, NT, QD, C]) for s in range(PAIR)]
        SQ = [sb(f"sq{s}", [P, NT, QD, C]) for s in range(PAIR)]
        XT = [sb(f"xT{s}", [P, S]) for s in range(PAIR)]
        MEAN, VAR, RT, TM = [sb(n, [P, W]) for n in ("mean", "var", "rt", "tm")]
        RH, RT_RING, RU = 3, 2, 2
        HS = [sb(f"hs{i}", [P, QB]) for i in range(4)]
        W1 = [sb(f"w1{n}", [P, HID]) for n in "ab"]
        W2 = [sb(f"w2{n}", [HID, C]) for n in "ab"]
        B1 = [sb(f"b1{n}", [HID, 1]) for n in "ab"]
        GC = [sb(f"gc{n}", [P, 1]) for n in "ab"]
        BC = [sb(f"bc{n}", [C, 1]) for n in "ab"]
        DG = [sb(f"dg{n}", [P, P]) for n in "ab"]
        BR = [sb(f"br{n}", [P, QB], BF16) for n in "ab"]
        ONES = sb("ones", [P, P], BF16)
        ROW = {n: sb(f"row_{n}", [P, C]) for n in
               ("bo_time", "g2", "be2", "bo_recv", "g4", "be4", "be1", "be3", "b2a", "b2b")}
        PT_ = [sb(f"part{i}", [P, C], BF16) for i in range(3)]
        RM_ = sb("rem", [P, C])
        TR = [pb(f"tr{i}", [P, QB]) for i in range(RT_RING)]
        H = [pb(f"h{i}", [P, QB]) for i in range(RH)]
        U = [pb(f"u{i}", [P, QB]) for i in range(RU)]

        w_in, w_mm, w_step = sem("w_in"), sem("w_mm"), sem("w_step")
        with nc.Block() as block:
            @block.sync
            def _(sp):
                n = 0
                for i, x in enumerate("ab"):
                    g, be = ("g1", "be1") if x == "a" else ("g3", "be3")
                    for b in range(QD):
                        sp.dma_start(W1[i][b * C:(b + 1) * C, :], w["W1" + x]).then_inc(w_in, 16)
                        sp.dma_start(GC[i][b * C:(b + 1) * C, :], w[g][:, None]).then_inc(w_in, 16)
                    sp.dma_start(W2[i][:], w["W2" + x]).then_inc(w_in, 16)
                    sp.dma_start(B1[i][:], w["b1" + x][:, None]).then_inc(w_in, 16)
                    sp.dma_start(BC[i][:], w[be][:, None]).then_inc(w_in, 16)
                    n += 11
                for name, t in ROW.items():
                    sp.dma_start(t[:], w[name][None, :].to_broadcast([P, C])).then_inc(w_in, 16)
                    n += 1
                assert n == 32

            @block.tensor
            def _(pe):
                pe.wait_ge(w_in, 16 * 32)
                for i in range(2):
                    nc.tensor.matmul(U[i][:, 0:1], W1[i][0:C, :], BC[i][:], start=True, stop=True).then_inc(w_mm, 1)

            @block.vector
            def _(dve):
                n = [0]

                def step(ins):
                    n[0] += 1
                    ins.then_inc(w_step, 1)
                    dve.wait_ge(w_step, n[0])

                dve.wait_ge(w_in, 16 * 32)
                dve.wait_ge(w_mm, 2)
                step(nc.vector.memset(ONES[:], 1.0))
                for i in range(2):
                    step(nc.vector.tensor_tensor(B1[i][:], B1[i][:], U[i][:, 0:1], ALU.add))
                    step(nc.vector.tensor_scalar(W1[i][:], W1[i][:], GC[i][:], None, ALU.mult))
                    step(nc.vector.tensor_scalar(DG[i][:], k.ident[:], GC[i][:], None, ALU.mult))
                    be, b2 = ROW["be1" if i == 0 else "be3"], ROW["b2a" if i == 0 else "b2b"]
                    step(nc.vector.tensor_tensor(RM_[:], be[:], b2[:], ALU.add))
                    step(nc.vector.memset(BR[i][:], 0.0))
                    for q in range(3):
                        step(nc.vector.tensor_copy(PT_[q][:], RM_[:]))
                        step(nc.vector.tensor_tensor(RM_[:], RM_[:], PT_[q][:], ALU.subtract))
                        step(nc.vector.tensor_copy(
                            BR[i][32 * q:32 * q + 1, :].rearrange("p (r c) -> p r c", c=C),
                            PT_[q][32 * q:32 * q + 1, None, :].to_broadcast([1, QB // C, C])))
                step(nc.vector.tensor_tensor(ROW["be2"][:], ROW["be2"][:], ROW["bo_recv"][:], ALU.add))

        added = sem("added")
        centred, squared = sem("centred"), sem("squared")
        vec = sem("vec")
        normed = sem("normed")
        affine = sem("affine")
        pool_step = sem("pool_step")
        tr_full, tr_read = sem("tr_full"), sem("tr_read")
        h_full, gelu_done = sem("h_full"), sem("gelu_done")
        parts_done, u_read = sem("parts_done"), sem("u_read")
        LNS = [(s, 1) for s in range(PAIR)]
        for s in range(PAIR):
            LNS += [(s, 2), (s, 3)]
        LNS += [(s, 4) for s in range(PAIR)]
        NL = len(LNS)
        MLPS = [(s, i) for i in range(2) for s in range(PAIR)]
        NM_ = len(MLPS)
        N = NF * QD
        VS = NL * (4 + RSQRT_STEPS)

        with nc.Fori(0, NQ // PAIR) as o:
            with nc.Block() as block:
                @block.gpsimd
                def _(pool):
                    steps = [0]

                    def step(ins):
                        steps[0] += 1
                        ins.then_inc(pool_step, 1)
                        pool.wait_ge(pool_step, o * (PAIR * 2) + steps[0])

                    for s in range(PAIR):
                        img = bass.ds((o * PAIR + s) * QD, QD)
                        nc.gpsimd.tensor_tensor(X[s][:], m.T[:, img].rearrange("p b t c -> p t b c"),
                                                ROW["bo_time"][:, None, None, :].to_broadcast([P, NT, QD, C]),
                                                ALU.add).then_inc(added, 1)
                    aff = 0
                    for n, (s, which) in enumerate(LNS):
                        pool.wait_ge(centred, o * NL + n + 1)
                        nc.gpsimd.tensor_tensor(SQ[s][:], X[s][:], X[s][:], ALU.mult).then_inc(squared, 1)
                        if which in (2, 4):
                            pool.wait_ge(normed, o * NL + n + 1)
                            row = [ROW[f"{x}{which}"][:, None, None, :].to_broadcast([P, NT, QD, C])
                                   for x in ("g", "be")]
                            img = bass.ds((o * PAIR + s) * QD, QD)
                            out = X[s][:] if which == 2 else m.T[:, img].rearrange("p b t c -> p t b c")
                            step(nc.gpsimd.tensor_tensor(X[s][:], X[s][:], row[0], ALU.mult))
                            if which == 4:
                                pool.nop(nofuse=True)
                                nc.gpsimd.tensor_tensor(m.T[:, img, 0:NT - 1].rearrange("p b t c -> p t b c"),
                                                        X[s][:, 0:NT - 1],
                                                        ROW["be4"][:, None, None, :].to_broadcast([P, NT - 1, QD, C]),
                                                        ALU.add)
                                nc.gpsimd.tensor_tensor(m.T[0:LAST, img, NT - 1],
                                                        X[s][0:LAST, NT - 1],
                                                        ROW["be4"][0:LAST, None, :].to_broadcast([LAST, QD, C]),
                                                        ALU.add).then_inc(affine, 1)
                            else:
                                nc.gpsimd.tensor_tensor(X[s][:], X[s][:], row[1], ALU.add).then_inc(affine, 1)
                            aff += 1
                    pool.wait_ge(affine, o * (2 * PAIR) + aff)
                    pool.nop(nofuse=True)

                @block.vector
                def _(dve):
                    steps = [0]

                    def step(ins):
                        steps[0] += 1
                        ins.then_inc(vec, 1)
                        dve.wait_ge(vec, o * VS + steps[0])

                    for n, (s, which) in enumerate(LNS):
                        x = X[s][:].rearrange("p t b c -> p (t b) c")
                        sq = SQ[s][:].rearrange("p t b c -> p (t b) c")
                        wide = [P, W, C]
                        if which == 1:
                            dve.wait_ge(added, o * PAIR + s + 1)
                        elif which == 3:
                            dve.wait_ge(affine, o * 2 * PAIR + s + 1)
                        else:
                            mlp = MLPS.index((s, which // 2 - 1))
                            dve.wait_ge(u_read, (o * NM_ + mlp + 1) * NF)
                        step(nc.vector.tensor_reduce(MEAN[:], x, AX.X, ALU.add))
                        step(nc.vector.tensor_scalar(MEAN[:], MEAN[:], 1.0 / C, None, ALU.mult))
                        nc.vector.tensor_tensor(x, x, MEAN[:][:, :, None].to_broadcast(wide),
                                                ALU.subtract).then_inc(centred, 1)
                        dve.wait_ge(squared, o * NL + n + 1)
                        step(nc.vector.tensor_reduce(VAR[:], sq, AX.X, ALU.add))
                        step(nc.vector.tensor_scalar(VAR[:], VAR[:], 1.0 / C, eps, ALU.mult, ALU.add))
                        rsqrt_steps(nc, RT[:], VAR[:], TM[:], step)
                        nc.vector.tensor_tensor(x, x, RT[:][:, :, None].to_broadcast(wide),
                                                ALU.mult).then_inc(normed, 1)
                        dve.wait_ge(normed, o * NL + n + 1)
                        dve.nop(nofuse=True)

                @block.tensor
                def _(pe):
                    for q, (s, i) in enumerate(MLPS):
                        t0 = q * NF
                        n0 = q * N
                        pe.wait_ge(normed, o * NL + LNS.index((s, 1 if i == 0 else 3)) + 1)

                        def flip(f):
                            if t0 + f >= RT_RING:
                                pe.wait_ge(tr_read, o * (NM_ * NF) + t0 + f - RT_RING + 1)
                                pe.nop(nofuse=True)
                            for t in range(TB * f, min(TB * f + TB, NT)):
                                r = rows(t)
                                last = nc.tensor.transpose(TR[(t0 + f) % RT_RING][:, (t % TB) * P:(t % TB) * P + r],
                                                           X[s][0:r, t].rearrange("p b c -> p (b c)"),
                                                           k.ident[0:r, 0:r])
                            last.then_inc(tr_full, 1)

                        def second(n):
                            f, b = n // QD, n % QD
                            bank = U[(t0 + f) % RU]
                            tiles = range(TB * f, min(TB * f + TB, NT))
                            width = len(tiles) * P
                            r = rows(tiles[0])
                            if b == 0:
                                if t0 + f >= RU:
                                    pe.wait_ge(u_read, o * (NM_ * NF) + t0 + f - RU + 1)
                                nc.tensor.matmul(bank[0:r, 0:width], ONES[0:65, 0:r], BR[i][0:65, 0:width],
                                                 start=True, stop=False)
                                for t in tiles:
                                    c0 = (t % TB) * P
                                    nc.tensor.matmul(bank[0:r, c0:c0 + P], XT[s][:, t * P:t * P + r], DG[i][:],
                                                     start=False, stop=False)
                            pe.wait_ge(gelu_done, o * (NM_ * N) + n0 + n + 1)
                            for t in tiles:
                                c0 = (t % TB) * P + b * C
                                last = nc.tensor.matmul(bank[0:r, c0:c0 + C],
                                                        HS[(n0 + n) % 4][:, (t % TB) * P:(t % TB) * P + r], W2[i][:],
                                                        start=False, stop=(b == QD - 1 and t == tiles[-1]))
                            last.then_inc(parts_done, 1)

                        flip(0)
                        for n in range(N):
                            f, b = n // QD, n % QD
                            lo, hi = span(f)
                            if b == 0:
                                if f + 1 < NF:
                                    flip(f + 1)
                                pe.wait_ge(tr_read, o * (NM_ * NF) + t0 + f + 1)
                            if n0 + n >= RH:
                                pe.wait_ge(gelu_done, o * (NM_ * N) + n0 + n - RH + 1)
                            nc.tensor.matmul(H[(n0 + n) % RH][:, 0:hi - lo], W1[i][b * C:(b + 1) * C, :],
                                             XT[s][b * C:(b + 1) * C, lo:hi], start=True, stop=True).then_inc(h_full, 1)
                            if n >= 2:
                                second(n - 2)
                        second(N - 2)
                        second(N - 1)

                @block.scalar
                def _(act):
                    nc.scalar.preload_act_table(ACT.Gelu)
                    for q, (s, i) in enumerate(MLPS):
                        t0, n0 = q * NF, q * N

                        def take_flip(f):
                            lo, hi = span(f)
                            act.wait_ge(tr_full, o * (NM_ * NF) + t0 + f + 1)
                            nc.scalar.copy(XT[s][:, lo:hi], TR[(t0 + f) % RT_RING][:, 0:hi - lo]).then_inc(tr_read, 1)

                        def take_out(f):
                            act.wait_ge(parts_done, o * (NM_ * N) + n0 + QD * f + QD)
                            bank = U[(t0 + f) % RU]
                            if f < NF - 1:
                                ins = nc.scalar.copy(X[s][:, TB * f:TB * f + TB].rearrange("p t b c -> p (t b c)"), bank[:])
                            else:
                                ins = nc.scalar.copy(X[s][0:LAST, NT - 1].rearrange("p b c -> p (b c)"), bank[0:LAST, 0:P])
                            ins.then_inc(u_read, 1)

                        take_flip(0)
                        for n in range(N):
                            f, b = n // QD, n % QD
                            lo, hi = span(f)
                            if b == 0 and f + 1 < NF:
                                take_flip(f + 1)
                            act.wait_ge(h_full, o * (NM_ * N) + n0 + n + 1)
                            if n0 + n >= 4:
                                act.wait_ge(parts_done, o * (NM_ * N) + n0 + n - 3)
                            nc.scalar.activation(HS[(n0 + n) % 4][:, 0:hi - lo], H[(n0 + n) % RH][:, 0:hi - lo],
                                                 ACT.Gelu, bias=B1[i][:]).then_inc(gelu_done, 1)
                            if n >= 2 and (n - 2) % QD == QD - 1:
                                take_out((n - 2) // QD)
                        take_out(NF - 1)


IMG = 56
WS = 7
DISP = WS // 2
NW = IMG // WS
K = WS * WS
SLOT = 64
HEADS = 4


def window_attention(nc, m, k, wqkvT, pos, w_out, b_out, eps, tag):
    NB = m.NB
    HK = HEADS * K
    ROWC = NW * HK
    XR0, ONE, BIAS = 0, 32, 64
    KR = BIAS + K
    NF = -(-NT // 4)
    NBK = -(-NT // 16)
    SQ_, SK_ = 4, 3
    HALF = HK * 2

    def rows(t):
        return P if t < NT - 1 else LAST

    with ExitStack() as ctx:
        def sb(name, shape, dt=F32):
            return ctx.enter_context(nc.sbuf_tensor(f"{tag}_{name}", shape, dt))

        def pb(name, shape, dt=F32):
            return ctx.enter_context(nc.psum_tensor(f"{tag}_{name}", shape, dt))

        def sem(name):
            return ctx.enter_context(nc.semaphore(f"{tag}_{name}"))

        XW = sb("xw", [KR, 2, NW * NW, SLOT])
        MQ = sb("mq", [KR, SQ_, 2, NW // 2, HEADS, K])
        MK = sb("mk", [KR, SK_, 2, NW // 2, HEADS, K])
        XC = sb("xc", [P, NT, C])
        XR = sb("xr", [C, S])
        OT = sb("ot", [C, S])
        PT = sb("pt", [P, 2, 2 * HALF])
        RL = sb("rl", [P, 2, 2 * HALF])
        YB = sb("yb", [P, 2, NW // 2, HEADS, 2, C])
        NMX = sb("nmx", [P, 2, NW // 2 * HEADS])
        NMT = sb("nmt", [NW // 2 * HEADS, 2, P])
        BN = sb("bn", [C, NF, 6])
        MV = sb("mv", [C, 2])
        VE, RS, TM, SH = [sb(x, [C, 1]) for x in ("ve", "rs", "tm", "sh")]
        BO = sb("bo", [C, 1])
        ACAT, ATCAT, BCAT = [sb(x, [C, HEADS * C]) for x in ("acat", "atcat", "bcat")]
        WQT, WKT, WVT, WO = [sb(x, [C, HEADS, C]) for x in ("wqT", "wkT", "wvT", "wo")]
        BLOCK1 = sb("block1", [P, P])
        U4 = sb("u4", [33, 4, K], BF16)
        MSK = sb("msk", [P, 4, K])
        MSKT = sb("mskT", [P, 4, K])
        PQ, PK = pb("pq", [P, 512]), pb("pk", [P, 512])
        MXB = [pb(f"mx{i}", [P, 512]) for i in range(2)]
        SL = [pb(f"sl{i}", [P, 512]) for i in range(2)]
        YP = pb("yp", [P, 512])
        DP = pb("dp", [P, 512])

        w_in, w_mm, w_st, w_pl = sem("w_in"), sem("w_mm"), sem("w_st"), sem("w_pl")
        with nc.Block() as block:
            @block.sync
            def _(sp):
                for i, t in enumerate((WQT, WKT, WVT)):
                    sp.dma_start(t[:], wqkvT[i * P:(i + 1) * P, :].rearrange("(h d) c -> d h c", d=C)).then_inc(w_in, 16)
                sp.dma_start(WO[:], w_out.rearrange("(h d) c -> d h c", d=C)).then_inc(w_in, 16)
                sp.dma_start(BO[:], b_out[:, None]).then_inc(w_in, 16)
                for q in range(K):
                    a, b = WS - 1 - q // WS, WS - 1 - q % WS
                    sp.dma_start(MSK[BIAS + q:BIAS + q + 1, 0, :].rearrange("p (a b) -> p a b", a=WS),
                                 pos[None, a:a + WS, b:b + WS]).then_inc(w_in, 16)

            @block.gpsimd
            def _(pool):
                n = [0]

                def step(ins):
                    n[0] += 1
                    ins.then_inc(w_pl, 1)
                    pool.wait_ge(w_pl, n[0])

                step(nc.gpsimd.memset(BLOCK1[:], 1.0))
                for h, sign in ((0, -1), (1, 1)):
                    cols = BLOCK1[:, h * SLOT:(h + 1) * SLOT]
                    step(nc.gpsimd.affine_select(out=cols, in_=cols, compare_op=ALU.is_ge, fill=0.0,
                                                 base=K - 1 if h == 0 else -SLOT, pattern=[[0, SLOT]],
                                                 channel_multiplier=sign))
                cols = BLOCK1[:, SLOT:P]
                step(nc.gpsimd.affine_select(out=cols, in_=cols, compare_op=ALU.is_ge, fill=0.0,
                                             base=SLOT + K - 1, pattern=[[0, SLOT]], channel_multiplier=-1))
                step(nc.gpsimd.memset(XW[:], 0.0))
                step(nc.gpsimd.memset(MQ[:], 0.0))
                step(nc.gpsimd.memset(MK[:], 0.0))
                step(nc.gpsimd.memset(YB[:], 0.0))
                step(nc.gpsimd.memset(U4[:], 0.0))
                for i, v in enumerate((lambda t: t[:, :, 4:7], lambda t: t[:, 4:7, :])):
                    st = U4[:, 2 * i, :].rearrange("p (a b) -> p a b", a=WS)
                    mv = U4[:, 2 * i + 1, :].rearrange("p (a b) -> p a b", a=WS)
                    step(nc.gpsimd.memset(v(st[0:1]), 1.0))
                    step(nc.gpsimd.memset(st[32:33], 1.0))
                    step(nc.gpsimd.memset(v(st[32:33]), 0.0))
                    step(nc.gpsimd.memset(mv[0:1], NEG))
                    step(nc.gpsimd.memset(v(mv[0:1]), 0.0))
                    step(nc.gpsimd.memset(v(mv[32:33]), NEG))
                for s in range(2):
                    step(nc.gpsimd.memset(XW[ONE:ONE + 1, s, :, 0:K], 1.0))
                    idn = XW[BIAS:BIAS + K, s, :, 0:K]
                    step(nc.gpsimd.affine_select(out=idn, in_=idn, compare_op=ALU.not_equal, fill=1.0, base=0,
                                                 pattern=[[0, NW * NW], [-1, K]], channel_multiplier=1))

            @block.tensor
            def _(pe):
                pe.wait_ge(w_in, 16 * (5 + K))
                for h in range(HEADS):
                    o = slice(h * C, (h + 1) * C)
                    nc.tensor.matmul(PQ[0:C, o], WQT[:, h], WKT[:, h], start=True, stop=True)
                    nc.tensor.matmul(PK[0:C, o], WKT[:, h], WQT[:, h], start=True, stop=True)
                    nc.tensor.matmul(YP[0:C, o], WVT[:, h], WO[:, h], start=True, stop=True).then_inc(w_mm, 1)
                pe.wait_ge(w_pl, 21)
                for i in range(2):
                    nc.tensor.matmul(MXB[i][0:K, 0:K], U4[:, 2 * i, :], U4[:, 2 * i + 1, :],
                                     start=True, stop=True).then_inc(w_mm, 1)
                pe.wait_ge(w_st, 7)
                for i in range(4):
                    nc.tensor.transpose(SL[0][0:K, i * K:(i + 1) * K], MSK[BIAS:BIAS + K, i, :],
                                        k.ident[BIAS:BIAS + K, BIAS:BIAS + K]).then_inc(w_mm, 1)

            @block.vector
            def _(dve):
                n = [0]

                def step(ins):
                    n[0] += 1
                    ins.then_inc(w_st, 1)
                    dve.wait_ge(w_st, n[0])

                scale = float(C) ** -0.5
                dve.wait_ge(w_mm, HEADS)
                step(nc.vector.tensor_scalar(ACAT[:], PQ[0:C, 0:P], scale, None, ALU.mult))
                step(nc.vector.tensor_scalar(ATCAT[:], PK[0:C, 0:P], scale, None, ALU.mult))
                step(nc.vector.tensor_copy(BCAT[:], YP[0:C, 0:P]))
                dve.wait_ge(w_in, 16 * (5 + K))
                dve.wait_ge(w_mm, HEADS + 2)
                r = slice(BIAS, BIAS + K)
                step(nc.vector.tensor_tensor(MSK[r, 1], MSK[r, 0], MXB[0][0:K, 0:K], ALU.add))
                step(nc.vector.tensor_tensor(MSK[r, 2], MSK[r, 0], MXB[1][0:K, 0:K], ALU.add))
                step(nc.vector.tensor_tensor(MSK[r, 3], MSK[r, 1], MXB[1][0:K, 0:K], ALU.add))
                step(nc.vector.tensor_copy(TM[:], BO[:]))
                dve.wait_ge(w_mm, HEADS + 6)
                step(nc.vector.tensor_copy(MSKT[r].rearrange("p m c -> p (m c)"), SL[0][0:K, 0:4 * K]))
                for buf, src, n_slots in ((MQ, MSKT, SQ_), (MK, MSK, SK_)):
                    for s in range(n_slots):
                        low = 2 if s == n_slots - 1 else 0
                        for half in range(2):
                            step(nc.vector.tensor_copy(buf[r, s, half].rearrange("p w h c -> p (w h) c"),
                                                       src[r, low, None, :].to_broadcast([K, NW // 2 * HEADS, K])))
                        step(nc.vector.tensor_copy(buf[r, s, 1, NW // 2 - 1],
                                                   src[r, low + 1, None, :].to_broadcast([K, HEADS, K])))
                step(nc.vector.memset(XR[:], 0.0))

        yp_full, yp_read = sem("yp_full"), sem("yp_read")
        dp_full, dp_read = sem("dp_full"), sem("dp_read")
        prj_full = sem("prj_full")
        mq_ready, mk_ready = sem("mq_ready"), sem("mk_ready")
        mx_full, max_done = sem("mx_full"), sem("max_done")
        shift_in = sem("shift_in")
        s_full, exp_done, l_full, rec_done = sem("s_full"), sem("exp_done"), sem("l_full"), sem("rec_done")
        pt_ready, pv_done = sem("pt_ready"), sem("pv_done")
        xc_ready = sem("xc_ready")
        bn_done, stat_step, stat_done, xw_ready = sem("bn_done"), sem("stat_step"), sem("stat_done"), sem("xw_ready")

        YP_ITEMS = [[("y", i)] + ([("xT", f) for f in range(2 * i, min(2 * i + 2, NF))]) for i in range(NW)]
        yp_at = {x: n for n, x in enumerate(x for r in YP_ITEMS for x in r)}
        YPN = len(yp_at)
        DP_ITEMS = [([("pv", i - 1)] if i else []) + [("nmT", i)] for i in range(NW)]
        DP_ITEMS[-1] += [("pv", NW - 1)] + [("back", f) for f in range(NBK)]
        dp_at = {x: n for n, x in enumerate(x for r in DP_ITEMS for x in r)}
        DPN = len(dp_at)
        STATS = 3 + RSQRT_STEPS
        PRE_YP, PRE_DP = NF, 1

        def yp_base(g):
            return g * YPN + PRE_YP

        def dp_base(g):
            return g * DPN + PRE_DP

        def q_slot(par, i):
            return SQ_ - 1 if i == NW - 1 else ((NW - 1) * par + i) % (SQ_ - 1)

        def k_slot(i):
            return SK_ - 1 if i == NW - 1 else i % (SK_ - 1)

        with nc.Block() as block:
            @block.tensor
            def _(pe):
                def flip(img, base, f, at):
                    pe.wait_ge(yp_read, base + at + 1)
                    if f == 0:
                        pe.wait_ge(xc_ready, img + 1)
                    for t in range(4 * f, min(4 * f + 4, NT)):
                        c0 = (t % 4) * P
                        last = nc.tensor.transpose(YP[0:C, c0:c0 + P], XC[:, t, :], k.ident[:])
                    last.then_inc(yp_full, 1)

                def project(n, par, i, img):
                    pe.wait_ge(mq_ready, n + 1)
                    pe.wait_ge(mk_ready, n + 1)
                    if i == 0:
                        pe.wait_ge(xw_ready, img + 1)
                    x = XW[0:C, par, i * NW:(i + 1) * NW, 0:K]
                    nc.tensor.matmul(PQ[:, 0:NW * K], ACAT[:], x, start=True, stop=True)
                    nc.tensor.matmul(PK[:, 0:NW * K], ATCAT[:], x, start=True, stop=True).then_inc(prj_full, 1)

                def pairs(banks, par, i, buf, slot):
                    for p in range(NW // 2):
                        bank = banks[p // 2]
                        c0 = (p % 2) * HK
                        for half in range(2):
                            w = 2 * p + half
                            last = nc.tensor.matmul(bank[half * SLOT:(half + 1) * SLOT, c0:c0 + HK],
                                                    XW[:, par, i * NW + w, :],
                                                    buf[:, slot, half, p].rearrange("p h c -> p (h c)"),
                                                    start=True, stop=True)
                        yield last

                def maxima(n, par, i):
                    pe.wait_ge(mk_ready, n + 2)
                    pe.wait_ge(max_done, n + 1)
                    for last in pairs(MXB, par, i, MK, k_slot(i)):
                        pass
                    last.then_inc(mx_full, 1)

                def max_flip(n, base, at, i):
                    pe.wait_ge(dp_read, base + at + 1)
                    pe.wait_ge(max_done, n + 2)
                    nc.tensor.transpose(DP[0:NW // 2 * HEADS, 0:P], NMX[:, i % 2, :], k.ident[:]).then_inc(dp_full, 1)

                def weigh(g, par, i, at):
                    n = g * NW + i
                    pe.wait_ge(dp_read, dp_base(g) + at + 1)
                    pe.wait_ge(pt_ready, n + 1)
                    pe.wait_ge(yp_read, yp_base(g) + yp_at[("y", i)] + 2)
                    for p in range(NW // 2):
                        o0, c0 = (p % 2) * SLOT, (p // 2) * K
                        for h in range(HEADS):
                            last = nc.tensor.matmul(DP[o0:o0 + 2 * C, c0:c0 + K],
                                                    YB[:, i % 2, p, h].rearrange("p a c -> p (a c)"),
                                                    PT[:, i % 2, p * HK + h * K:p * HK + (h + 1) * K],
                                                    start=(h == 0), stop=(h == HEADS - 1))
                    last.then_inc(dp_full, 1)

                for f in range(NF):
                    flip(0, 0, f, f)
                for i in range(2):
                    project(i, 0, i, 0)
                    maxima(i, 0, i)
                max_flip(0, 0, 0, 0)
                with pe.Fori(0, NB // 2) as pair_of:
                    for par in range(2):
                        g = pair_of * 2 + par
                        for i in range(NW):
                            n = g * NW + i
                            i2, par2 = (i + 2) % NW, par if i + 2 < NW else 1 - par
                            pe.wait_ge(mq_ready, n + 2)
                            pe.wait_ge(shift_in, (n + 1) * 32 + 1)
                            pe.wait_ge(rec_done, 2 * n + 1)
                            for p, last in enumerate(pairs(SL, par, i, MQ, q_slot(par, i))):
                                if p % 2:
                                    last.then_inc(s_full, 1)
                            project(n + 2, par2, i2, g + 1)
                            for x in YP_ITEMS[i]:
                                if x[0] == "xT":
                                    flip(g + 1, yp_base(g), x[1], yp_at[x])
                                    continue
                                pe.wait_ge(yp_read, yp_base(g) + yp_at[x] + 1)
                                for p in range(NW // 2):
                                    for half in range(2):
                                        last = nc.tensor.matmul(YP[half * SLOT:(half + 1) * SLOT, p * P:(p + 1) * P],
                                                                XW[0:C, par, i * NW + 2 * p + half, :], BCAT[:],
                                                                start=True, stop=True)
                                last.then_inc(yp_full, 1)
                            if i:
                                weigh(g, par, i - 1, dp_at[("pv", i - 1)])
                            for b in range(2):
                                pe.wait_ge(exp_done, 2 * n + b + 1)
                                nc.tensor.matmul(SL[b][:, 0:HALF], BLOCK1[:], PT[:, i % 2, b * HALF:(b + 1) * HALF],
                                                 start=True, stop=True).then_inc(l_full, 1)
                            max_flip(n + 1, dp_base(g), dp_at[("nmT", i)], i + 1)
                            maxima(n + 2, par2, i2)
                            if i == NW - 1:
                                weigh(g, par, i, dp_at[("pv", i)])
                                for f in range(NBK):
                                    pe.wait_ge(dp_read, dp_base(g) + dp_at[("back", f)] + 1)
                                    for t in range(16 * f, min(16 * f + 16, NT)):
                                        c0, r = (t % 16) * C, rows(t)
                                        if t == 16 * f:
                                            nc.tensor.matmul(DP[0:r, c0:c0 + C], OT[:, t * P:t * P + r],
                                                             k.ident[0:C, 0:C], start=True, stop=True)
                                        else:
                                            last = nc.tensor.transpose(DP[0:r, c0:c0 + C], OT[:, t * P:t * P + r],
                                                                       k.ident[0:C, 0:C])
                                    last.then_inc(dp_full, 1)

            @block.scalar
            def _(act):
                act.sem_inc(yp_read, 1)
                act.sem_inc(mq_ready, 1)

                def take_flip(base, f, at):
                    lo, hi = 512 * f, min(512 * f + 512, S)
                    act.wait_ge(yp_full, base + at + 1)
                    nc.scalar.copy(XR[:, lo:hi], YP[0:C, 0:hi - lo]).then_inc(yp_read, 1)

                def fill_q(n, par, i):
                    act.wait_ge(prj_full, n + 1)
                    for h in range(HEADS):
                        last = nc.scalar.copy(MQ[0:C, q_slot(par, i), :, :, h, :],
                                              PQ[h * C:(h + 1) * C, 0:NW * K].rearrange("p (w f c) -> p f w c", f=2, c=K))
                    last.then_inc(mq_ready, 1)

                nc.scalar.preload_act_table(ACT.Exp)
                for f in range(NF):
                    take_flip(0, f, f)
                for i in range(2):
                    fill_q(i, 0, i)
                with act.Fori(0, NB // 2) as pair_of:
                    for par in range(2):
                        g = pair_of * 2 + par
                        for i in range(NW):
                            n = g * NW + i
                            act.wait_ge(pv_done, n + 1)
                            for b in range(2):
                                act.wait_ge(s_full, 2 * n + b + 1)
                                nc.scalar.activation(PT[:, i % 2, b * HALF:(b + 1) * HALF], SL[b][:, 0:HALF],
                                                     ACT.Exp).then_inc(exp_done, 1)
                            fill_q(n + 2, par if i + 2 < NW else 1 - par, (i + 2) % NW)
                            for x in YP_ITEMS[i]:
                                if x[0] == "xT":
                                    if x[1] == 0:
                                        act.wait_ge(xw_ready, g + 1)
                                    take_flip(yp_base(g), x[1], yp_at[x])
                                    continue
                                act.wait_ge(yp_full, yp_base(g) + yp_at[x] + 1)
                                for half in range(2):
                                    r = slice(half * SLOT, (half + 1) * SLOT)
                                    last = nc.scalar.copy(YB[r, i % 2, :, :, half, :].rearrange("p a h c -> p (a h) c"),
                                                          YP[r, :].rearrange("p (a c) -> p a c", c=C))
                                last.then_inc(yp_read, 1)

            @block.vector
            def _(dve):
                for s in (dp_read, mk_ready, max_done, rec_done, pv_done, stat_step):
                    dve.sem_inc(s, 1)
                dve.sem_inc(pv_done, 1)

                def fill_k(n, i):
                    dve.wait_ge(prj_full, n + 1)
                    for h in range(HEADS):
                        last = nc.vector.tensor_copy(MK[0:C, k_slot(i), :, :, h, :],
                                                     PK[h * C:(h + 1) * C, 0:NW * K].rearrange("p (w f c) -> p f w c", f=2, c=K))
                    last.then_inc(mk_ready, 1)

                def take_max(n, i):
                    dve.wait_ge(mx_full, n + 1)
                    for b in range(2):
                        last = nc.vector.tensor_reduce(NMX[:, i % 2, b * 2 * HEADS:(b + 1) * 2 * HEADS],
                                                       MXB[b][:, 0:HALF].rearrange("p (a c) -> p a c", c=K),
                                                       AX.X, ALU.max, negate=True)
                    last.then_inc(max_done, 1)

                def take_flip(n, base, at, i):
                    dve.wait_ge(dp_full, base + at + 1)
                    if not isinstance(n, int):
                        dve.wait_ge(shift_in, (n - 1) * 32 + 1)
                    nc.vector.tensor_copy(NMT[:, i % 2, :], DP[0:NW // 2 * HEADS, 0:P]).then_inc(dp_read, 1)

                def stats(img):
                    base = img * STATS + 1
                    n = [0]

                    def step(ins):
                        n[0] += 1
                        ins.then_inc(stat_step, 1)
                        dve.wait_ge(stat_step, base + n[0])

                    dve.wait_ge(bn_done, (img + 1) * NF)
                    nc.vector.memset(VE[:], 0.0)
                    step(nc.vector.bn_aggr(MV[:], BN[:].rearrange("p a b -> p (a b)")))
                    step(nc.vector.tensor_scalar(VE[:], MV[:, 1:2], eps, None, ALU.add))
                    rsqrt_steps(nc, RS[:], VE[:], TM[:], step)
                    step(nc.vector.tensor_tensor(TM[:], MV[:, 0:1], RS[:], ALU.mult))
                    nc.vector.tensor_scalar(SH[:], TM[:], -1.0, None, ALU.mult).then_inc(stat_done, 1)
                    dve.wait_ge(stat_done, img + 1)

                def bn(base, f, at):
                    lo, hi = 512 * f, min(512 * f + 512, S)
                    dve.wait_ge(yp_read, base + at + 2)
                    nc.vector.bn_stats(BN[:, f, :], XR[:, lo:hi]).then_inc(bn_done, 1)

                def take_out(g, par, i):
                    dve.wait_ge(dp_full, dp_base(g) + dp_at[("pv", i)] + 1)
                    y0 = WS * i + DISP
                    parts = [(0, WS, y0)] if i < NW - 1 else [(0, WS - DISP, y0), (WS - DISP, DISP, 0)]
                    told = False
                    for r0, nr, y in parts:
                        out = OT[:, y * IMG:(y + nr) * IMG].rearrange("c (y x) -> c y x", x=IMG)
                        for b in range(4):
                            blk = DP[b * C:(b + 1) * C, 0:2 * K].rearrange("c (g y x) -> c g y x", g=2, x=WS)
                            for gr in range(2):
                                j = 4 * gr + b
                                x0 = WS * j + DISP
                                cols = [(0, WS, x0)] if j < NW - 1 else [(0, WS - DISP, x0), (WS - DISP, DISP, 0)]
                                for c0, ncol, x in cols:
                                    last = nc.vector.tensor_scalar(out[:, :, x:x + ncol],
                                                                   blk[:, gr, r0:r0 + nr, c0:c0 + ncol],
                                                                   BO[:], None, ALU.add)
                                    if not told:
                                        last.then_inc(pv_done, 1)
                                        told = True
                    last.then_inc(dp_read, 1)

                def out_rows(g, f):
                    lo, hi = 16 * f, min(16 * f + 16, NT)
                    full = min(hi, NT - 1)
                    dve.wait_ge(dp_full, dp_base(g) + dp_at[("back", f)] + 1)
                    if hi > full:
                        t = m.T[0:LAST, g, full, :]
                        nc.vector.tensor_tensor(t, t, DP[0:LAST, (full - lo) * C:(hi - lo) * C], ALU.add)
                    t = m.T[:, g, lo:full, :].rearrange("p t c -> p (t c)")
                    nc.vector.tensor_tensor(t, t, DP[:, 0:(full - lo) * C], ALU.add).then_inc(dp_read, 1)

                for f in range(NF):
                    bn(0, f, f)
                stats(0)
                for i in range(2):
                    fill_k(i, i)
                    take_max(i, i)
                take_flip(0, 0, 0, 0)
                with dve.Fori(0, NB // 2) as pair_of:
                    for par in range(2):
                        g = pair_of * 2 + par
                        for i in range(NW):
                            n = g * NW + i
                            fill_k(n + 2, (i + 2) % NW)
                            for x in YP_ITEMS[i]:
                                if x[0] == "xT":
                                    bn(yp_base(g), x[1], yp_at[x])
                            if i == NF // 2 + 1:
                                stats(g + 1)
                            if i:
                                take_out(g, par, i - 1)
                            for b in range(2):
                                dve.wait_ge(l_full, 2 * n + b + 1)
                                nc.vector.reciprocal(RL[:, i % 2, b * HALF:(b + 1) * HALF],
                                                     SL[b][:, 0:HALF]).then_inc(rec_done, 1)
                            take_flip(n + 1, dp_base(g), dp_at[("nmT", i)], i + 1)
                            take_max(n + 2, i)
                            if i == NW - 1:
                                take_out(g, par, i)
                                for f in range(NBK):
                                    out_rows(g, f)

            @block.gpsimd
            def _(pool):
                def windows(img, par):
                    for i in range(NW):
                        y0 = WS * i + DISP
                        parts = [(0, WS, y0)] if i < NW - 1 else [(0, WS - DISP, y0), (WS - DISP, DISP, 0)]
                        for r0, nr, y in parts:
                            src = XR[:, y * IMG:(y + nr) * IMG].rearrange("c (y x) -> c y x", x=IMG)
                            for j0, nj, c0, ncol, x in ((0, NW - 1, 0, WS, DISP),
                                                        (NW - 1, 1, 0, WS - DISP, IMG - WS + DISP),
                                                        (NW - 1, 1, WS - DISP, DISP, 0)):
                                dst = XW[0:C, par, i * NW + j0:i * NW + j0 + nj, 0:K]\
                                    .rearrange("c j (y x) -> c y j x", x=WS)[:, r0:r0 + nr, :, c0:c0 + ncol]
                                if nj > 1:
                                    s = src[:, :, x:x + nj * WS].rearrange("c y (j x) -> c y j x", x=WS)
                                else:
                                    s = src[:, :, None, x:x + ncol]
                                last = nc.gpsimd.tensor_scalar(dst, s, RS[:], SH[:], ALU.mult, ALU.add)
                    last.then_inc(xw_ready, 1)

                def fetch(img):
                    nc.gpsimd.tensor_copy(XC[:], m.T[:, img]).then_inc(xc_ready, 1)

                fetch(0)
                pool.wait_ge(stat_done, 1)
                windows(0, 0)
                with pool.Fori(0, NB // 2) as pair_of:
                    for par in range(2):
                        g = pair_of * 2 + par
                        for i in range(NW):
                            n = g * NW + i
                            if i == 0:
                                fetch(g + 1)
                            pool.wait_ge(rec_done, 2 * n + 3)
                            nc.gpsimd.tensor_tensor(PT[:, i % 2, :], PT[:, i % 2, :], RL[:, i % 2, :],
                                                    ALU.mult).then_inc(pt_ready, 1)
                            if i == NF // 2 + 1:
                                windows(g + 1, 1 - par)

            @block.sync
            def _(sp):
                def send(n, par, i):
                    for half in range(2):
                        sp.dma_start(MQ[ONE:ONE + 1, q_slot(par, i), half].rearrange("o p h c -> o (p h) c"),
                                     NMT[:, i % 2, half * SLOT:half * SLOT + K]).then_inc(shift_in, 16)

                sp.sem_inc(shift_in, 1)
                sp.wait_ge(dp_read, 2)
                send(0, 0, 0)
                with sp.Fori(0, NB // 2) as pair_of:
                    for par in range(2):
                        g = pair_of * 2 + par
                        for i in range(NW):
                            sp.wait_ge(dp_read, dp_base(g) + dp_at[("nmT", i)] + 2)
                            sp.wait_ge(shift_in, 32 * (g * NW + i + 1) + 1)
                            send(g * NW + i + 1, par if i + 1 < NW else 1 - par, (i + 1) % NW)
                sp.wait_ge(shift_in, 32 * (NB * NW + 1) + 1)


E_ = 16
TOPK = 8
TAKEN = -3.0e38


def expert_choice(nc, m, k, gate_wT, gate_b, weight1, weight2, tag):
    QD = 4
    NH = 2
    NI = QD * NH
    NO = m.NB // NI
    QB = 512
    CH = -(-S // QB)
    TB = QB // P
    NB4 = -(-NT // TB)

    def rows(t):
        return P if t < NT - 1 else LAST

    def span(f):
        return QB * f, min(QB * (f + 1), S)

    with ExitStack() as ctx:
        def sb(name, shape, dt=F32):
            return ctx.enter_context(nc.sbuf_tensor(f"{tag}_{name}", shape, dt))

        def pb(name, shape, dt=F32):
            return ctx.enter_context(nc.psum_tensor(f"{tag}_{name}", shape, dt))

        def sem(name):
            return ctx.enter_context(nc.semaphore(f"{tag}_{name}"))

        XN = sb("xn", [P, NT, NI, C])
        XT = sb("xT", [P, S])
        LG = sb("lg", [P, S])
        EX = sb("ex", [P, S])
        WT = sb("wT", [P, NT, P])
        GW = sb("gw", [P, QD * E_])
        GB = sb("gb", [P, 1])
        W1 = sb("w1", [C + 1, E_, HID])
        W2 = sb("w2", [HID, E_, C])
        B2 = sb("b2", [C, E_])
        SAME = sb("same", [P, QD, C])
        M8 = sb("m8", [P, TOPK])
        NM = sb("nm", [P, 1])
        SUM = sb("sum", [P, 1])
        RS = sb("rs", [P, 1])
        PM = sb("pm", [P, QD, C])
        PL = sb("pl", [P, C])
        PN = sb("pn", [P, C])
        PT = sb("pT", [C + 1, E_, NI])
        HT = sb("hT", [HID, E_ * NI])
        OT = sb("oT", [C, NI, E_])
        OB = sb("ob", [P, C])
        OK = sb("ok", [P, QD, C])
        RING = 4
        R = [pb(f"r{i}", [P, QB]) for i in range(RING)]
        PP = pb("pp", [P, QD * C])
        SM = [pb(f"sm{i}", [P, P]) for i in range(3)]

        w_in, w_set = sem("w_in"), sem("w_set")
        with nc.Block() as block:
            @block.vector
            def _(dve):
                nc.vector.memset(GW[:], 0.0).then_inc(w_set, 1)
                nc.vector.memset(PT[:], 1.0).then_inc(w_set, 1)
                dve.wait_ge(w_set, 2)

            @block.gpsimd
            def _(pool):
                s1, s2 = sem("s1"), sem("s2")
                nc.gpsimd.memset(SAME[:], 1.0).then_inc(s1, 1)
                pool.wait_ge(s1, 1)
                n = 1
                for h in range(NH):
                    part = SAME[h * 64:(h + 1) * 64]
                    for sign, base in ((1, 0), (-1, E_ - 1)):
                        nc.gpsimd.affine_select(out=part, in_=part, compare_op=ALU.is_ge, fill=0.0, base=base,
                                                pattern=[[-sign * E_, QD], [0, C]],
                                                channel_multiplier=sign).then_inc(s1, 1)
                        n += 1
                        pool.wait_ge(s1, n)

            @block.sync
            def _(sp):
                sp.wait_ge(w_set, 1)
                for b in range(QD):
                    sp.dma_start(GW[b * C:(b + 1) * C, b * E_:(b + 1) * E_], gate_wT).then_inc(w_in, 16)
                for b in range(NI):
                    sp.dma_start(GB[b * E_:(b + 1) * E_, :], gate_b[:, None]).then_inc(w_in, 16)
                sp.dma_start(W1[:], weight1.rearrange("e d h -> d e h")).then_inc(w_in, 16)
                sp.dma_start(W2[:], weight2[:, 0:HID, :].rearrange("e h o -> h e o")).then_inc(w_in, 16)
                sp.dma_start(B2[:], weight2[:, HID, :].rearrange("e o -> o e"), allow_slow_non_contiguous=True).then_inc(w_in, 16)
                sp.wait_ge(w_in, 16 * (QD + NI + 3))

        norm_step = sem("norm_step")
        ring_full, ring_read_a, ring_read_v = sem("ring_full"), sem("ring_read_a"), sem("ring_read_v")
        vec, exp_done = sem("vec"), sem("exp_done")
        pooled_done, small_full, gelu_done = sem("pooled_done"), sem("small_full"), sem("gelu_done")
        FILLS = [(x, h, f) for h in range(NH) for x in ("xT", "lg") for f in range(NB4)]
        FILLS += [("wT", 0, f) for f in range(NB4)]
        N_A = len(FILLS)
        FILLS += [("out", h, f) for h in range(NH) for f in range(NB4)]
        N_V = len(FILLS) - N_A
        N_ALL = N_A + N_V
        VEC = 13

        with nc.Fori(0, NO) as o:
            with nc.Block() as block:
                @block.tensor
                def _(pe):
                    def free(n):
                        if n >= RING:
                            prev = n - RING
                            if prev < N_A:
                                pe.wait_ge(ring_read_a, o * N_A + prev + 1)
                            else:
                                pe.wait_ge(ring_read_v, o * N_V + prev - N_A + 1)

                    for n, (x, h, f) in enumerate(FILLS):
                        free(n)
                        pe.nop(nofuse=True)
                        bank = R[n % RING]
                        lo, hi = span(f)
                        if x == "xT":
                            if f == 0:
                                pe.wait_ge(norm_step, o * NH * 2 + 2 * h + 2)
                            for t in range(TB * f, min(TB * f + TB, NT)):
                                c0, r = (t % TB) * P, rows(t)
                                last = nc.tensor.transpose(bank[:, c0:c0 + r],
                                                           XN[0:r, t, QD * h:QD * (h + 1)].rearrange("p b c -> p (b c)"),
                                                           k.ident[0:r, 0:r])
                        elif x == "lg":
                            pe.wait_ge(ring_read_a, o * N_A + FILLS.index(("xT", h, f)) + 1)
                            pe.nop(nofuse=True)
                            last = nc.tensor.matmul(bank[64 * h:64 * h + 64, 0:hi - lo], GW[:], XT[:, lo:hi],
                                                    start=True, stop=True)
                        elif x == "wT":
                            if f == 0:
                                pe.wait_ge(vec, o * VEC + 4)
                                pe.nop(nofuse=True)
                            for t in range(TB * f, min(TB * f + TB, NT)):
                                c0, r = (t % TB) * P, rows(t)
                                last = nc.tensor.transpose(bank[0:r, c0:c0 + P], EX[:, t * P:t * P + r], k.ident[:])
                        else:
                            if n == N_A:
                                pe.wait_ge(ring_read_a, o * N_A + N_A)
                                for hh in range(NH):
                                    for t in range(NT):
                                        r = rows(t)
                                        s = nc.tensor.matmul(PP[64 * hh:64 * hh + 64, :],
                                                             WT[0:r, t, 64 * hh:64 * hh + 64],
                                                             XN[0:r, t, QD * hh:QD * (hh + 1)].rearrange("p b c -> p (b c)"),
                                                             start=(t == 0), stop=(t == NT - 1))
                                s.then_inc(pooled_done, 1)
                                pe.wait_ge(vec, o * VEC + 9)
                                nc.tensor.transpose(SM[0][0:C, :], PN[:], k.ident[:]).then_inc(small_full, 1)
                                pe.wait_ge(vec, o * VEC + 10)
                                for e in range(E_):
                                    s = nc.tensor.matmul(SM[1][:, e * NI:(e + 1) * NI], W1[:, e, :], PT[:, e, :],
                                                         start=True, stop=True)
                                s.then_inc(small_full, 1)
                                pe.wait_ge(gelu_done, o + 1)
                                for e in range(E_):
                                    s = nc.tensor.matmul(SM[2][0:C, e * NI:(e + 1) * NI], W2[:, e, :],
                                                         HT[:, e * NI:(e + 1) * NI], start=True, stop=True)
                                s.then_inc(small_full, 1)
                                pe.wait_ge(vec, o * VEC + 11)
                                pe.nop(nofuse=True)
                                nc.tensor.transpose(SM[0][:, 0:C], OT[:].rearrange("o b e -> o (b e)"),
                                                    k.ident[0:C, 0:C]).then_inc(small_full, 1)
                                pe.wait_ge(vec, o * VEC + 13)
                            for t in range(TB * f, min(TB * f + TB, NT)):
                                c0, r = (t % TB) * P, rows(t)
                                last = nc.tensor.matmul(bank[0:r, c0:c0 + P],
                                                        EX[64 * h:64 * h + 64, t * P:t * P + r],
                                                        OK[64 * h:64 * h + 64].rearrange("p b c -> p (b c)"),
                                                        start=True, stop=True)
                        last.then_inc(ring_full, 1)

                @block.scalar
                def _(act):
                    for n in range(N_A):
                        x, h, f = FILLS[n]
                        bank = R[n % RING]
                        lo, hi = span(f)
                        act.wait_ge(ring_full, o * N_ALL + n + 1)
                        if x == "xT":
                            if h and f == 0:
                                pass
                            ins = nc.scalar.copy(XT[:, lo:hi], bank[:, 0:hi - lo])
                        elif x == "lg":
                            ins = nc.scalar.activation(LG[64 * h:64 * h + 64, lo:hi], bank[64 * h:64 * h + 64, 0:hi - lo],
                                                       ACT.Identity, bias=GB[64 * h:64 * h + 64, :])
                        else:
                            if f == NB4 - 1:
                                ins = nc.scalar.copy(WT[0:LAST, NT - 1, :], bank[0:LAST, 0:P])
                            else:
                                ins = nc.scalar.copy(WT[:, TB * f:TB * f + TB, :].rearrange("p t e -> p (t e)"), bank[:])
                        ins.then_inc(ring_read_a, 1)
                        if n == NH * 2 * NB4 - 1:
                            act.wait_ge(vec, o * VEC + 2)
                            nc.scalar.activation(EX[:], LG[:], ACT.Exp, bias=NM[:],
                                                 accum_out=SUM[:]).then_inc(exp_done, 1)
                    act.wait_ge(small_full, o * 4 + 2)
                    nc.scalar.activation(HT[:], SM[1][:], ACT.Gelu).then_inc(gelu_done, 1)

                @block.vector
                def _(dve):
                    for h in range(NH):
                        img = bass.ds(o * NI + h * QD, QD)
                        xn = XN[:, :, QD * h:QD * (h + 1), :]
                        shape = [P, NT, QD, C]
                        nc.vector.tensor_tensor(
                            xn, m.T[:, img].rearrange("p b t c -> p t b c"),
                            m.mean[:, img].rearrange("p b t -> p t b")[:, :, :, None].to_broadcast(shape),
                            ALU.subtract).then_inc(norm_step, 1)
                        dve.wait_ge(norm_step, o * NH * 2 + 2 * h + 1)
                        nc.vector.tensor_tensor(
                            xn, xn, m.rstd[:, img].rearrange("p b t -> p t b")[:, :, :, None].to_broadcast(shape),
                            ALU.mult).then_inc(norm_step, 1)

                    n = [0]

                    def step(ins):
                        n[0] += 1
                        ins.then_inc(vec, 1)
                        dve.wait_ge(vec, o * VEC + n[0])

                    dve.wait_ge(ring_read_a, o * N_A + NH * 2 * NB4)
                    dve.nop(nofuse=True)
                    step(nc.vector.max(M8[:], LG[:]))
                    step(nc.vector.tensor_scalar(NM[:], M8[:, 0:1], -1.0, None, ALU.mult))
                    dve.wait_ge(exp_done, o + 1)
                    dve.nop(nofuse=True)
                    step(nc.vector.match_replace(LG[:], M8[:], LG[:], TAKEN))
                    step(nc.vector.scalar_tensor_tensor(out=EX[:], in0=LG[:], scalar=TAKEN, in1=EX[:],
                                                        op0=ALU.is_equal, op1=ALU.mult))
                    step(nc.vector.reciprocal(RS[:], SUM[:]))
                    dve.wait_ge(pooled_done, o + 1)
                    step(nc.vector.tensor_tensor(PM[:], PP[:].rearrange("p (b c) -> p b c", b=QD), SAME[:], ALU.mult))
                    step(nc.vector.tensor_reduce(PL[:], PM[:].rearrange("p b c -> p c b"), AX.X, ALU.add))
                    step(nc.vector.tensor_scalar(PN[:], PL[:], RS[:], None, ALU.mult))
                    step(nc.vector.tensor_copy(NM[:], RS[:]))
                    dve.wait_ge(small_full, o * 4 + 1)
                    step(nc.vector.tensor_copy(PT[0:C].rearrange("c e b -> c b e"),
                                               SM[0][0:C, :].rearrange("c (b e) -> c b e", e=E_)))
                    dve.wait_ge(small_full, o * 4 + 3)
                    step(nc.vector.tensor_tensor(OT[:].rearrange("o b e -> o e b"),
                                                 SM[2][0:C, :].rearrange("o (e b) -> o e b", b=NI),
                                                 B2[:][:, :, None].to_broadcast([C, E_, NI]), ALU.add))
                    dve.wait_ge(small_full, o * 4 + 4)
                    step(nc.vector.tensor_scalar(OB[:], SM[0][:, 0:C], RS[:], None, ALU.mult))
                    step(nc.vector.tensor_tensor(OK[:], SAME[:], OB[:][:, None, :].to_broadcast([P, QD, C]), ALU.mult))
                    assert n[0] == VEC
                    for i in range(N_V):
                        x, h, f = FILLS[N_A + i]
                        bank = R[(N_A + i) % RING]
                        r, nt = (P, TB) if f < NB4 - 1 else (LAST, 1)
                        dve.wait_ge(ring_full, o * N_ALL + N_A + i + 1)
                        t = m.T[0:r, bass.ds(o * NI + h * QD, QD), TB * f:TB * f + nt, :].rearrange("p b t c -> p t b c")
                        nc.vector.tensor_tensor(t, t, bank[0:r, 0:nt * P].rearrange("p (t b c) -> p t b c", t=nt, b=QD),
                                                ALU.add).then_inc(ring_read_v, 1)
                    dve.wait_ge(ring_read_v, o * N_V + N_V)
                    dve.nop(nofuse=True)


NB = 16


def load_images(nc, m, x):
    cleared, loaded = m.sem("T_cleared"), m.sem("T_loaded")
    with nc.Block() as block:
        @block.gpsimd
        def _(pool):
            nc.gpsimd.memset(m.T[:, m.NB], 0.0).then_inc(cleared, 1)
            pool.wait_ge(cleared, 1)
            nc.gpsimd.memset(m.T[LAST:P, :, NT - 1], 0.0).then_inc(cleared, 1)
            pool.wait_ge(cleared, 2)

        @block.sync
        def _(sp):
            for i in range(m.NB):
                sp.dma_start(m.T[:, i, 0:NT - 1, :],
                             x[i, 0:(NT - 1) * P, :].rearrange("(t p) c -> p t c", p=P)).then_inc(loaded, 16)
                sp.dma_start(m.T[0:LAST, i, NT - 1, :], x[i, (NT - 1) * P:S, :]).then_inc(loaded, 16)
            sp.wait_ge(loaded, 32 * m.NB)


def store_images(nc, m, out):
    stored = m.sem("T_stored")
    with nc.Block() as block:
        @block.sync
        def _(sp):
            for i in range(m.NB):
                sp.dma_start(out[i, 0:(NT - 1) * P, :].rearrange("(t p) c -> p t c", p=P),
                             m.T[:, i, 0:NT - 1, :]).then_inc(stored, 16)
                sp.dma_start(out[i, (NT - 1) * P:S, :], m.T[0:LAST, i, NT - 1, :]).then_inc(stored, 16)
            sp.wait_ge(stored, 32 * m.NB)


def program(nc, a, out):
    with ExitStack() as ctx:
        k = make_constants(nc, ctx)
        m = Shared()
        m.NB = NB
        m.sem = lambda name: ctx.enter_context(nc.semaphore(name))
        m.T = ctx.enter_context(nc.sbuf_tensor("T", [P, NB + 1, NT, C], F32))
        m.mean = ctx.enter_context(nc.sbuf_tensor("mean", [P, NB + 1, NT], F32))
        m.rstd = ctx.enter_context(nc.sbuf_tensor("rstd", [P, NB + 1, NT], F32))
        load_images(nc, m, a["x"])
        window_attention(nc, m, k, a["L0_conv_w_qkv"], a["L0_conv_pos_emb"], a["L0_conv_w_out"],
                         a["L0_conv_b_out"], 1e-5, "win")
        token_mlps(nc, m, k, {n[8:]: t for n, t in a.items() if n.startswith("L1_conv_")}, 1e-5, "mlp")
        for layer, wq, wk, wv in (("L2", "W_Q", "W_K", "W_V"), ("L3", "Wq", "Wk", "Wv")):
            token_stats(nc, m, 1e-5, f"{layer}as")
            causal_attention(nc, m, k, *(a[f"{layer}_attn_{w}"] for w in (wq, wk, wv)), f"{layer}a")
            token_stats(nc, m, 1e-5, f"{layer}fs")
            expert_choice(nc, m, k, *(a[f"{layer}_ffn_{w}"] for w in ("gate_w", "gate_b", "weight1", "weight2")),
                          f"{layer}f")
        store_images(nc, m, out)


TRANSPOSED = ("L0_conv_w_qkv", "L2_ffn_gate_w", "L3_ffn_gate_w", "L3_attn_Wq", "L3_attn_Wk", "L3_attn_Wv")
UNUSED = ("L1_conv_router", "L1_conv_bo_send")


def kernel(**inputs):
    import numpy as _np
    import concourse.bacc as _bacc
    from concourse import mybir as _mybir
    from concourse.bass_utils import run_bass_kernel_spmd as _run

    nc = _bacc.Bacc("TRN2", target_bir_lowering=False, num_devices=1)
    arrays, args = {}, {}
    for name, value in inputs.items():
        if name in UNUSED:
            continue
        v = _np.asarray(value)
        if name in TRANSPOSED:
            v = v.T
        if name == "x":
            v = v.reshape(NB, S, C)
        v = _np.ascontiguousarray(v)
        arrays[f"in_{name}"] = v
        args[name] = nc.dram_tensor(f"in_{name}", v.shape, _mybir.dt.from_np(v.dtype), kind="ExternalInput").ap()
    out = nc.dram_tensor("out_0", (NB, S, C), F32, kind="ExternalOutput").ap()
    program(nc, args, out)
    r = _run(nc, [arrays], core_ids=[0])
    return r.results[0]["out_0"].reshape(NB, IMG, IMG, C)
```

```python
from contextlib import ExitStack

import concourse.bass as bass
from concourse import mybir
from concourse.alu_op_type import AluOpType as ALU


class Shared:
    pass

F32, BF16, I32 = mybir.dt.float32, mybir.dt.bfloat16, mybir.dt.int32
ACT = mybir.ActivationFunctionType
AX = mybir.AxisListType

P = 128
C = 32
S = 56 * 56
NT = -(-S // P)
LAST = S - (NT - 1) * P
NEG = -1e30


def make_constants(nc, ctx):
    def sb(name, shape, dt):
        return ctx.enter_context(nc.sbuf_tensor(name, shape, dt))
    k = Shared()
    k.ident = sb("ident", [P, P], F32)
    k.ident_bf = sb("ident_bf", [P, P], BF16)
    k.mask_qk = sb("mask_qk", [P, P], BF16)
    k.mask_kq = sb("mask_kq", [P, 4 * P], BF16)
    k.basis = sb("basis", [C, 4 * C], F32)
    made = ctx.enter_context(nc.semaphore("const_made"))
    with nc.Block() as block:
        @block.gpsimd
        def _(pool):
            nc.gpsimd.memset(k.ident[:], 0.0).then_inc(made, 1)
            nc.gpsimd.memset(k.mask_qk[:], 0.0).then_inc(made, 1)
            nc.gpsimd.memset(k.mask_kq[:], 0.0).then_inc(made, 1)
            nc.gpsimd.memset(k.basis[:], 0.0).then_inc(made, 1)
            pool.wait_ge(made, 4)
            nc.gpsimd.affine_select(out=k.ident[:], in_=k.ident[:], compare_op=ALU.not_equal, fill=1.0,
                                    base=0, pattern=[[-1, P]], channel_multiplier=1).then_inc(made, 1)
            nc.gpsimd.affine_select(out=k.mask_qk[:], in_=k.mask_qk[:], compare_op=ALU.is_ge, fill=NEG,
                                    base=0, pattern=[[-1, P]], channel_multiplier=1).then_inc(made, 1)
            nc.gpsimd.affine_select(out=k.mask_kq[:], in_=k.mask_kq[:], compare_op=ALU.is_ge, fill=NEG,
                                    base=-3 * P, pattern=[[1, 4 * P]], channel_multiplier=-1).then_inc(made, 1)
            nc.gpsimd.affine_select(out=k.basis[:].rearrange("p (r c) -> p r c", r=4),
                                    in_=k.basis[:].rearrange("p (r c) -> p r c", r=4),
                                    compare_op=ALU.not_equal, fill=1.0,
                                    base=0, pattern=[[0, 4], [-1, C]], channel_multiplier=1).then_inc(made, 1)
            pool.wait_ge(made, 8)
            nc.gpsimd.memset(k.basis[0:1, :], -1.0).then_inc(made, 1)
            nc.gpsimd.tensor_copy(k.ident_bf[:], k.ident[:]).then_inc(made, 1)
            pool.wait_ge(made, 10)
            nc.gpsimd.memset(k.basis[:, 0:4 * C:C], 0.0).then_inc(made, 1)
            pool.wait_ge(made, 11)
    return k


def token_stats(nc, m, eps, tag):
    GB = min(4, m.NB)
    NG = m.NB // GB
    W = GB * NT
    with ExitStack() as ctx:
        def sem(name):
            return ctx.enter_context(nc.semaphore(f"{tag}_{name}"))
        cent = ctx.enter_context(nc.sbuf_tensor(f"{tag}_cent", [P, 2, W, C], F32))
        sq = ctx.enter_context(nc.sbuf_tensor(f"{tag}_sq", [P, 2, W, C], F32))
        var = ctx.enter_context(nc.sbuf_tensor(f"{tag}_var", [P, m.NB * NT], F32))
        sd = ctx.enter_context(nc.sbuf_tensor(f"{tag}_sd", [P, m.NB * NT], F32))
        summed, scaled, centred = sem("summed"), sem("scaled"), sem("centred")
        squared, var_summed, var_scaled = sem("squared"), sem("var_summed"), sem("var_scaled")
        rooted, pad_done = sem("rooted"), sem("pad_done")
        tok = [m.T[:, g * GB:(g + 1) * GB, :, :].rearrange("p b t c -> p (b t) c") for g in range(NG)]
        mean = [m.mean[:, g * GB:(g + 1) * GB, :].rearrange("p b t -> p (b t)") for g in range(NG)]
        with nc.Block() as block:
            @block.vector
            def _(dve):
                def sum_squares(g):
                    dve.wait_ge(squared, g + 1)
                    nc.vector.tensor_reduce(var[:, g * W:(g + 1) * W], sq[:, g % 2], AX.X,
                                            ALU.add).then_inc(var_summed, 1)

                for g in range(NG):
                    nc.vector.tensor_reduce(mean[g], tok[g], AX.X, ALU.add).then_inc(summed, 1)
                    dve.wait_ge(summed, g + 1)
                    nc.vector.tensor_scalar(mean[g], mean[g], 1.0 / C, None, ALU.mult).then_inc(scaled, 1)
                    dve.wait_ge(scaled, g + 1)
                    if g >= 2:
                        dve.wait_ge(squared, g - 1)
                    nc.vector.tensor_tensor(cent[:, g % 2], tok[g], mean[g][:, :, None].to_broadcast([P, W, C]),
                                            ALU.subtract).then_inc(centred, 1)
                    if g >= 1:
                        sum_squares(g - 1)
                sum_squares(NG - 1)
                dve.wait_ge(var_summed, NG)
                nc.vector.tensor_scalar(var[:], var[:], 1.0 / C, eps, ALU.mult, ALU.add).then_inc(var_scaled, 1)
                dve.wait_ge(rooted, 1)
                nc.vector.reciprocal(m.rstd[:, 0:m.NB, :].rearrange("p b t -> p (b t)"), sd[:]).then_inc(pad_done, 1)
                nc.vector.memset(m.mean[:, m.NB, :], 0.0).then_inc(pad_done, 1)
                nc.vector.memset(m.rstd[:, m.NB, :], 1.0).then_inc(pad_done, 1)
                dve.wait_ge(pad_done, 3)

            @block.scalar
            def _(act):
                for g in range(NG):
                    act.wait_ge(centred, g + 1)
                    if g >= 2:
                        act.wait_ge(var_summed, g - 1)
                    nc.scalar.activation(sq[:, g % 2], cent[:, g % 2], ACT.Square).then_inc(squared, 1)
                act.wait_ge(var_scaled, 1)
                nc.scalar.activation(sd[:], var[:], ACT.Sqrt).then_inc(rooted, 1)


def causal_attention(nc, m, k, wq, wk, wv, tag):
    NB = m.NB
    QB = 512
    NJ = -(-S // QB)
    QT = QB // P
    n_tiles = [QT * (j + 1) if j < NJ - 1 else NT for j in range(NJ)]
    PACK = QB // LAST
    units = [[[u] for u in range(n_tiles[j])] for j in range(NJ - 1)]
    units += [[list(range(u, min(u + PACK, NT - 1))) for u in range(0, NT - 1, PACK)] + [[NT - 1]]]
    first = [sum(len(x) for x in units[:j]) for j in range(NJ)]
    UNITS = sum(len(x) for x in units)
    q_tiles = [QT] * (NJ - 1) + [NT - QT * (NJ - 1)]
    MAXES = sum(q_tiles[j] * (j + 1) for j in range(NJ))
    first_max = [sum(q_tiles[i] * (i + 1) for i in range(j)) for j in range(NJ)]
    RS, RP, RM, RQ = 2, 8, 3, 2
    TG = 8
    NTG = -(-NT // TG)
    LEAD = 4

    def rows(t):
        return P if t < NT - 1 else LAST

    def width(j):
        return QB if j < NJ - 1 else LAST

    def skipped(j, u):
        return max(P * (u - QT * j), 0) if j > 0 else 0

    with ExitStack() as ctx:
        def sb(name, shape, dt):
            return ctx.enter_context(nc.sbuf_tensor(f"{tag}_{name}", shape, dt))

        def pb(name, shape, dt):
            return ctx.enter_context(nc.psum_tensor(f"{tag}_{name}", shape, dt))

        def sem(name):
            return ctx.enter_context(nc.semaphore(f"{tag}_{name}"))

        V = sb("v", [P, 2, NT, C], F32)
        VT = sb("vT", [C, NT * P], F32)
        Q = sb("q", [P, NT, C], F32)
        RES = sb("res", [P, NT, C], F32)
        VA = sb("va", [P, NT, 4, C], BF16)
        VB = sb("vb", [P, NT, 2, C], BF16)
        QA = sb("qa", [P, 2, NT, 4, C], BF16)
        QBp = sb("qb", [P, NT, 2, C], BF16)
        VAT = sb("vaT", [P, 2, S], BF16)
        VBT = sb("vbT", [2 * C, 2, S], BF16)
        QAT = sb("qaT", [P, 2, S], BF16)
        QBT = sb("qbT", [2 * C, 2, S], BF16)
        QS = sb("qs", [P, RQ, QB], BF16)
        E = sb("e", [P, RP, QB], F32)
        MX = sb("mx", [P, QT, NJ], F32)
        NM = sb("nm", [P, QT], F32)
        NR = sb("nr", [P, QT], F32)
        O = sb("o", [P, 2, QB], F32)
        RD = sb("rd", [P, QT], F32)
        OT = sb("ot", [P, QT, C], F32)
        A = sb("A", [C, C], F32)
        WF = sb("wf", [P, C + 1], F32)
        WQ, WK, WV = sb("wq", [C, C], F32), sb("wk", [C, C], F32), sb("wv", [C, C], F32)
        WQB, WKB = sb("wqb", [C, C], F32), sb("wkb", [C, C], F32)

        SC = [pb(f"sc{i}", [P, QB], F32) for i in range(RS)]
        MB = [pb(f"mb{i}", [P, QB], F32) for i in range(RM)]
        ACC = pb("acc", [P, QB], F32)
        MA = pb("ma", [P, 2 * QB], BF16)
        MD = pb("md", [P, QB], F32)
        MAf = MA[:].bitcast(F32)

        w_in, w_mm, w_out = sem("w_in"), sem("w_mm"), sem("w_out")
        with nc.Block() as block:
            @block.sync
            def _(sp):
                sp.dma_start(WQ[:], wq).then_inc(w_in, 16)
                sp.dma_start(WK[:], wk).then_inc(w_in, 16)
                sp.dma_start(WV[:], wv).then_inc(w_in, 16)

            @block.tensor
            def _(pe):
                pe.wait_ge(w_in, 48)
                b = k.basis[:, 0:C]
                nc.tensor.matmul(MD[0:C, 0:C], WQ[:], b, start=True, stop=True).then_inc(w_mm, 1)
                pe.wait_ge(w_out, 1)
                nc.tensor.matmul(MD[0:C, 0:C], WK[:], b, start=True, stop=True).then_inc(w_mm, 1)
                pe.wait_ge(w_out, 2)
                nc.tensor.matmul(MD[0:C, 0:C], WQB[:], WKB[:], start=True, stop=True).then_inc(w_mm, 1)
                pe.wait_ge(w_out, 3)
                nc.tensor.matmul(MD[:, 0:C], k.basis[:], WV[:], start=True, stop=True).then_inc(w_mm, 1)

            @block.vector
            def _(dve):
                dve.wait_ge(w_mm, 1)
                nc.vector.tensor_copy(WQB[:], MD[0:C, 0:C]).then_inc(w_out, 1)
                dve.wait_ge(w_mm, 2)
                nc.vector.tensor_copy(WKB[:], MD[0:C, 0:C]).then_inc(w_out, 1)
                dve.wait_ge(w_mm, 3)
                nc.vector.tensor_scalar(A[:], MD[0:C, 0:C], float(C) ** -0.5, None, ALU.mult).then_inc(w_out, 1)
                dve.wait_ge(w_mm, 4)
                nc.vector.tensor_copy(WF[:, 0:C], MD[:, 0:C]).then_inc(w_out, 1)
                for g in range(4):
                    nc.vector.tensor_copy(WF[g * C:(g + 1) * C, C:C + 1], k.ident[0:C, 0:1]).then_inc(w_out, 1)
                nc.vector.memset(V[:, :, :, 0:1], 1.0).then_inc(w_out, 1)
                nc.vector.memset(Q[:, NT - 1], 0.0).then_inc(w_out, 1)
                dve.wait_ge(w_out, 10)

        v_ready = sem("v_ready")
        v_parts = sem("v_parts")
        q_parts = sem("q_parts")
        pool_step = sem("pool_step")
        ma_full, ma_read = sem("ma_full"), sem("ma_read")
        md_full, md_read = sem("md_full"), sem("md_read")
        max_full, max_read = sem("max_full"), sem("max_read")
        shift_step, shift_ready = sem("shift_step"), sem("shift_ready")
        scores_full, exp_done = sem("scores_full"), sem("exp_done")
        pv_done = sem("pv_done")
        acc_read = sem("acc_read")
        out_step, out_done = sem("out_step"), sem("out_done")

        def prep_items():
            vt = [("vT", f) for f in range(-(-NT // 4))]
            q = [("q", f) for f in range(-(-NT // 16))]
            vs = [(s, f) for f in range(-(-NT // TG)) for s in ("va", "vb")]
            qs = [(s, f) for f in range(-(-NT // TG)) for s in ("qa", "qb")]
            return vt, q, vs, qs

        def max_items(j):
            return [("max", j, i, c) for i in range(q_tiles[j]) for c in range(j + 1)]

        vt, q, vs, qs = prep_items()
        prologue = vt + q + vs + qs + max_items(0) + [("shift", 0)]
        for j in range(1, LEAD):
            prologue += max_items(j)
        worth = [sum(width(j) - skipped(j, u) for u in unit) / QB for j in range(NJ) for unit in units[j]]
        begins = [sum(worth[:t]) for t in range(UNITS + 1)]
        spread = []

        def put(items, lo, hi):
            spread.extend((lo + (hi - lo) * n / len(items), x) for n, x in enumerate(items))

        TAIL = 5
        own = [x for j in range(LEAD, NJ) for x in max_items(j)]
        following = [x for j in range(LEAD) for x in max_items(j)]
        tail, following = following[-TAIL:], following[:-TAIL]
        turn_at = begins[UNITS] * len(own) / (MAXES - TAIL)
        put(own, 0, turn_at)
        put(following, turn_at, begins[UNITS])
        put(vt, 4, 16)
        put(q, 19, 22)
        put(vs, 17, 31)
        put(qs, 32, turn_at - 1)
        for j in range(NJ - 1):
            put([("shift", j + 1)], begins[first[j + 1] - 3], 0)
            put([("final", j)], begins[first[j + 1] + 2], 0)
        put([("shift", 0)], begins[first[NJ - 1] + 1], 0)
        spread.sort(key=lambda x: x[0])
        PLAN = [[[x for at, x in spread if begins[first[j] + u] <= at < begins[first[j] + u + 1]]
                 for u in range(len(units[j]))] for j in range(NJ)]
        flat = [x for step in PLAN for after in step for x in after] + tail + [("final", NJ - 1)]

        def indices(items):
            kinds = {"vT": "ma", "va": "ma", "vb": "ma", "qa": "ma", "qb": "ma", "shift": "ma",
                     "q": "md", "final": "md", "max": "max"}
            seen = {"ma": 0, "md": 0, "max": 0}
            at = {}
            for x in items:
                at[x] = seen[kinds[x[0]]]
                seen[kinds[x[0]]] += 1
            return at, seen

        AT0, PRO = indices(prologue)
        AT1, PER = indices(flat)

        def before(g, kind):
            return 1 if g is None else g * PER[kind] + (1 + PRO[kind])

        def units_before(g):
            return g * UNITS + 1

        def blocks_before(g):
            return g * NJ + 1

        PS = 9

        with nc.Block() as block:
            @block.gpsimd
            def _(pool):
                for s in (v_ready, v_parts, q_parts, pool_step):
                    pool.sem_inc(s, 1)

                def copy(out, in_):
                    return nc.gpsimd.tensor_scalar(out, in_, 1.0, 0.0, ALU.mult, ALU.add)

                def prepare(g, img, par):
                    n = [img * PS + 1]

                    def step(ins):
                        n[0] = n[0] + 1
                        ins.then_inc(pool_step, 1)
                        pool.wait_ge(pool_step, n[0])
                        pool.nop(nofuse=True)

                    pair = [P, NT, 2, C]
                    if g is not None:
                        pool.wait_ge(pv_done, units_before(g))
                    step(nc.gpsimd.tensor_tensor(
                        RES[:, :, 1:C], m.T[:, img, :, 1:C],
                        m.mean[:, img, :][:, :, None].to_broadcast([P, NT, C - 1]), ALU.subtract))
                    nc.gpsimd.tensor_tensor(
                        V[:, par, :, 1:C], RES[:, :, 1:C],
                        m.rstd[:, img, :][:, :, None].to_broadcast([P, NT, C - 1]), ALU.mult).then_inc(v_ready, 1)
                    pool.wait_ge(v_ready, img + 2)
                    if g is not None:
                        pool.wait_ge(ma_full, before(g, "ma") - 1)
                    pool.nop(nofuse=True)
                    step(copy(VA[:, :, 0:4:2, :], V[:, par][:, :, None, :].to_broadcast(pair)))
                    step(nc.gpsimd.tensor_tensor(RES[:], V[:, par], VA[:, :, 0, :], ALU.subtract))
                    step(copy(VA[:, :, 1:4:2, :], RES[:][:, :, None, :].to_broadcast(pair)))
                    step(nc.gpsimd.tensor_tensor(VB[:, :, 0, :], RES[:], VA[:, :, 1, :], ALU.subtract))
                    copy(VB[:, :, 1, :], VA[:, :, 0, :]).then_inc(v_parts, 1)
                    at = AT0 if g is None else AT1
                    pool.wait_ge(md_read, before(g, "md") + at[("q", len(q) - 1)] + 1)
                    pool.nop(nofuse=True)
                    step(copy(QA[:, par, :, 0:2, :], Q[:][:, :, None, :].to_broadcast(pair)))
                    step(nc.gpsimd.tensor_tensor(RES[:], Q[:], QA[:, par, :, 0, :], ALU.subtract))
                    step(copy(QA[:, par, :, 2:4, :], RES[:][:, :, None, :].to_broadcast(pair)))
                    step(nc.gpsimd.tensor_tensor(QBp[:, :, 1, :], RES[:], QA[:, par, :, 2, :], ALU.subtract))
                    copy(QBp[:, :, 0, :], QA[:, par, :, 0, :]).then_inc(q_parts, 1)

                prepare(None, 0, 0)
                with pool.Fori(0, NB // 2) as pair_of:
                    for par in range(2):
                        g = pair_of * 2 + par
                        prepare(g, g + 1, 1 - par)

            @block.tensor
            def _(pe):
                def item(g, img, par, x, at):
                    kind = x[0]
                    if kind == "max":
                        _, j, i, c = x
                        par_m = par if (g is None or j < LEAD) else 1 - par
                        n, qt = at[x], QT * j + i
                        r, hi = rows(qt), min(QB * (c + 1), P * (qt + 1), S)
                        bank = MB[n % RM]
                        pe.wait_ge(max_read, before(g, "max") + max(n - RM + 1, 0))
                        if i == 0 and c == 0:
                            if g is None:
                                pe.wait_ge(ma_read, before(None, "ma") + AT0[qs[-1]] + 1)
                            elif j == 0:
                                pe.wait_ge(ma_read, before(g, "ma") + AT1[qs[-1]] + 1)
                        q_t = QAT[:, par_m, qt * P:qt * P + r]
                        if c < j:
                            nc.tensor.matmul(bank[0:r, 0:QB], q_t, VAT[:, par_m, c * QB:hi],
                                             start=True, stop=True).then_inc(max_full, 1)
                        else:
                            w = hi - c * QB
                            nc.tensor.matmul(bank[0:r, 0:w], q_t, VAT[:, par_m, c * QB:hi], start=True, stop=False)
                            nc.tensor.matmul(bank[0:r, w - r:w], k.ident_bf[0:r, 0:r], k.mask_qk[0:r, 0:r],
                                             start=False, stop=True).then_inc(max_full, 1)
                        return
                    if kind in ("q", "final"):
                        pe.wait_ge(md_read, before(g, "md") + at[x])
                        if kind == "q":
                            pe.wait_ge(ma_read, before(g, "ma") + at[vt[-1]] + 1)
                            for t in range(16 * x[1], min(16 * x[1] + 16, NT)):
                                o = (t % 16) * C
                                last = nc.tensor.matmul(MD[0:rows(t), o:o + C], VT[:, t * P:t * P + rows(t)], A[:],
                                                        start=True, stop=True)
                        else:
                            j = x[1]
                            pe.wait_ge(acc_read, blocks_before(g) + j + 1)
                            for i in range(q_tiles[j]):
                                r = rows(QT * j + i)
                                o = i * (C + 1)
                                last = nc.tensor.matmul(MD[0:r, o:o + C + 1],
                                                        O[:, (1 - par + j) % 2, i * P:i * P + r], WF[:],
                                                        start=True, stop=True)
                        last.then_inc(md_full, 1)
                        return
                    pe.wait_ge(ma_read, before(g, "ma") + at[x])
                    if kind == "vT":
                        if x[1] == 0:
                            pe.wait_ge(v_ready, img + 2)
                        pe.nop(nofuse=True)
                        for t in range(4 * x[1], min(4 * x[1] + 4, NT)):
                            o = (t % 4) * P
                            last = nc.tensor.transpose(MAf[0:C, o:o + rows(t)], V[0:rows(t), par, t, :],
                                                       k.ident[0:rows(t), 0:rows(t)])
                    elif kind == "shift":
                        j = x[1]
                        par_s = par if j == 0 else 1 - par
                        pe.wait_ge(shift_ready, (blocks_before(img) if j == 0 else blocks_before(g)) + j + 1)
                        if j == NJ - 1:
                            pe.nop(nofuse=True)
                        for i in range(q_tiles[j]):
                            r = rows(QT * j + i)
                            last = nc.tensor.transpose(MA[:, i * P:i * P + r],
                                                       QA[0:r, par_s, QT * j + i].rearrange("p s c -> p (s c)"),
                                                       k.ident_bf[0:r, 0:r])
                    else:
                        src = {"va": VA[:], "vb": VB[:], "qa": QA[:, par], "qb": QBp[:]}[kind]
                        m_rows = P if kind in ("va", "qa") else 2 * C
                        if x[1] == 0:
                            pe.wait_ge(v_parts if kind in ("va", "vb") else q_parts, img + 2)
                        pe.nop(nofuse=True)
                        for t in range(TG * x[1], min(TG * x[1] + TG, NT)):
                            o = (t % TG) * P
                            last = nc.tensor.transpose(MA[0:m_rows, o:o + rows(t)],
                                                       src[0:rows(t), t].rearrange("p s c -> p (s c)"),
                                                       k.ident_bf[0:rows(t), 0:rows(t)])
                    last.then_inc(ma_full, 1)

                def weigh(g, par, j, n_unit):
                    i = first[j] + n_unit
                    w = width(j)
                    pe.wait_ge(exp_done, units_before(g) + i + 1)
                    if n_unit == 0:
                        pe.wait_ge(acc_read, blocks_before(g) + j)
                    for at, u in enumerate(units[j][n_unit]):
                        r, c0, off = rows(u), skipped(j, u), at * w
                        if r < P:
                            pe.nop(nofuse=True)
                        cg = C * (u % 4)
                        last = nc.tensor.matmul(ACC[cg:cg + C, c0:w], V[0:r, par, u, :],
                                                E[0:r, i % RP, off + c0:off + w],
                                                start=(u < 4), stop=(u >= n_tiles[j] - 4))
                    last.then_inc(pv_done, 1)

                def turn(g, par):
                    for j in range(NJ):
                        w = width(j)
                        slot = (par + j) % 2
                        done = 0
                        for n_unit, unit in enumerate(units[j]):
                            i = first[j] + n_unit
                            bank = SC[i % RS]
                            pe.wait_ge(exp_done, units_before(g) + max(i - RS + 1, 0))
                            if n_unit == 0:
                                if j == 0:
                                    n = before(g, "ma") - (PER["ma"] - AT1[("shift", 0)] - 1)
                                    pe.wait_ge(ma_read, n)
                                else:
                                    pe.wait_ge(ma_read, before(g, "ma") + AT1[("shift", j)] + 1)
                            for at, u in enumerate(unit):
                                r, d, c0, off = rows(u), u - QT * j, skipped(j, u), at * w
                                kt = slice(u * P, u * P + r)
                                nc.tensor.matmul(bank[0:r, off + c0:off + w], VAT[:, par, kt], QS[:, slot, c0:w],
                                                 start=True, stop=False)
                                last = nc.tensor.matmul(bank[0:r, off + c0:off + w], VBT[:, par, kt],
                                                        QBT[:, par, j * QB + c0:j * QB + w], start=False, stop=d < 0)
                                if d >= 0:
                                    lo = 0 if j == 0 else c0
                                    hi = min(P * (d + 1), w)
                                    m0 = 3 * P - (P * d - lo)
                                    last = nc.tensor.matmul(bank[0:r, lo:hi], k.ident_bf[0:r, 0:r],
                                                            k.mask_kq[0:r, m0:m0 + hi - lo], start=False, stop=True)
                            last.then_inc(scores_full, 1)
                            for x in PLAN[j][n_unit]:
                                item(g, g + 1, 1 - par, x, AT1)
                            if (j < NJ - 1 and n_unit % 4 == 1 and n_unit >= 5) or (j == NJ - 1 and n_unit >= 1):
                                ready = done + 4 if j < NJ - 1 else n_unit
                                for v in range(done, ready):
                                    weigh(g, par, j, v)
                                done = ready
                        for v in range(done, len(units[j])):
                            weigh(g, par, j, v)
                    for x in tail + [("final", NJ - 1)]:
                        item(g, g + 1, 1 - par, x, AT1)

                for x in prologue:
                    item(None, 0, 0, x, AT0)
                with pe.Fori(0, NB // 2) as pair_of:
                    for par in range(2):
                        turn(pair_of * 2 + par, par)

            @block.scalar
            def _(act):
                for s in (ma_read, exp_done):
                    act.sem_inc(s, 1)

                def item(g, img, par, x, at):
                    kind = x[0]
                    if kind not in ("vT", "shift", "va", "vb", "qa", "qb"):
                        return
                    act.wait_ge(ma_full, before(g, "ma") + at[x])
                    if kind == "shift":
                        j = x[1]
                        slot = ((par if j == 0 else 1 - par) + j) % 2
                        w = width(j)
                        ins = nc.scalar.copy(QS[:, slot, 0:w], MA[:, 0:w])
                    elif kind == "vT":
                        lo, hi = 4 * P * x[1], min(4 * P * (x[1] + 1), S)
                        ins = nc.scalar.copy(VT[:, lo:hi], MAf[0:C, 0:hi - lo])
                    else:
                        dst = {"va": VAT, "vb": VBT, "qa": QAT, "qb": QBT}[kind]
                        lo, hi = TG * P * x[1], min(TG * P * (x[1] + 1), S)
                        n = dst.shape[0]
                        ins = nc.scalar.copy(dst[:, par, lo:hi], MA[0:n, 0:hi - lo])
                    ins.then_inc(ma_read, 1)

                nc.scalar.preload_act_table(ACT.Exp)
                for x in prologue:
                    item(None, 0, 0, x, AT0)
                with act.Fori(0, NB // 2) as pair_of:
                    for par in range(2):
                        g = pair_of * 2 + par
                        for j in range(NJ):
                            w = width(j)
                            for n_unit, unit in enumerate(units[j]):
                                i = first[j] + n_unit
                                r, c0, hi = rows(unit[0]), skipped(j, unit[0]), w * len(unit)
                                act.wait_ge(scores_full, units_before(g) - 1 + i + 1)
                                act.wait_ge(pv_done, units_before(g) + (i - RP + 1 if i >= RP else 0))
                                nc.scalar.activation(E[0:r, i % RP, c0:hi], SC[i % RS][0:r, c0:hi],
                                                     ACT.Exp).then_inc(exp_done, 1)
                                for x in PLAN[j][n_unit]:
                                    item(g, g + 1, 1 - par, x, AT1)
                        for x in tail + [("final", NJ - 1)]:
                            item(g, g + 1, 1 - par, x, AT1)

            @block.vector
            def _(dve):
                for s in (md_read, max_read, shift_ready, acc_read, pv_done, shift_step, out_step, out_done):
                    dve.sem_inc(s, 1)

                def shift(g, blk, par_m, j, n):
                    nq, r = q_tiles[j], rows(QT * j)
                    hi = QA[0:r, par_m, QT * j:QT * j + nq, 0, 0:1]
                    lo = QA[0:r, par_m, QT * j:QT * j + nq, 2, 0:1]
                    nm, nr = NM[0:r, 0:nq, None], NR[0:r, 0:nq, None]
                    dve.wait_ge(max_read, before(g, "max") + n + 1)
                    nc.vector.tensor_reduce(NM[0:r, 0:nq], MX[0:r, 0:nq, 0:j + 1], AX.X, ALU.max,
                                            negate=True).then_inc(shift_step, 1)
                    dve.wait_ge(shift_step, blk * 3 + 2)
                    nc.vector.tensor_copy(hi, nm).then_inc(shift_step, 1)
                    dve.wait_ge(shift_step, blk * 3 + 3)
                    dve.wait_ge(shift_ready, blk + 1)
                    nc.vector.tensor_tensor(nr, nm, hi, ALU.subtract).then_inc(shift_step, 1)
                    dve.wait_ge(shift_step, blk * 3 + 4)
                    nc.vector.tensor_copy(lo, nr).then_inc(shift_ready, 1)

                def item(g, img, par, x, at):
                    kind = x[0]
                    if kind == "max":
                        _, j, i, c = x
                        n, qt = at[x], QT * j + i
                        r, w = rows(qt), min(QB * (c + 1), P * (qt + 1), S) - c * QB
                        later = g is None or j < LEAD
                        blk = (img if later else g) * NJ + j
                        if i == 0 and c == 0:
                            dve.wait_ge(shift_step, blk * 3 + 1)
                        dve.wait_ge(max_full, before(g, "max") + n)
                        nc.vector.tensor_reduce(MX[0:r, i, c:c + 1], MB[n % RM][0:r, 0:w], AX.X,
                                                ALU.max).then_inc(max_read, 1)
                        if i == q_tiles[j] - 1 and c == j:
                            shift(g, blk, par if later else 1 - par, j, n)
                    elif kind == "q":
                        lo, hi = 16 * x[1], min(16 * (x[1] + 1), NT)
                        full = min(hi, NT - 1)
                        dve.wait_ge(md_full, before(g, "md") + at[x])
                        dve.wait_ge(q_parts, img + 1)
                        if hi > full:
                            nc.vector.tensor_copy(Q[0:LAST, full], MD[0:LAST, (full - lo) * C:(hi - lo) * C])
                        nc.vector.tensor_copy(Q[:, lo:full].rearrange("p t c -> p (t c)"),
                                              MD[:, 0:(full - lo) * C]).then_inc(md_read, 1)
                    elif kind == "final":
                        j = x[1]
                        nq, r = q_tiles[j], rows(QT * j)
                        blk = g * NJ + j
                        md = MD[0:r, 0:nq * (C + 1)].rearrange("p (q c) -> p q c", c=C + 1)
                        dve.wait_ge(md_full, before(g, "md") + at[x])
                        dve.wait_ge(md_read, before(g, "md") + at[x])
                        nc.vector.reciprocal(RD[0:r, 0:nq, None], md[:, :, C:C + 1]).then_inc(out_step, 1)
                        dve.wait_ge(out_step, blk + 2)
                        dve.wait_ge(out_done, blk + 1)
                        nc.vector.tensor_tensor(OT[0:r, 0:nq], md[:, :, 0:C],
                                                RD[0:r, 0:nq, None].to_broadcast([r, nq, C]),
                                                ALU.mult).then_inc(md_read, 1)
                        dve.wait_ge(md_read, before(g, "md") + at[x] + 1)
                        t = m.T[0:r, g, QT * j:QT * j + nq, :]
                        nc.vector.tensor_tensor(t, t, OT[0:r, 0:nq], ALU.add).then_inc(out_done, 1)

                for x in prologue:
                    item(None, 0, 0, x, AT0)
                with dve.Fori(0, NB // 2) as pair_of:
                    for par in range(2):
                        g = pair_of * 2 + par
                        for j in range(NJ):
                            for after in PLAN[j]:
                                for x in after:
                                    item(g, g + 1, 1 - par, x, AT1)
                            w = width(j)
                            dve.wait_ge(pv_done, units_before(g) + first[j] + len(units[j]))
                            nc.vector.tensor_copy(O[:, (par + j) % 2, 0:w], ACC[:, 0:w]).then_inc(acc_read, 1)
                        for x in tail + [("final", NJ - 1)]:
                            item(g, g + 1, 1 - par, x, AT1)
                dve.wait_ge(out_done, NB * NJ + 1)


HID = 128
MAGIC = 0x5F3759DF


def rsqrt_steps(nc, y, v, t, step):
    step(nc.vector.tensor_single_scalar(y.bitcast(I32), v.bitcast(I32), 1, ALU.logical_shift_right))
    step(nc.vector.tensor_scalar(y.bitcast(I32), y.bitcast(I32), -1.0, float(MAGIC), ALU.mult, ALU.add))
    for _ in range(3):
        step(nc.vector.tensor_tensor(t, y, y, ALU.mult))
        step(nc.vector.tensor_tensor(t, t, v, ALU.mult))
        step(nc.vector.tensor_scalar(t, t, -0.5, 1.5, ALU.mult, ALU.add))
        step(nc.vector.tensor_tensor(y, y, t, ALU.mult))


RSQRT_STEPS = 14


def token_mlps(nc, m, k, w, eps, tag):
    QD = 4
    NQ = m.NB // QD
    PAIR = 2 if NQ % 2 == 0 else 1
    QB, TB = 512, 4
    NF = -(-NT // TB)
    W = NT * QD

    def rows(t):
        return P if t < NT - 1 else LAST

    def span(f):
        return QB * f, min(QB * (f + 1), S)

    with ExitStack() as ctx:
        def sb(name, shape, dt=F32):
            return ctx.enter_context(nc.sbuf_tensor(f"{tag}_{name}", shape, dt))

        def pb(name, shape, dt=F32):
            return ctx.enter_context(nc.psum_tensor(f"{tag}_{name}", shape, dt))

        def sem(name):
            return ctx.enter_context(nc.semaphore(f"{tag}_{name}"))

        X = [sb(f"x{s}", [P, NT, QD, C]) for s in range(PAIR)]
        SQ = [sb(f"sq{s}", [P, NT, QD, C]) for s in range(PAIR)]
        XT = [sb(f"xT{s}", [P, S]) for s in range(PAIR)]
        MEAN, VAR, RT, TM = [sb(n, [P, W]) for n in ("mean", "var", "rt", "tm")]
        RH, RT_RING, RU = 3, 2, 2
        HR = 2 * QD
        HS = [sb(f"hs{i}", [P, QB]) for i in range(HR)]
        Z = [sb(f"z{i}", [P, QB]) for i in range(2)]
        W1 = [sb(f"w1{n}", [P, HID]) for n in "ab"]
        W1Z = [[sb(f"w1{n}{b}", [P, HID]) for b in range(QD)] for n in "ab"]
        W2 = [sb(f"w2{n}", [HID, C]) for n in "ab"]
        B1 = [sb(f"b1{n}", [HID, 1]) for n in "ab"]
        GC = [sb(f"gc{n}", [P, 1]) for n in "ab"]
        BC = [sb(f"bc{n}", [C, 1]) for n in "ab"]
        DG = [sb(f"dg{n}", [P, P]) for n in "ab"]
        BB = [sb(f"bb{n}", [P, 1]) for n in "ab"]
        B2 = [sb(f"b2{n}", [P, 1]) for n in "ab"]
        ROW = {n: sb(f"row_{n}", [P, C]) for n in ("bo_time", "g2", "be2", "bo_recv", "g4", "be4")}
        TR = [pb(f"tr{i}", [P, QB]) for i in range(RT_RING)]
        H = [pb(f"h{i}", [P, QB]) for i in range(RH)]
        U = [pb(f"u{i}", [P, QB]) for i in range(RU)]
        OB = pb("ob", [P, QB])

        LOADS = 2 * (4 * QD + 3) + len(ROW)
        w_in, w_mm, w_step = sem("w_in"), sem("w_mm"), sem("w_step")
        with nc.Block() as block:
            @block.sync
            def _(sp):
                n = 0
                for i, x in enumerate("ab"):
                    g, be = ("g1", "be1") if x == "a" else ("g3", "be3")
                    for b in range(QD):
                        r = slice(b * C, (b + 1) * C)
                        sp.dma_start(W1[i][r, :], w["W1" + x]).then_inc(w_in, 16)
                        for t, v in ((GC, w[g]), (BB, w[be]), (B2, w["b2" + x])):
                            sp.dma_start(t[i][r, :], v[:, None]).then_inc(w_in, 16)
                    sp.dma_start(W2[i][:], w["W2" + x]).then_inc(w_in, 16)
                    sp.dma_start(B1[i][:], w["b1" + x][:, None]).then_inc(w_in, 16)
                    sp.dma_start(BC[i][:], w[be][:, None]).then_inc(w_in, 16)
                    n += 4 * QD + 3
                for name, t in ROW.items():
                    sp.dma_start(t[:], w[name][None, :].to_broadcast([P, C])).then_inc(w_in, 16)
                    n += 1
                assert n == LOADS

            @block.tensor
            def _(pe):
                pe.wait_ge(w_in, 16 * LOADS)
                for i in range(2):
                    nc.tensor.matmul(U[i][:, 0:1], W1[i][0:C, :], BC[i][:], start=True, stop=True).then_inc(w_mm, 1)

            @block.vector
            def _(dve):
                n = [0]

                def step(ins):
                    n[0] += 1
                    ins.then_inc(w_step, 1)
                    dve.wait_ge(w_step, n[0])

                dve.wait_ge(w_in, 16 * LOADS)
                dve.wait_ge(w_mm, 2)
                for i in range(2):
                    step(nc.vector.tensor_tensor(B1[i][:], B1[i][:], U[i][:, 0:1], ALU.add))
                    step(nc.vector.tensor_scalar(W1[i][:], W1[i][:], GC[i][:], None, ALU.mult))
                    for b in range(QD):
                        r = slice(b * C, (b + 1) * C)
                        step(nc.vector.memset(W1Z[i][b][:], 0.0))
                        step(nc.vector.tensor_copy(W1Z[i][b][r, :], W1[i][r, :]))
                    step(nc.vector.tensor_scalar(DG[i][:], k.ident[:], GC[i][:], None, ALU.mult))
                    step(nc.vector.tensor_tensor(BB[i][:], BB[i][:], B2[i][:], ALU.add))
                step(nc.vector.tensor_tensor(ROW["be2"][:], ROW["be2"][:], ROW["bo_recv"][:], ALU.add))

        added = sem("added")
        centred, squared = sem("centred"), sem("squared")
        vec = sem("vec")
        normed = sem("normed")
        affine = sem("affine")
        pool_step = sem("pool_step")
        tr_full, tr_read = sem("tr_full"), sem("tr_read")
        h_full, gelu_done = sem("h_full"), sem("gelu_done")
        u_full, z_done = sem("u_full"), sem("z_done")
        ob_full, u_read = sem("ob_full"), sem("u_read")
        LNS = [(s, 1) for s in range(PAIR)]
        for s in range(PAIR):
            LNS += [(s, 2), (s, 3)]
        LNS += [(s, 4) for s in range(PAIR)]
        NL = len(LNS)
        MLPS = [(s, i) for i in range(2) for s in range(PAIR)]
        NM_ = len(MLPS)
        N = NF * QD
        VS = NL * (4 + RSQRT_STEPS)

        with nc.Fori(0, NQ // PAIR) as o:
            with nc.Block() as block:
                @block.gpsimd
                def _(pool):
                    steps = [0]

                    def step(ins):
                        steps[0] += 1
                        ins.then_inc(pool_step, 1)
                        pool.wait_ge(pool_step, o * (PAIR * 2) + steps[0])

                    for s in range(PAIR):
                        img = bass.ds((o * PAIR + s) * QD, QD)
                        nc.gpsimd.tensor_tensor(X[s][:], m.T[:, img].rearrange("p b t c -> p t b c"),
                                                ROW["bo_time"][:, None, None, :].to_broadcast([P, NT, QD, C]),
                                                ALU.add).then_inc(added, 1)
                    aff = 0
                    for n, (s, which) in enumerate(LNS):
                        pool.wait_ge(centred, o * NL + n + 1)
                        nc.gpsimd.tensor_tensor(SQ[s][:], X[s][:], X[s][:], ALU.mult).then_inc(squared, 1)
                        if which in (2, 4):
                            pool.wait_ge(normed, o * NL + n + 1)
                            row = [ROW[f"{x}{which}"][:, None, None, :].to_broadcast([P, NT, QD, C])
                                   for x in ("g", "be")]
                            img = bass.ds((o * PAIR + s) * QD, QD)
                            out = X[s][:] if which == 2 else m.T[:, img].rearrange("p b t c -> p t b c")
                            step(nc.gpsimd.tensor_tensor(X[s][:], X[s][:], row[0], ALU.mult))
                            if which == 4:
                                pool.nop(nofuse=True)
                                nc.gpsimd.tensor_tensor(m.T[:, img, 0:NT - 1].rearrange("p b t c -> p t b c"),
                                                        X[s][:, 0:NT - 1],
                                                        ROW["be4"][:, None, None, :].to_broadcast([P, NT - 1, QD, C]),
                                                        ALU.add)
                                nc.gpsimd.tensor_tensor(m.T[0:LAST, img, NT - 1],
                                                        X[s][0:LAST, NT - 1],
                                                        ROW["be4"][0:LAST, None, :].to_broadcast([LAST, QD, C]),
                                                        ALU.add).then_inc(affine, 1)
                            else:
                                nc.gpsimd.tensor_tensor(X[s][:], X[s][:], row[1], ALU.add).then_inc(affine, 1)
                            aff += 1
                    pool.wait_ge(affine, o * (2 * PAIR) + aff)
                    pool.nop(nofuse=True)

                @block.vector
                def _(dve):
                    steps = [0]

                    def step(ins):
                        steps[0] += 1
                        ins.then_inc(vec, 1)
                        dve.wait_ge(vec, o * VS + steps[0])

                    for n, (s, which) in enumerate(LNS):
                        x = X[s][:].rearrange("p t b c -> p (t b) c")
                        sq = SQ[s][:].rearrange("p t b c -> p (t b) c")
                        wide = [P, W, C]
                        if which == 1:
                            dve.wait_ge(added, o * PAIR + s + 1)
                        elif which == 3:
                            dve.wait_ge(affine, o * 2 * PAIR + s + 1)
                        else:
                            mlp = MLPS.index((s, which // 2 - 1))
                            dve.wait_ge(u_read, (o * NM_ + mlp + 1) * NF)
                        step(nc.vector.tensor_reduce(MEAN[:], x, AX.X, ALU.add))
                        step(nc.vector.tensor_scalar(MEAN[:], MEAN[:], 1.0 / C, None, ALU.mult))
                        nc.vector.tensor_tensor(x, x, MEAN[:][:, :, None].to_broadcast(wide),
                                                ALU.subtract).then_inc(centred, 1)
                        dve.wait_ge(squared, o * NL + n + 1)
                        step(nc.vector.tensor_reduce(VAR[:], sq, AX.X, ALU.add))
                        step(nc.vector.tensor_scalar(VAR[:], VAR[:], 1.0 / C, eps, ALU.mult, ALU.add))
                        rsqrt_steps(nc, RT[:], VAR[:], TM[:], step)
                        nc.vector.tensor_tensor(x, x, RT[:][:, :, None].to_broadcast(wide),
                                                ALU.mult).then_inc(normed, 1)
                        dve.wait_ge(normed, o * NL + n + 1)
                        dve.nop(nofuse=True)

                @block.tensor
                def _(pe):
                    for q, (s, i) in enumerate(MLPS):
                        t0 = q * NF
                        n0 = q * N
                        pe.wait_ge(normed, o * NL + LNS.index((s, 1 if i == 0 else 3)) + 1)

                        def flip(f):
                            if t0 + f >= RT_RING:
                                pe.wait_ge(tr_read, o * (NM_ * NF) + t0 + f - RT_RING + 1)
                                pe.nop(nofuse=True)
                            for t in range(TB * f, min(TB * f + TB, NT)):
                                r = rows(t)
                                last = nc.tensor.transpose(TR[(t0 + f) % RT_RING][:, (t % TB) * P:(t % TB) * P + r],
                                                           X[s][0:r, t].rearrange("p b c -> p (b c)"),
                                                           k.ident[0:r, 0:r])
                            last.then_inc(tr_full, 1)

                        def second(f):
                            lo, hi = span(f)
                            bank = U[(t0 + f) % RU]
                            if t0 + f >= RU:
                                pe.wait_ge(z_done, o * (NM_ * NF) + t0 + f - RU + 1)
                            nc.tensor.matmul(bank[:, 0:hi - lo], DG[i][:], XT[s][:, lo:hi], start=True, stop=False)
                            pe.wait_ge(gelu_done, o * (NM_ * N) + n0 + QD * f + QD)
                            for b in range(QD):
                                last = nc.tensor.matmul(bank[b * C:(b + 1) * C, 0:hi - lo], W2[i][:],
                                                        HS[(n0 + QD * f + b) % HR][:, 0:hi - lo],
                                                        start=False, stop=True)
                            last.then_inc(u_full, 1)

                        def flip_back(f):
                            pe.wait_ge(z_done, o * (NM_ * NF) + t0 + f + 1)
                            if t0 + f >= 1:
                                pe.wait_ge(u_read, o * (NM_ * NF) + t0 + f)
                            pe.nop(nofuse=True)
                            for t in range(TB * f, min(TB * f + TB, NT)):
                                c0, r = (t % TB) * P, rows(t)
                                last = nc.tensor.transpose(OB[0:r, c0:c0 + P], Z[(t0 + f) % 2][:, c0:c0 + r],
                                                           k.ident[:])
                            last.then_inc(ob_full, 1)

                        flip(0)
                        for n in range(N):
                            f, b = n // QD, n % QD
                            lo, hi = span(f)
                            if b == 0:
                                if f + 1 < NF:
                                    flip(f + 1)
                                pe.wait_ge(tr_read, o * (NM_ * NF) + t0 + f + 1)
                            if n0 + n >= RH:
                                pe.wait_ge(gelu_done, o * (NM_ * N) + n0 + n - RH + 1)
                            nc.tensor.matmul(H[(n0 + n) % RH][:, 0:hi - lo], W1Z[i][b][:],
                                             XT[s][:, lo:hi], start=True, stop=True).then_inc(h_full, 1)
                            if f and b == 1:
                                second(f - 1)
                            if f and b == QD - 1:
                                flip_back(f - 1)
                        second(NF - 1)
                        flip_back(NF - 1)

                @block.scalar
                def _(act):
                    nc.scalar.preload_act_table(ACT.Gelu)
                    for q, (s, i) in enumerate(MLPS):
                        t0, n0 = q * NF, q * N

                        def take_flip(f):
                            lo, hi = span(f)
                            act.wait_ge(tr_full, o * (NM_ * NF) + t0 + f + 1)
                            nc.scalar.copy(XT[s][:, lo:hi], TR[(t0 + f) % RT_RING][:, 0:hi - lo]).then_inc(tr_read, 1)

                        def take_z(f):
                            lo, hi = span(f)
                            act.wait_ge(u_full, o * (NM_ * NF) + t0 + f + 1)
                            nc.scalar.activation(Z[(t0 + f) % 2][:, 0:hi - lo], U[(t0 + f) % RU][:, 0:hi - lo],
                                                 ACT.Identity, bias=BB[i][:]).then_inc(z_done, 1)

                        def take_out(f):
                            act.wait_ge(ob_full, o * (NM_ * NF) + t0 + f + 1)
                            if f < NF - 1:
                                ins = nc.scalar.copy(X[s][:, TB * f:TB * f + TB].rearrange("p t b c -> p (t b c)"), OB[:])
                            else:
                                ins = nc.scalar.copy(X[s][0:LAST, NT - 1].rearrange("p b c -> p (b c)"), OB[0:LAST, 0:P])
                            ins.then_inc(u_read, 1)

                        take_flip(0)
                        for n in range(N):
                            f, b = n // QD, n % QD
                            lo, hi = span(f)
                            if b == 0 and f + 1 < NF:
                                take_flip(f + 1)
                            act.wait_ge(h_full, o * (NM_ * N) + n0 + n + 1)
                            if b == 0 and t0 + f >= 2:
                                act.wait_ge(u_full, o * (NM_ * NF) + t0 + f - 1)
                            nc.scalar.activation(HS[(n0 + n) % HR][:, 0:hi - lo], H[(n0 + n) % RH][:, 0:hi - lo],
                                                 ACT.Gelu, bias=B1[i][:]).then_inc(gelu_done, 1)
                            if f and b == 2:
                                take_z(f - 1)
                            if f and b == QD - 1:
                                take_out(f - 1)
                        take_z(NF - 1)
                        take_out(NF - 1)


IMG = 56
WS = 7
DISP = WS // 2
NW = IMG // WS
K = WS * WS
SLOT = 64
HEADS = 4


def window_attention(nc, m, k, wqkvT, pos, w_out, b_out, eps, tag, load):
    NB = m.NB
    HK = HEADS * K
    ROWC = NW * HK
    XR0, ONE, BIAS = 0, 32, 64
    KR = BIAS + K
    NF = -(-NT // 4)
    NBK = -(-NT // 16)
    SQ_, SK_ = 4, 3
    HALF = HK * 2

    def rows(t):
        return P if t < NT - 1 else LAST

    with ExitStack() as ctx:
        def sb(name, shape, dt=F32):
            return ctx.enter_context(nc.sbuf_tensor(f"{tag}_{name}", shape, dt))

        def pb(name, shape, dt=F32):
            return ctx.enter_context(nc.psum_tensor(f"{tag}_{name}", shape, dt))

        def sem(name):
            return ctx.enter_context(nc.semaphore(f"{tag}_{name}"))

        XW = sb("xw", [KR, 2, NW * NW, SLOT])
        MQ = sb("mq", [KR, SQ_, 2, NW // 2, HEADS, K])
        MK = sb("mk", [KR, SK_, 2, NW // 2, HEADS, K])
        XC = sb("xc", [P, NT, C])
        XR = sb("xr", [C, S])
        OT = sb("ot", [P, S])
        PT = sb("pt", [P, 2, 2 * HALF])
        EXQ = sb("exq", [P, 2 * HALF])
        LS = sb("ls", [P, NW // 2 * HEADS])
        LN = sb("ln", [P, NW // 2 * HEADS])
        YB = sb("yb", [P, 2, NW // 2, HEADS, 2, C])
        NMX = sb("nmx", [P, 2, NW // 2 * HEADS])
        NMT = sb("nmt", [NW // 2 * HEADS, 2, P])
        BN = sb("bn", [C, NF, 6])
        MV = sb("mv", [C, 2])
        VE, RS, TM, SH = [sb(x, [C, 1]) for x in ("ve", "rs", "tm", "sh")]
        BO = sb("bo", [C, 1])
        ACAT, ATCAT, BCAT = [sb(x, [KR, HEADS * C]) for x in ("acat", "atcat", "bcat")]
        WQT, WKT, WVT, WO = [sb(x, [C, HEADS, C]) for x in ("wqT", "wkT", "wvT", "wo")]
        U4 = sb("u4", [33, 4, K], BF16)
        MSK = sb("msk", [P, 4, K])
        MSKT = sb("mskT", [P, 4, K])
        PQ, PK = pb("pq", [P, 512]), pb("pk", [P, 512])
        MXB = [pb(f"mx{i}", [P, 512]) for i in range(2)]
        SL = [pb(f"sl{i}", [P, 512]) for i in range(2)]
        YP = pb("yp", [P, 512])
        DP = pb("dp", [P, 512])

        w_in, w_mm, w_st, w_pl = sem("w_in"), sem("w_mm"), sem("w_st"), sem("w_pl")
        with nc.Block() as block:
            @block.sync
            def _(sp):
                for i, t in enumerate((WQT, WKT, WVT)):
                    sp.dma_start(t[:], wqkvT[i * P:(i + 1) * P, :].rearrange("(h d) c -> d h c", d=C)).then_inc(w_in, 16)
                sp.dma_start(WO[:], w_out.rearrange("(h d) c -> d h c", d=C)).then_inc(w_in, 16)
                sp.dma_start(BO[:], b_out[:, None]).then_inc(w_in, 16)
                for q in range(K):
                    a, b = WS - 1 - q // WS, WS - 1 - q % WS
                    sp.dma_start(MSK[BIAS + q:BIAS + q + 1, 0, :].rearrange("p (a b) -> p a b", a=WS),
                                 pos[None, a:a + WS, b:b + WS]).then_inc(w_in, 16)
                load(sp)

            @block.gpsimd
            def _(pool):
                n = [0]

                def step(ins):
                    n[0] += 1
                    ins.then_inc(w_pl, 1)
                    pool.wait_ge(w_pl, n[0])

                step(nc.gpsimd.memset(XW[:], 0.0))
                step(nc.gpsimd.memset(MQ[:], 0.0))
                step(nc.gpsimd.memset(MK[:], 0.0))
                step(nc.gpsimd.memset(YB[:], 0.0))
                step(nc.gpsimd.memset(U4[:], 0.0))
                for i, v in enumerate((lambda t: t[:, :, 4:7], lambda t: t[:, 4:7, :])):
                    st = U4[:, 2 * i, :].rearrange("p (a b) -> p a b", a=WS)
                    mv = U4[:, 2 * i + 1, :].rearrange("p (a b) -> p a b", a=WS)
                    step(nc.gpsimd.memset(v(st[0:1]), 1.0))
                    step(nc.gpsimd.memset(st[32:33], 1.0))
                    step(nc.gpsimd.memset(v(st[32:33]), 0.0))
                    step(nc.gpsimd.memset(mv[0:1], NEG))
                    step(nc.gpsimd.memset(v(mv[0:1]), 0.0))
                    step(nc.gpsimd.memset(v(mv[32:33]), NEG))
                for s in range(2):
                    step(nc.gpsimd.memset(XW[ONE:ONE + 1, s, :, 0:K], 1.0))
                    idn = XW[BIAS:BIAS + K, s, :, 0:K]
                    step(nc.gpsimd.affine_select(out=idn, in_=idn, compare_op=ALU.not_equal, fill=1.0, base=0,
                                                 pattern=[[0, NW * NW], [-1, K]], channel_multiplier=1))

            @block.tensor
            def _(pe):
                pe.wait_ge(w_in, 16 * (5 + K))
                for h in range(HEADS):
                    o = slice(h * C, (h + 1) * C)
                    nc.tensor.matmul(PQ[0:C, o], WQT[:, h], WKT[:, h], start=True, stop=True)
                    nc.tensor.matmul(PK[0:C, o], WKT[:, h], WQT[:, h], start=True, stop=True)
                    nc.tensor.matmul(YP[0:C, o], WVT[:, h], WO[:, h], start=True, stop=True).then_inc(w_mm, 1)
                pe.wait_ge(w_pl, 17)
                for i in range(2):
                    nc.tensor.matmul(MXB[i][0:K, 0:K], U4[:, 2 * i, :], U4[:, 2 * i + 1, :],
                                     start=True, stop=True).then_inc(w_mm, 1)
                pe.wait_ge(w_st, 10)
                for i in range(4):
                    nc.tensor.transpose(SL[0][0:K, i * K:(i + 1) * K], MSK[BIAS:BIAS + K, i, :],
                                        k.ident[BIAS:BIAS + K, BIAS:BIAS + K]).then_inc(w_mm, 1)

            @block.vector
            def _(dve):
                n = [0]

                def step(ins):
                    n[0] += 1
                    ins.then_inc(w_st, 1)
                    dve.wait_ge(w_st, n[0])

                scale = float(C) ** -0.5
                dve.wait_ge(w_mm, HEADS)
                for t in (ACAT, ATCAT, BCAT):
                    step(nc.vector.memset(t[:], 0.0))
                step(nc.vector.tensor_scalar(ACAT[0:C], PQ[0:C, 0:P], scale, None, ALU.mult))
                step(nc.vector.tensor_scalar(ATCAT[0:C], PK[0:C, 0:P], scale, None, ALU.mult))
                step(nc.vector.tensor_copy(BCAT[0:C], YP[0:C, 0:P]))
                dve.wait_ge(w_in, 16 * (5 + K))
                dve.wait_ge(w_mm, HEADS + 2)
                r = slice(BIAS, BIAS + K)
                step(nc.vector.tensor_tensor(MSK[r, 1], MSK[r, 0], MXB[0][0:K, 0:K], ALU.add))
                step(nc.vector.tensor_tensor(MSK[r, 2], MSK[r, 0], MXB[1][0:K, 0:K], ALU.add))
                step(nc.vector.tensor_tensor(MSK[r, 3], MSK[r, 1], MXB[1][0:K, 0:K], ALU.add))
                step(nc.vector.tensor_copy(TM[:], BO[:]))
                dve.wait_ge(w_mm, HEADS + 6)
                step(nc.vector.tensor_copy(MSKT[r].rearrange("p m c -> p (m c)"), SL[0][0:K, 0:4 * K]))
                for buf, src, n_slots in ((MQ, MSKT, SQ_), (MK, MSK, SK_)):
                    for s in range(n_slots):
                        low = 2 if s == n_slots - 1 else 0
                        for half in range(2):
                            step(nc.vector.tensor_copy(buf[r, s, half].rearrange("p w h c -> p (w h) c"),
                                                       src[r, low, None, :].to_broadcast([K, NW // 2 * HEADS, K])))
                        step(nc.vector.tensor_copy(buf[r, s, 1, NW // 2 - 1],
                                                   src[r, low + 1, None, :].to_broadcast([K, HEADS, K])))
                step(nc.vector.memset(XR[:], 0.0))
                step(nc.vector.memset(OT[:], 0.0))

        yp_full, yp_read = sem("yp_full"), sem("yp_read")
        dp_full, dp_read = sem("dp_full"), sem("dp_read")
        prj_full = sem("prj_full")
        mq_ready = sem("mq_ready")
        mk_half, mk_ready = sem("mk_half"), sem("mk_ready")
        mx_full, nmx_done, max_done = sem("mx_full"), sem("nmx_done"), sem("max_done")
        exq_done, sum_done, ln_done, shift_done = sem("exq_done"), sem("sum_done"), sem("ln_done"), sem("shift_done")
        shift_in = sem("shift_in")
        s_full, exp_done, pv_done = sem("s_full"), sem("exp_done"), sem("pv_done")
        xc_ready = sem("xc_ready")
        bn_done, stat_step, stat_done, xw_ready = sem("bn_done"), sem("stat_step"), sem("stat_done"), sem("xw_ready")

        YP_ITEMS = [[("y", i)] + ([("xT", f) for f in range(2 * i, min(2 * i + 2, NF))]) for i in range(NW)]
        yp_at = {x: n for n, x in enumerate(x for r in YP_ITEMS for x in r)}
        YPN = len(yp_at)
        DP_ITEMS = [[("nmT", i)] + ([("pv", i - 1)] if i else []) for i in range(NW)]
        DP_ITEMS[-1] += [("pv", NW - 1)] + [("back", f) for f in range(NBK)]
        dp_at = {x: n for n, x in enumerate(x for r in DP_ITEMS for x in r)}
        DPN = len(dp_at)
        STATS = 3 + RSQRT_STEPS
        PRE_YP, PRE_DP = NF, 1

        def ahead(par, i, by):
            return (i + by) % NW, par if i + by < NW else 1 - par

        def yp_base(g):
            return g * YPN + PRE_YP

        def dp_base(g):
            return g * DPN + PRE_DP

        def q_slot(par, i):
            return SQ_ - 1 if i == NW - 1 else ((NW - 1) * par + i) % (SQ_ - 1)

        def k_slot(i):
            return SK_ - 1 if i == NW - 1 else i % (SK_ - 1)

        with nc.Block() as block:
            @block.tensor
            def _(pe):
                def flip(img, base, f, at):
                    pe.wait_ge(yp_read, base + at + 1)
                    if f == 0:
                        pe.wait_ge(xc_ready, img + 1)
                    for t in range(4 * f, min(4 * f + 4, NT)):
                        c0 = (t % 4) * P
                        last = nc.tensor.transpose(YP[0:C, c0:c0 + P], XC[:, t, :], k.ident[:])
                    last.then_inc(yp_full, 1)

                def project(n, par, i, img):
                    pe.wait_ge(mq_ready, n + 1)
                    pe.wait_ge(mk_ready, n + 1)
                    pe.wait_ge(mk_half, n + 1)
                    if i == 0:
                        pe.wait_ge(xw_ready, img + 1)
                    x = XW[:, par, i * NW:(i + 1) * NW, 0:K]
                    nc.tensor.matmul(PQ[:, 0:NW * K], ACAT[:], x, start=True, stop=True)
                    nc.tensor.matmul(PK[:, 0:NW * K], ATCAT[:], x, start=True, stop=True).then_inc(prj_full, 1)

                def pairs(banks, par, i, buf, slot):
                    for p in range(NW // 2):
                        bank = banks[p // 2]
                        c0 = (p % 2) * HK
                        for half in range(2):
                            w = 2 * p + half
                            last = nc.tensor.matmul(bank[half * SLOT:(half + 1) * SLOT, c0:c0 + HK],
                                                    XW[:, par, i * NW + w, :],
                                                    buf[:, slot, half, p].rearrange("p h c -> p (h c)"),
                                                    start=True, stop=True)
                        yield last

                def maxima(n, par, i):
                    pe.wait_ge(mk_ready, n + 2)
                    pe.wait_ge(mk_half, n + 2)
                    pe.wait_ge(max_done, n + 1)
                    for last in pairs(MXB, par, i, MK, k_slot(i)):
                        pass
                    last.then_inc(mx_full, 1)

                def max_flip(n, base, at, i):
                    pe.wait_ge(dp_read, base + at + 1)
                    pe.wait_ge(shift_done, n + 1)
                    nc.tensor.transpose(DP[0:NW // 2 * HEADS, 0:P], NMX[:, i % 2, :], k.ident[:]).then_inc(dp_full, 1)

                def weigh(g, par, i, at):
                    n = g * NW + i
                    pe.wait_ge(dp_read, dp_base(g) + at + 1)
                    pe.wait_ge(exp_done, 2 * n + 3)
                    pe.wait_ge(yp_read, yp_base(g) + yp_at[("y", i)] + 2)
                    for pp in range(NW // 4):
                        c0 = pp * K
                        for h in range(HEADS):
                            for o in range(2):
                                p, o0 = 2 * pp + o, o * SLOT
                                last = nc.tensor.matmul(DP[o0:o0 + 2 * C, c0:c0 + K],
                                                        YB[:, i % 2, p, h].rearrange("p a c -> p (a c)"),
                                                        PT[:, i % 2, p * HK + h * K:p * HK + (h + 1) * K],
                                                        start=(h == 0), stop=(h == HEADS - 1))
                    last.then_inc(dp_full, 1)

                for f in range(NF):
                    flip(0, 0, f, f)
                for i in range(2):
                    project(i, 0, i, 0)
                    maxima(i, 0, i)
                project(2, 0, 2, 0)
                max_flip(0, 0, 0, 0)
                with pe.Fori(0, NB // 2) as pair_of:
                    for par in range(2):
                        g = pair_of * 2 + par

                        def flips(i, which):
                            x = YP_ITEMS[i][1 + which:2 + which]
                            if x:
                                flip(g + 1, yp_base(g), x[0][1], yp_at[x[0]])

                        for i in range(NW):
                            n = g * NW + i
                            (i2, par2), (i3, par3) = ahead(par, i, 2), ahead(par, i, 3)
                            pe.wait_ge(mq_ready, n + 2)
                            pe.wait_ge(shift_in, (n + 1) * 32 + 1)
                            pe.wait_ge(exp_done, 2 * n + 1)
                            for p, last in enumerate(pairs(SL, par, i, MQ, q_slot(par, i))):
                                if p % 2:
                                    last.then_inc(s_full, 1)
                            maxima(n + 2, par2, i2)
                            max_flip(n + 1, dp_base(g), dp_at[("nmT", i)], i + 1)
                            pe.wait_ge(yp_read, yp_base(g) + yp_at[("y", i)] + 1)
                            for p in range(NW // 2):
                                for half in range(2):
                                    last = nc.tensor.matmul(YP[half * SLOT:(half + 1) * SLOT, p * P:(p + 1) * P],
                                                            XW[:, par, i * NW + 2 * p + half, :], BCAT[:],
                                                            start=True, stop=True)
                            last.then_inc(yp_full, 1)
                            flips(i, 0)
                            project(n + 3, par3, i3, g + (1 if i + 3 >= NW else 0))
                            if i:
                                weigh(g, par, i - 1, dp_at[("pv", i - 1)])
                            flips(i, 1)
                            if i == NW - 1:
                                weigh(g, par, i, dp_at[("pv", i)])
                                for f in range(NBK):
                                    pe.wait_ge(dp_read, dp_base(g) + dp_at[("back", f)] + 1)
                                    for t in range(16 * f, min(16 * f + 16, NT)):
                                        c0, r = (t % 16) * C, rows(t)
                                        last = nc.tensor.matmul(DP[0:r, c0:c0 + C], OT[:, t * P:t * P + r],
                                                                k.ident[:, 0:C], start=True, stop=True)
                                    last.then_inc(dp_full, 1)

            @block.scalar
            def _(act):
                act.sem_inc(yp_read, 1)
                act.sem_inc(mq_ready, 1)
                act.sem_inc(mk_half, 1)
                act.sem_inc(exp_done, 1)

                def take_flip(base, f, at):
                    lo, hi = 512 * f, min(512 * f + 512, S)
                    act.wait_ge(yp_full, base + at + 1)
                    nc.scalar.copy(XR[:, lo:hi], YP[0:C, 0:hi - lo]).then_inc(yp_read, 1)

                def fill_q(n, par, i):
                    act.wait_ge(prj_full, n + 1)
                    for h in range(HEADS):
                        last = nc.scalar.copy(MQ[0:C, q_slot(par, i), :, :, h, :],
                                              PQ[h * C:(h + 1) * C, 0:NW * K].rearrange("p (w f c) -> p f w c", f=2, c=K))
                    last.then_inc(mq_ready, 1)
                    for h in range(HEADS // 2):
                        last = nc.scalar.copy(MK[0:C, k_slot(i), :, :, h, :],
                                              PK[h * C:(h + 1) * C, 0:NW * K].rearrange("p (w f c) -> p f w c", f=2, c=K))
                    last.then_inc(mk_half, 1)

                def exp_q(n):
                    act.wait_ge(max_done, n + 2)
                    nc.scalar.activation(EXQ[:], EXQ[:], ACT.Exp).then_inc(exq_done, 1)

                def log_sum(n):
                    act.wait_ge(sum_done, n + 1)
                    nc.scalar.activation(LN[:], LS[:], ACT.Ln).then_inc(ln_done, 1)

                nc.scalar.preload_act_table_set("natural_log_exp_and_others")
                for f in range(NF):
                    take_flip(0, f, f)
                for i in range(2):
                    fill_q(i, 0, i)
                    exp_q(i)
                    log_sum(i)
                fill_q(2, 0, 2)
                with act.Fori(0, NB // 2) as pair_of:
                    for par in range(2):
                        g = pair_of * 2 + par

                        def flips(i, which):
                            x = YP_ITEMS[i][1 + which:2 + which]
                            if x:
                                if x[0][1] == 0:
                                    act.wait_ge(xw_ready, g + 1)
                                take_flip(yp_base(g), x[0][1], yp_at[x[0]])

                        for i in range(NW):
                            n = g * NW + i
                            i3, par3 = ahead(par, i, 3)
                            act.wait_ge(pv_done, n + 1)
                            for b in range(2):
                                act.wait_ge(s_full, 2 * n + b + 1)
                                nc.scalar.activation(PT[:, i % 2, b * HALF:(b + 1) * HALF], SL[b][:, 0:HALF],
                                                     ACT.Exp).then_inc(exp_done, 1)
                            act.wait_ge(yp_full, yp_base(g) + yp_at[("y", i)] + 1)
                            for half in range(2):
                                r = slice(half * SLOT, (half + 1) * SLOT)
                                last = nc.scalar.copy(YB[r, i % 2, :, :, half, :].rearrange("p a h c -> p (a h) c"),
                                                      YP[r, :].rearrange("p (a c) -> p a c", c=C))
                            last.then_inc(yp_read, 1)
                            exp_q(n + 2)
                            flips(i, 0)
                            fill_q(n + 3, par3, i3)
                            flips(i, 1)
                            log_sum(n + 2)

            @block.vector
            def _(dve):
                for s in (dp_read, mk_ready, max_done, pv_done, stat_step):
                    dve.sem_inc(s, 1)
                dve.sem_inc(pv_done, 1)

                def fill_k(n, i):
                    dve.wait_ge(prj_full, n + 1)
                    for h in range(HEADS // 2, HEADS):
                        last = nc.vector.tensor_copy(MK[0:C, k_slot(i), :, :, h, :],
                                                     PK[h * C:(h + 1) * C, 0:NW * K].rearrange("p (w f c) -> p f w c", f=2, c=K))
                    last.then_inc(mk_ready, 1)

                def take_max(n, i):
                    dve.wait_ge(mx_full, n + 1)
                    for b in range(2):
                        last = nc.vector.tensor_reduce(NMX[:, i % 2, b * 2 * HEADS:(b + 1) * 2 * HEADS],
                                                       MXB[b][:, 0:HALF].rearrange("p (a c) -> p a c", c=K),
                                                       AX.X, ALU.max, negate=True)
                    last.then_inc(nmx_done, 1)
                    dve.wait_ge(nmx_done, n + 1)
                    for b in range(2):
                        groups = slice(b * 2 * HEADS, (b + 1) * 2 * HEADS)
                        last = nc.vector.tensor_tensor(
                            EXQ[:, b * HALF:(b + 1) * HALF].rearrange("p (a c) -> p a c", c=K),
                            MXB[b][:, 0:HALF].rearrange("p (a c) -> p a c", c=K),
                            NMX[:, i % 2, groups][:, :, None].to_broadcast([P, 2 * HEADS, K]), ALU.add)
                    last.then_inc(max_done, 1)

                def take_sum(n):
                    dve.wait_ge(exq_done, n + 1)
                    nc.vector.tensor_reduce(LS[:], EXQ[:].rearrange("p (a c) -> p a c", c=K), AX.X,
                                            ALU.add).then_inc(sum_done, 1)

                def take_log(n, i):
                    dve.wait_ge(ln_done, n + 1)
                    nc.vector.tensor_tensor(NMX[:, i % 2, :], NMX[:, i % 2, :], LN[:],
                                            ALU.subtract).then_inc(shift_done, 1)

                def take_flip(n, base, at, i):
                    dve.wait_ge(dp_full, base + at + 1)
                    if not isinstance(n, int):
                        dve.wait_ge(shift_in, (n - 1) * 32 + 1)
                    nc.vector.tensor_copy(NMT[:, i % 2, :], DP[0:NW // 2 * HEADS, 0:P]).then_inc(dp_read, 1)

                def stats(img):
                    base = img * STATS + 1
                    n = [0]

                    def step(ins):
                        n[0] += 1
                        ins.then_inc(stat_step, 1)
                        dve.wait_ge(stat_step, base + n[0])

                    dve.wait_ge(bn_done, (img + 1) * NF)
                    nc.vector.memset(VE[:], 0.0)
                    step(nc.vector.bn_aggr(MV[:], BN[:].rearrange("p a b -> p (a b)")))
                    step(nc.vector.tensor_scalar(VE[:], MV[:, 1:2], eps, None, ALU.add))
                    rsqrt_steps(nc, RS[:], VE[:], TM[:], step)
                    step(nc.vector.tensor_tensor(TM[:], MV[:, 0:1], RS[:], ALU.mult))
                    nc.vector.tensor_scalar(SH[:], TM[:], -1.0, None, ALU.mult).then_inc(stat_done, 1)
                    dve.wait_ge(stat_done, img + 1)

                def bn(base, f, at):
                    lo, hi = 512 * f, min(512 * f + 512, S)
                    dve.wait_ge(yp_read, base + at + 2)
                    nc.vector.bn_stats(BN[:, f, :], XR[:, lo:hi]).then_inc(bn_done, 1)

                def take_out(g, par, i):
                    dve.wait_ge(dp_full, dp_base(g) + dp_at[("pv", i)] + 1)
                    y0 = WS * i + DISP
                    parts = [(0, WS, y0)] if i < NW - 1 else [(0, WS - DISP, y0), (WS - DISP, DISP, 0)]
                    told = False
                    for r0, nr, y in parts:
                        out = OT[0:C, y * IMG:(y + nr) * IMG].rearrange("c (y x) -> c y x", x=IMG)
                        for b in range(4):
                            blk = DP[b * C:(b + 1) * C, 0:2 * K].rearrange("c (g y x) -> c g y x", g=2, x=WS)
                            for gr in range(2):
                                j = 4 * gr + b
                                x0 = WS * j + DISP
                                cols = [(0, WS, x0)] if j < NW - 1 else [(0, WS - DISP, x0), (WS - DISP, DISP, 0)]
                                for c0, ncol, x in cols:
                                    last = nc.vector.tensor_scalar(out[:, :, x:x + ncol],
                                                                   blk[:, gr, r0:r0 + nr, c0:c0 + ncol],
                                                                   BO[:], None, ALU.add)
                                    if not told:
                                        last.then_inc(pv_done, 1)
                                        told = True
                    last.then_inc(dp_read, 1)

                def out_rows(g, f):
                    lo, hi = 16 * f, min(16 * f + 16, NT)
                    full = min(hi, NT - 1)
                    dve.wait_ge(dp_full, dp_base(g) + dp_at[("back", f)] + 1)
                    if hi > full:
                        t = m.T[0:LAST, g, full, :]
                        nc.vector.tensor_tensor(t, t, DP[0:LAST, (full - lo) * C:(hi - lo) * C], ALU.add)
                    t = m.T[:, g, lo:full, :].rearrange("p t c -> p (t c)")
                    nc.vector.tensor_tensor(t, t, DP[:, 0:(full - lo) * C], ALU.add).then_inc(dp_read, 1)

                for f in range(NF):
                    bn(0, f, f)
                stats(0)
                for i in range(2):
                    fill_k(i, i)
                    take_max(i, i)
                    take_sum(i)
                    if i == 0:
                        take_log(0, 0)
                fill_k(2, 2)
                take_flip(0, 0, 0, 0)
                with dve.Fori(0, NB // 2) as pair_of:
                    for par in range(2):
                        g = pair_of * 2 + par
                        for i in range(NW):
                            n = g * NW + i
                            take_log(n + 1, i + 1)
                            take_max(n + 2, i)
                            take_flip(n + 1, dp_base(g), dp_at[("nmT", i)], i + 1)
                            take_sum(n + 2)
                            fill_k(n + 3, (i + 3) % NW)
                            if i:
                                take_out(g, par, i - 1)
                            for x in YP_ITEMS[i][1:]:
                                bn(yp_base(g), x[1], yp_at[x])
                            if i == NF // 2 + 1:
                                stats(g + 1)
                            if i == NW - 1:
                                take_out(g, par, i)
                                for f in range(NBK):
                                    out_rows(g, f)

            @block.gpsimd
            def _(pool):
                def windows(img, par):
                    for i in range(NW):
                        y0 = WS * i + DISP
                        parts = [(0, WS, y0)] if i < NW - 1 else [(0, WS - DISP, y0), (WS - DISP, DISP, 0)]
                        for r0, nr, y in parts:
                            src = XR[:, y * IMG:(y + nr) * IMG].rearrange("c (y x) -> c y x", x=IMG)
                            for j0, nj, c0, ncol, x in ((0, NW - 1, 0, WS, DISP),
                                                        (NW - 1, 1, 0, WS - DISP, IMG - WS + DISP),
                                                        (NW - 1, 1, WS - DISP, DISP, 0)):
                                dst = XW[0:C, par, i * NW + j0:i * NW + j0 + nj, 0:K]\
                                    .rearrange("c j (y x) -> c y j x", x=WS)[:, r0:r0 + nr, :, c0:c0 + ncol]
                                if nj > 1:
                                    s = src[:, :, x:x + nj * WS].rearrange("c y (j x) -> c y j x", x=WS)
                                else:
                                    s = src[:, :, None, x:x + ncol]
                                last = nc.gpsimd.tensor_scalar(dst, s, RS[:], SH[:], ALU.mult, ALU.add)
                    last.then_inc(xw_ready, 1)

                def fetch(img):
                    nc.gpsimd.tensor_copy(XC[:], m.T[:, img]).then_inc(xc_ready, 1)

                pool.wait_ge(m.loaded, 32 * NB)
                fetch(0)
                pool.wait_ge(stat_done, 1)
                windows(0, 0)
                with pool.Fori(0, NB // 2) as pair_of:
                    for par in range(2):
                        g = pair_of * 2 + par
                        fetch(g + 1)
                        pool.wait_ge(stat_done, g + 2)
                        pool.nop(nofuse=True)
                        windows(g + 1, 1 - par)

            @block.sync
            def _(sp):
                def send(n, par, i):
                    for half in range(2):
                        sp.dma_start(MQ[ONE:ONE + 1, q_slot(par, i), half].rearrange("o p h c -> o (p h) c"),
                                     NMT[:, i % 2, half * SLOT:half * SLOT + K]).then_inc(shift_in, 16)

                sp.sem_inc(shift_in, 1)
                sp.wait_ge(dp_read, 2)
                send(0, 0, 0)
                with sp.Fori(0, NB // 2) as pair_of:
                    for par in range(2):
                        g = pair_of * 2 + par
                        for i in range(NW):
                            sp.wait_ge(dp_read, dp_base(g) + dp_at[("nmT", i)] + 2)
                            sp.wait_ge(shift_in, 32 * (g * NW + i + 1) + 1)
                            send(g * NW + i + 1, par if i + 1 < NW else 1 - par, (i + 1) % NW)
                sp.wait_ge(shift_in, 32 * (NB * NW + 1) + 1)


E_ = 16
TOPK = 8
TAKEN = -3.0e38


def expert_choice(nc, m, k, gate_wT, gate_b, weight1, weight2, tag):
    QD = 4
    NH = 2
    NI = QD * NH
    NO = m.NB // NI
    QB = 512
    CH = -(-S // QB)
    TB = QB // P
    NB4 = -(-NT // TB)

    def rows(t):
        return P if t < NT - 1 else LAST

    def span(f):
        return QB * f, min(QB * (f + 1), S)

    with ExitStack() as ctx:
        def sb(name, shape, dt=F32):
            return ctx.enter_context(nc.sbuf_tensor(f"{tag}_{name}", shape, dt))

        def pb(name, shape, dt=F32):
            return ctx.enter_context(nc.psum_tensor(f"{tag}_{name}", shape, dt))

        def sem(name):
            return ctx.enter_context(nc.semaphore(f"{tag}_{name}"))

        XN = sb("xn", [P, NT, NI, C])
        XT = sb("xT", [P, S])
        LG = sb("lg", [P, S])
        EX = sb("ex", [P, S])
        WT = sb("wT", [P, NT, P])
        GW = sb("gw", [P, QD * E_])
        GB = sb("gb", [P, 1])
        W1 = sb("w1", [C + 1, E_, HID])
        W2 = sb("w2", [HID, E_, C])
        B2 = sb("b2", [C, E_])
        SAME = sb("same", [P, QD, C])
        M8 = sb("m8", [P, TOPK])
        NM = sb("nm", [P, 1])
        SUM = sb("sum", [P, 1])
        RS = sb("rs", [P, 1])
        PM = sb("pm", [P, QD, C])
        PL = sb("pl", [P, C])
        PN = sb("pn", [P, C])
        PT = sb("pT", [C + 1, E_, NI])
        HT = sb("hT", [HID, E_ * NI])
        OT = sb("oT", [C, NI, E_])
        OB = sb("ob", [P, C])
        OK = sb("ok", [P, QD, C])
        RING = 4
        R = [pb(f"r{i}", [P, QB]) for i in range(RING)]
        PP = pb("pp", [P, QD * C])
        SM = [pb(f"sm{i}", [P, P]) for i in range(3)]

        w_in, w_set = sem("w_in"), sem("w_set")
        with nc.Block() as block:
            @block.vector
            def _(dve):
                nc.vector.memset(GW[:], 0.0).then_inc(w_set, 1)
                nc.vector.memset(PT[:], 1.0).then_inc(w_set, 1)
                dve.wait_ge(w_set, 2)

            @block.gpsimd
            def _(pool):
                s1, s2 = sem("s1"), sem("s2")
                nc.gpsimd.memset(SAME[:], 1.0).then_inc(s1, 1)
                pool.wait_ge(s1, 1)
                n = 1
                for h in range(NH):
                    part = SAME[h * 64:(h + 1) * 64]
                    for sign, base in ((1, 0), (-1, E_ - 1)):
                        nc.gpsimd.affine_select(out=part, in_=part, compare_op=ALU.is_ge, fill=0.0, base=base,
                                                pattern=[[-sign * E_, QD], [0, C]],
                                                channel_multiplier=sign).then_inc(s1, 1)
                        n += 1
                        pool.wait_ge(s1, n)

            @block.sync
            def _(sp):
                sp.wait_ge(w_set, 1)
                for b in range(QD):
                    sp.dma_start(GW[b * C:(b + 1) * C, b * E_:(b + 1) * E_], gate_wT).then_inc(w_in, 16)
                for b in range(NI):
                    sp.dma_start(GB[b * E_:(b + 1) * E_, :], gate_b[:, None]).then_inc(w_in, 16)
                sp.dma_start(W1[:], weight1.rearrange("e d h -> d e h")).then_inc(w_in, 16)
                sp.dma_start(W2[:], weight2[:, 0:HID, :].rearrange("e h o -> h e o")).then_inc(w_in, 16)
                sp.dma_start(B2[:], weight2[:, HID, :].rearrange("e o -> o e"), allow_slow_non_contiguous=True).then_inc(w_in, 16)
                sp.wait_ge(w_in, 16 * (QD + NI + 3))

        norm_step = sem("norm_step")
        ring_full, ring_read_a, ring_read_v = sem("ring_full"), sem("ring_read_a"), sem("ring_read_v")
        vec, exp_done = sem("vec"), sem("exp_done")
        pooled_done, small_full, gelu_done = sem("pooled_done"), sem("small_full"), sem("gelu_done")
        FILLS = [(x, h, f) for h in range(NH) for x in ("xT", "lg") for f in range(NB4)]
        FILLS += [("wT", 0, f) for f in range(NB4)]
        N_A = len(FILLS)
        FILLS += [("out", h, f) for h in range(NH) for f in range(NB4)]
        N_V = len(FILLS) - N_A
        N_ALL = N_A + N_V
        VEC = 13

        with nc.Fori(0, NO) as o:
            with nc.Block() as block:
                @block.tensor
                def _(pe):
                    def free(n):
                        if n >= RING:
                            prev = n - RING
                            if prev < N_A:
                                pe.wait_ge(ring_read_a, o * N_A + prev + 1)
                            else:
                                pe.wait_ge(ring_read_v, o * N_V + prev - N_A + 1)

                    for n, (x, h, f) in enumerate(FILLS):
                        free(n)
                        pe.nop(nofuse=True)
                        bank = R[n % RING]
                        lo, hi = span(f)
                        if x == "xT":
                            if f == 0:
                                pe.wait_ge(norm_step, o * NH * 2 + 2 * h + 2)
                            for t in range(TB * f, min(TB * f + TB, NT)):
                                c0, r = (t % TB) * P, rows(t)
                                last = nc.tensor.transpose(bank[:, c0:c0 + r],
                                                           XN[0:r, t, QD * h:QD * (h + 1)].rearrange("p b c -> p (b c)"),
                                                           k.ident[0:r, 0:r])
                        elif x == "lg":
                            pe.wait_ge(ring_read_a, o * N_A + FILLS.index(("xT", h, f)) + 1)
                            pe.nop(nofuse=True)
                            last = nc.tensor.matmul(bank[64 * h:64 * h + 64, 0:hi - lo], GW[:], XT[:, lo:hi],
                                                    start=True, stop=True)
                        elif x == "wT":
                            if f == 0:
                                pe.wait_ge(vec, o * VEC + 4)
                                pe.nop(nofuse=True)
                            for t in range(TB * f, min(TB * f + TB, NT)):
                                c0, r = (t % TB) * P, rows(t)
                                last = nc.tensor.transpose(bank[0:r, c0:c0 + P], EX[:, t * P:t * P + r], k.ident[:])
                        else:
                            if n == N_A:
                                pe.wait_ge(ring_read_a, o * N_A + N_A)
                                for hh in range(NH):
                                    for t in range(NT):
                                        r = rows(t)
                                        s = nc.tensor.matmul(PP[64 * hh:64 * hh + 64, :],
                                                             WT[0:r, t, 64 * hh:64 * hh + 64],
                                                             XN[0:r, t, QD * hh:QD * (hh + 1)].rearrange("p b c -> p (b c)"),
                                                             start=(t == 0), stop=(t == NT - 1))
                                s.then_inc(pooled_done, 1)
                                pe.wait_ge(vec, o * VEC + 9)
                                nc.tensor.transpose(SM[0][0:C, :], PN[:], k.ident[:]).then_inc(small_full, 1)
                                pe.wait_ge(vec, o * VEC + 10)
                                for e in range(E_):
                                    s = nc.tensor.matmul(SM[1][:, e * NI:(e + 1) * NI], W1[:, e, :], PT[:, e, :],
                                                         start=True, stop=True)
                                s.then_inc(small_full, 1)
                                pe.wait_ge(gelu_done, o + 1)
                                for e in range(E_):
                                    s = nc.tensor.matmul(SM[2][0:C, e * NI:(e + 1) * NI], W2[:, e, :],
                                                         HT[:, e * NI:(e + 1) * NI], start=True, stop=True)
                                s.then_inc(small_full, 1)
                                pe.wait_ge(vec, o * VEC + 11)
                                pe.nop(nofuse=True)
                                nc.tensor.transpose(SM[0][:, 0:C], OT[:].rearrange("o b e -> o (b e)"),
                                                    k.ident[0:C, 0:C]).then_inc(small_full, 1)
                                pe.wait_ge(vec, o * VEC + 13)
                            for t in range(TB * f, min(TB * f + TB, NT)):
                                c0, r = (t % TB) * P, rows(t)
                                last = nc.tensor.matmul(bank[0:r, c0:c0 + P],
                                                        EX[64 * h:64 * h + 64, t * P:t * P + r],
                                                        OK[64 * h:64 * h + 64].rearrange("p b c -> p (b c)"),
                                                        start=True, stop=True)
                        last.then_inc(ring_full, 1)

                @block.scalar
                def _(act):
                    for n in range(N_A):
                        x, h, f = FILLS[n]
                        bank = R[n % RING]
                        lo, hi = span(f)
                        act.wait_ge(ring_full, o * N_ALL + n + 1)
                        if x == "xT":
                            ins = nc.scalar.copy(XT[:, lo:hi], bank[:, 0:hi - lo])
                        elif x == "lg":
                            ins = nc.scalar.activation(LG[64 * h:64 * h + 64, lo:hi], bank[64 * h:64 * h + 64, 0:hi - lo],
                                                       ACT.Identity, bias=GB[64 * h:64 * h + 64, :])
                        else:
                            if f == NB4 - 1:
                                ins = nc.scalar.copy(WT[0:LAST, NT - 1, :], bank[0:LAST, 0:P])
                            else:
                                ins = nc.scalar.copy(WT[:, TB * f:TB * f + TB, :].rearrange("p t e -> p (t e)"), bank[:])
                        ins.then_inc(ring_read_a, 1)
                        if n == NH * 2 * NB4 - 1:
                            act.wait_ge(vec, o * VEC + 2)
                            nc.scalar.activation(EX[:], LG[:], ACT.Exp, bias=NM[:],
                                                 accum_out=SUM[:]).then_inc(exp_done, 1)
                    act.wait_ge(small_full, o * 4 + 2)
                    nc.scalar.activation(HT[:], SM[1][:], ACT.Gelu).then_inc(gelu_done, 1)

                @block.vector
                def _(dve):
                    for h in range(NH):
                        img = bass.ds(o * NI + h * QD, QD)
                        xn = XN[:, :, QD * h:QD * (h + 1), :]
                        shape = [P, NT, QD, C]
                        nc.vector.tensor_tensor(
                            xn, m.T[:, img].rearrange("p b t c -> p t b c"),
                            m.mean[:, img].rearrange("p b t -> p t b")[:, :, :, None].to_broadcast(shape),
                            ALU.subtract).then_inc(norm_step, 1)
                        dve.wait_ge(norm_step, o * NH * 2 + 2 * h + 1)
                        nc.vector.tensor_tensor(
                            xn, xn, m.rstd[:, img].rearrange("p b t -> p t b")[:, :, :, None].to_broadcast(shape),
                            ALU.mult).then_inc(norm_step, 1)

                    n = [0]

                    def step(ins):
                        n[0] += 1
                        ins.then_inc(vec, 1)
                        dve.wait_ge(vec, o * VEC + n[0])

                    dve.wait_ge(ring_read_a, o * N_A + NH * 2 * NB4)
                    dve.nop(nofuse=True)
                    step(nc.vector.max(M8[:], LG[:]))
                    step(nc.vector.tensor_scalar(NM[:], M8[:, 0:1], -1.0, None, ALU.mult))
                    dve.wait_ge(exp_done, o + 1)
                    dve.nop(nofuse=True)
                    step(nc.vector.match_replace(LG[:], M8[:], LG[:], TAKEN))
                    step(nc.vector.scalar_tensor_tensor(out=EX[:], in0=LG[:], scalar=TAKEN, in1=EX[:],
                                                        op0=ALU.is_equal, op1=ALU.mult))
                    step(nc.vector.reciprocal(RS[:], SUM[:]))
                    dve.wait_ge(pooled_done, o + 1)
                    step(nc.vector.tensor_tensor(PM[:], PP[:].rearrange("p (b c) -> p b c", b=QD), SAME[:], ALU.mult))
                    step(nc.vector.tensor_reduce(PL[:], PM[:].rearrange("p b c -> p c b"), AX.X, ALU.add))
                    step(nc.vector.tensor_scalar(PN[:], PL[:], RS[:], None, ALU.mult))
                    step(nc.vector.tensor_copy(NM[:], RS[:]))
                    dve.wait_ge(small_full, o * 4 + 1)
                    step(nc.vector.tensor_copy(PT[0:C].rearrange("c e b -> c b e"),
                                               SM[0][0:C, :].rearrange("c (b e) -> c b e", e=E_)))
                    dve.wait_ge(small_full, o * 4 + 3)
                    step(nc.vector.tensor_tensor(OT[:].rearrange("o b e -> o e b"),
                                                 SM[2][0:C, :].rearrange("o (e b) -> o e b", b=NI),
                                                 B2[:][:, :, None].to_broadcast([C, E_, NI]), ALU.add))
                    dve.wait_ge(small_full, o * 4 + 4)
                    step(nc.vector.tensor_scalar(OB[:], SM[0][:, 0:C], RS[:], None, ALU.mult))
                    step(nc.vector.tensor_tensor(OK[:], SAME[:], OB[:][:, None, :].to_broadcast([P, QD, C]), ALU.mult))
                    assert n[0] == VEC
                    for i in range(N_V):
                        x, h, f = FILLS[N_A + i]
                        bank = R[(N_A + i) % RING]
                        r, nt = (P, TB) if f < NB4 - 1 else (LAST, 1)
                        dve.wait_ge(ring_full, o * N_ALL + N_A + i + 1)
                        t = m.T[0:r, bass.ds(o * NI + h * QD, QD), TB * f:TB * f + nt, :].rearrange("p b t c -> p t b c")
                        nc.vector.tensor_tensor(t, t, bank[0:r, 0:nt * P].rearrange("p (t b c) -> p t b c", t=nt, b=QD),
                                                ALU.add).then_inc(ring_read_v, 1)
                    dve.wait_ge(ring_read_v, o * N_V + N_V)
                    dve.nop(nofuse=True)


NB = 16


def clear_padding(nc, m):
    cleared = m.sem("T_cleared")
    with nc.Block() as block:
        @block.gpsimd
        def _(pool):
            nc.gpsimd.memset(m.T[:, m.NB], 0.0).then_inc(cleared, 1)
            pool.wait_ge(cleared, 1)
            nc.gpsimd.memset(m.T[LAST:P, :, NT - 1], 0.0).then_inc(cleared, 1)
            pool.wait_ge(cleared, 2)


def load_images(m, x, sp):
    for i in range(m.NB):
        sp.dma_start(m.T[:, i, 0:NT - 1, :],
                     x[i, 0:(NT - 1) * P, :].rearrange("(t p) c -> p t c", p=P)).then_inc(m.loaded, 16)
        sp.dma_start(m.T[0:LAST, i, NT - 1, :], x[i, (NT - 1) * P:S, :]).then_inc(m.loaded, 16)


def store_images(nc, m, out):
    stored = m.sem("T_stored")
    with nc.Block() as block:
        @block.sync
        def _(sp):
            for i in range(m.NB):
                sp.dma_start(out[i, 0:(NT - 1) * P, :].rearrange("(t p) c -> p t c", p=P),
                             m.T[:, i, 0:NT - 1, :]).then_inc(stored, 16)
                sp.dma_start(out[i, (NT - 1) * P:S, :], m.T[0:LAST, i, NT - 1, :]).then_inc(stored, 16)
            sp.wait_ge(stored, 32 * m.NB)


def program(nc, a, out):
    with ExitStack() as ctx:
        k = make_constants(nc, ctx)
        m = Shared()
        m.NB = NB
        m.sem = lambda name: ctx.enter_context(nc.semaphore(name))
        m.T = ctx.enter_context(nc.sbuf_tensor("T", [P, NB + 1, NT, C], F32))
        m.mean = ctx.enter_context(nc.sbuf_tensor("mean", [P, NB + 1, NT], F32))
        m.rstd = ctx.enter_context(nc.sbuf_tensor("rstd", [P, NB + 1, NT], F32))
        m.loaded = m.sem("T_loaded")
        clear_padding(nc, m)
        window_attention(nc, m, k, a["L0_conv_w_qkv"], a["L0_conv_pos_emb"], a["L0_conv_w_out"],
                         a["L0_conv_b_out"], 1e-5, "win", load=lambda sp: load_images(m, a["x"], sp))
        token_mlps(nc, m, k, {n[8:]: t for n, t in a.items() if n.startswith("L1_conv_")}, 1e-5, "mlp")
        for layer, wq, wk, wv in (("L2", "W_Q", "W_K", "W_V"), ("L3", "Wq", "Wk", "Wv")):
            token_stats(nc, m, 1e-5, f"{layer}as")
            causal_attention(nc, m, k, *(a[f"{layer}_attn_{w}"] for w in (wq, wk, wv)), f"{layer}a")
            token_stats(nc, m, 1e-5, f"{layer}fs")
            expert_choice(nc, m, k, *(a[f"{layer}_ffn_{w}"] for w in ("gate_w", "gate_b", "weight1", "weight2")),
                          f"{layer}f")
        store_images(nc, m, out)


TRANSPOSED = ("L0_conv_w_qkv", "L2_ffn_gate_w", "L3_ffn_gate_w", "L3_attn_Wq", "L3_attn_Wk", "L3_attn_Wv")
UNUSED = ("L1_conv_router", "L1_conv_bo_send")


def kernel(**inputs):
    import numpy as _np
    import concourse.bacc as _bacc
    from concourse import mybir as _mybir
    from concourse.bass_utils import run_bass_kernel_spmd as _run

    nc = _bacc.Bacc("TRN2", target_bir_lowering=False, num_devices=1)
    arrays, args = {}, {}
    for name, value in inputs.items():
        if name in UNUSED:
            continue
        v = _np.asarray(value)
        if name in TRANSPOSED:
            v = v.T
        if name == "x":
            v = v.reshape(NB, S, C)
        v = _np.ascontiguousarray(v)
        arrays[f"in_{name}"] = v
        args[name] = nc.dram_tensor(f"in_{name}", v.shape, _mybir.dt.from_np(v.dtype), kind="ExternalInput").ap()
    out = nc.dram_tensor("out_0", (NB, S, C), F32, kind="ExternalOutput").ap()
    program(nc, args, out)
    r = _run(nc, [arrays], core_ids=[0])
    return r.results[0]["out_0"].reshape(NB, IMG, IMG, C)
```
